# Optimizing a Trainium2 kernel written in Bass

```python
import numpy as np
import jax
import jax.numpy as jnp

def _softmax(x, axis=-1):
    return jax.nn.softmax(x, axis=axis)

def _gelu(x):
    return jax.nn.gelu(x, approximate=True)

def _silu(x):
    return jax.nn.silu(x)

def _sigmoid(x):
    return jax.nn.sigmoid(x)

def _layernorm(x, axis=-1, eps=1e-05):
    m = jnp.mean(x, axis=axis, keepdims=True)
    v = jnp.var(x, axis=axis, keepdims=True)
    return (x - m) / jnp.sqrt(v + eps)

def _scatter_add(tgt, idx, src, axis=0):
    return tgt.at[idx].add(src)

def _segment_sum(src, seg, n):
    return jax.ops.segment_sum(src, seg, n)
kernel_name = 'mk_recurrent_d2_jaxref_r8_bb9a08'

def setup_inputs(seed: int=0):
    np.random.seed(seed)
    _w = jnp.asarray

    def _L0_attn_setup():
        import jax, jax.numpy as jnp
        import numpy as np
        K_FACTOR = 0.5
        key = jax.random.key(seed)
        k1, k2, k3, k4 = jax.random.split(key, 4)
        B, S, H, I = (1, 256, 512, 1376)
        x = jax.random.normal(k1, (B, S, H), dtype=jnp.float32)
        w_gate = jax.random.normal(k2, (I, H), dtype=jnp.float32) * 0.02
        w_up = jax.random.normal(k3, (I, H), dtype=jnp.float32) * 0.02
        w_down = jax.random.normal(k4, (H, I), dtype=jnp.float32) * 0.02
        return {'x': x, 'w_gate': w_gate, 'w_up': w_up, 'w_down': w_down}
    _L0_attn_in = _L0_attn_setup()

    def _L0_ffn_setup():
        import jax, jax.numpy as jnp
        import numpy as np

        def ternary_quantize(w):
            thresh = 0.7 * jnp.mean(jnp.abs(w), axis=-1, keepdims=True)
            q = jnp.where(w > thresh, 1.0, jnp.where(w < -thresh, -1.0, 0.0)).astype(w.dtype)
            return w + jax.lax.stop_gradient(q - w)
        key = jax.random.key(seed)
        k1, k2, k3 = jax.random.split(key, 3)
        B, S, D_in, D_out = (4, 256, 512, 512)
        x = jax.random.normal(k1, (B, S, D_in), dtype=jnp.float32)
        bound = float(np.sqrt(6.0 / D_in))
        weight = jax.random.uniform(k2, (D_out, D_in), dtype=jnp.float32, minval=-bound, maxval=bound)
        bias = jnp.zeros((D_out,), dtype=jnp.float32)
        return {'x': x, 'weight': weight, 'bias': bias}
    _L0_ffn_in = _L0_ffn_setup()

    def _L1_attn_setup():
        import jax, jax.numpy as jnp
        import numpy as np
        DEPTH, DIM, DFF, VOCAB = (4, 64, 256, 512)
        EPS = 1e-05

        def layernorm(x, w, b):
            mu = jnp.mean(x, axis=-1, keepdims=True)
            var = jnp.mean((x - mu) ** 2, axis=-1, keepdims=True)
            return (x - mu) * jax.lax.rsqrt(var + EPS) * w + b

        def sconv(x, phazor_c, last_conv_c):
            B, L, D = x.shape
            r = jnp.abs(phazor_c)
            p = jnp.tanh(r) * jnp.exp(1j * jnp.angle(phazor_c))
            prog = p[None, :] ** jnp.arange(L, dtype=jnp.float32)[:, None]
            filt_fft = jnp.fft.fft(prog, n=2 * L, axis=0)
            x_fft = jnp.fft.fft(x.astype(jnp.complex64), n=2 * L, axis=1)
            conv = jnp.fft.ifft(filt_fft[None] * x_fft, axis=1)[:, :L]
            conv = conv + last_conv_c[None, None, :] * prog[None] * p[None, None, :]
            return conv.real.astype(x.dtype)

        def _forward(x, Win, bin, ln1_w, ln1_b, phz_re, phz_im, lc_re, lc_im, sc_lin, ln2_w, ln2_b, W1, b1, W2, b2, lnl_w, lnl_b, Wout, bout):
            h = jnp.einsum('blv,dv->bld', x, Win) + bin

            def body(h, p):
                l1w, l1b, pr, pi, lr, li, scl, l2w, l2b, w1, b1_, w2, b2_ = p
                y = jax.nn.silu(layernorm(h, l1w, l1b))
                y = sconv(y, pr + 1j * pi, lr + 1j * li)
                h = h + y * scl
                y = layernorm(h, l2w, l2b)
                y = jax.nn.silu(jnp.einsum('bld,fd->blf', y, w1) + b1_)
                y = jnp.einsum('blf,df->bld', y, w2) + b2_
                return (h + y, None)
            xs = (ln1_w, ln1_b, phz_re, phz_im, lc_re, lc_im, sc_lin, ln2_w, ln2_b, W1, b1, W2, b2)
            h, _ = jax.lax.scan(body, h, xs)
            h = layernorm(h, lnl_w, lnl_b)
            return jnp.einsum('bld,vd->blv', h, Wout) + bout
        key = jax.random.key(seed)
        ks = jax.random.split(key, 20)
        f32 = jnp.float32
        inp = {}
        inp['x'] = jax.random.normal(ks[0], (2, 512, VOCAB), dtype=f32)
        inp['Win'] = jax.random.normal(ks[1], (DIM, VOCAB), dtype=f32) * VOCAB ** (-0.5)
        inp['bin'] = jnp.zeros((DIM,), f32)
        inp['ln1_w'] = jnp.ones((DEPTH, DIM), f32)
        inp['ln1_b'] = jnp.zeros((DEPTH, DIM), f32)
        ang = 2 * np.pi * jnp.arange(DIM, dtype=f32) / DIM
        mag = jnp.abs(jax.random.normal(ks[2], (DEPTH, DIM), dtype=f32))
        inp['phz_re'] = mag * jnp.cos(ang)[None]
        inp['phz_im'] = mag * jnp.sin(ang)[None]
        inp['lc_re'] = jax.random.normal(ks[3], (DEPTH, DIM), dtype=f32)
        inp['lc_im'] = jax.random.normal(ks[4], (DEPTH, DIM), dtype=f32)
        inp['sc_lin'] = jnp.ones((DEPTH, DIM), f32)
        inp['ln2_w'] = jnp.ones((DEPTH, DIM), f32)
        inp['ln2_b'] = jnp.zeros((DEPTH, DIM), f32)
        inp['W1'] = jax.random.normal(ks[5], (DEPTH, DFF, DIM), dtype=f32) * DIM ** (-0.5)
        inp['b1'] = jnp.zeros((DEPTH, DFF), f32)
        inp['W2'] = jax.random.normal(ks[6], (DEPTH, DIM, DFF), dtype=f32) * DFF ** (-0.5)
        inp['b2'] = jnp.zeros((DEPTH, DIM), f32)
        inp['lnl_w'] = jnp.ones((DIM,), f32)
        inp['lnl_b'] = jnp.zeros((DIM,), f32)
        inp['Wout'] = jax.random.normal(ks[7], (VOCAB, DIM), dtype=f32) * DIM ** (-0.5)
        inp['bout'] = jnp.zeros((VOCAB,), f32)
        return inp
    _L1_attn_in = _L1_attn_setup()

    def _L1_ffn_setup():
        import jax, jax.numpy as jnp
        import numpy as np
        key = jax.random.key(seed)
        k = jax.random.split(key, 6)
        x = jax.random.normal(k[0], (4, 256, 512), jnp.float32)
        W = jax.random.normal(k[1], (512, 512), jnp.float32) * 0.02
        bias = jax.random.normal(k[2], (512,), jnp.float32) * 0.02
        A = jax.random.normal(k[3], (16, 16, 512), jnp.float32) * 0.02
        Bf = jax.random.normal(k[4], (16, 512, 16), jnp.float32) * 0.02
        coeffs = jax.random.uniform(k[5], (16,), jnp.float32)
        scales = jnp.full((16,), 0.5, jnp.float32)
        return {'x': x, 'W': W, 'bias': bias, 'A': A, 'Bf': Bf, 'coeffs': coeffs, 'scales': scales}
    _L1_ffn_in = _L1_ffn_setup()
    _d = {'L0_attn_x': _L0_attn_in['x'], 'L0_attn_w_gate': _L0_attn_in['w_gate'], 'L0_attn_w_up': _L0_attn_in['w_up'], 'L0_attn_w_down': _L0_attn_in['w_down'], 'L0_ffn_weight': _L0_ffn_in['weight'], 'L0_ffn_bias': _L0_ffn_in['bias'], 'L1_attn_Win': _L1_attn_in['Win'], 'L1_attn_bin': _L1_attn_in['bin'], 'L1_attn_ln1_w': _L1_attn_in['ln1_w'], 'L1_attn_ln1_b': _L1_attn_in['ln1_b'], 'L1_attn_phz_re': _L1_attn_in['phz_re'], 'L1_attn_phz_im': _L1_attn_in['phz_im'], 'L1_attn_lc_re': _L1_attn_in['lc_re'], 'L1_attn_lc_im': _L1_attn_in['lc_im'], 'L1_attn_sc_lin': _L1_attn_in['sc_lin'], 'L1_attn_ln2_w': _L1_attn_in['ln2_w'], 'L1_attn_ln2_b': _L1_attn_in['ln2_b'], 'L1_attn_W1': _L1_attn_in['W1'], 'L1_attn_b1': _L1_attn_in['b1'], 'L1_attn_W2': _L1_attn_in['W2'], 'L1_attn_b2': _L1_attn_in['b2'], 'L1_attn_lnl_w': _L1_attn_in['lnl_w'], 'L1_attn_lnl_b': _L1_attn_in['lnl_b'], 'L1_attn_Wout': _L1_attn_in['Wout'], 'L1_attn_bout': _L1_attn_in['bout'], 'L1_ffn_W': _L1_ffn_in['W'], 'L1_ffn_bias': _L1_ffn_in['bias'], 'L1_ffn_A': _L1_ffn_in['A'], 'L1_ffn_Bf': _L1_ffn_in['Bf'], 'L1_ffn_coeffs': _L1_ffn_in['coeffs'], 'L1_ffn_scales': _L1_ffn_in['scales']}
    _x0 = _d['L0_attn_x']
    _d['L0_attn_x'] = jax.random.normal(jax.random.fold_in(jax.random.key(seed), 1), (2, 1024, 512), dtype=_x0.dtype)
    del _x0
    return _d

def reference(L0_attn_x, L0_attn_w_gate, L0_attn_w_up, L0_attn_w_down, L0_ffn_weight, L0_ffn_bias, L1_attn_Win, L1_attn_bin, L1_attn_ln1_w, L1_attn_ln1_b, L1_attn_phz_re, L1_attn_phz_im, L1_attn_lc_re, L1_attn_lc_im, L1_attn_sc_lin, L1_attn_ln2_w, L1_attn_ln2_b, L1_attn_W1, L1_attn_b1, L1_attn_W2, L1_attn_b2, L1_attn_lnl_w, L1_attn_lnl_b, L1_attn_Wout, L1_attn_bout, L1_ffn_W, L1_ffn_bias, L1_ffn_A, L1_ffn_Bf, L1_ffn_coeffs, L1_ffn_scales):

    def _L0_attn_ref(x, w_gate, w_up, w_down):
        import jax, jax.numpy as jnp
        import numpy as np
        K_FACTOR = 0.5
        s = jax.nn.silu(jnp.einsum('bsh,ih->bsi', x, w_gate))
        B, S, I = s.shape
        k = int(K_FACTOR * I)
        _, idx = jax.lax.top_k(-jnp.abs(s), k)
        flat = s.reshape(B * S, I)
        rows = jnp.arange(B * S)[:, None]
        flat = flat.at[rows, idx.reshape(B * S, k)].set(0.0)
        s = flat.reshape(B, S, I)
        s = s * jnp.einsum('bsh,ih->bsi', x, w_up)
        return jnp.einsum('bsi,hi->bsh', s, w_down)

    def _L0_ffn_ref(x, weight, bias):
        import jax, jax.numpy as jnp
        import numpy as np

        def ternary_quantize(w):
            thresh = 0.7 * jnp.mean(jnp.abs(w), axis=-1, keepdims=True)
            q = jnp.where(w > thresh, 1.0, jnp.where(w < -thresh, -1.0, 0.0)).astype(w.dtype)
            return w + jax.lax.stop_gradient(q - w)
        q_weight = ternary_quantize(weight)
        return jnp.einsum('bsd,od->bso', x, q_weight) + bias

    def _L1_attn_ref(x, Win, bin, ln1_w, ln1_b, phz_re, phz_im, lc_re, lc_im, sc_lin, ln2_w, ln2_b, W1, b1, W2, b2, lnl_w, lnl_b, Wout, bout):
        import jax, jax.numpy as jnp
        import numpy as np
        DEPTH, DIM, DFF, VOCAB = (4, 64, 256, 512)
        EPS = 1e-05

        def layernorm(x, w, b):
            mu = jnp.mean(x, axis=-1, keepdims=True)
            var = jnp.mean((x - mu) ** 2, axis=-1, keepdims=True)
            return (x - mu) * jax.lax.rsqrt(var + EPS) * w + b

        def sconv(x, phazor_c, last_conv_c):
            B, L, D = x.shape
            r = jnp.abs(phazor_c)
            p = jnp.tanh(r) * jnp.exp(1j * jnp.angle(phazor_c))
            prog = p[None, :] ** jnp.arange(L, dtype=jnp.float32)[:, None]
            filt_fft = jnp.fft.fft(prog, n=2 * L, axis=0)
            x_fft = jnp.fft.fft(x.astype(jnp.complex64), n=2 * L, axis=1)
            conv = jnp.fft.ifft(filt_fft[None] * x_fft, axis=1)[:, :L]
            conv = conv + last_conv_c[None, None, :] * prog[None] * p[None, None, :]
            return conv.real.astype(x.dtype)

        def _forward(x, Win, bin, ln1_w, ln1_b, phz_re, phz_im, lc_re, lc_im, sc_lin, ln2_w, ln2_b, W1, b1, W2, b2, lnl_w, lnl_b, Wout, bout):
            h = jnp.einsum('blv,dv->bld', x, Win) + bin

            def body(h, p):
                l1w, l1b, pr, pi, lr, li, scl, l2w, l2b, w1, b1_, w2, b2_ = p
                y = jax.nn.silu(layernorm(h, l1w, l1b))
                y = sconv(y, pr + 1j * pi, lr + 1j * li)
                h = h + y * scl
                y = layernorm(h, l2w, l2b)
                y = jax.nn.silu(jnp.einsum('bld,fd->blf', y, w1) + b1_)
                y = jnp.einsum('blf,df->bld', y, w2) + b2_
                return (h + y, None)
            xs = (ln1_w, ln1_b, phz_re, phz_im, lc_re, lc_im, sc_lin, ln2_w, ln2_b, W1, b1, W2, b2)
            h, _ = jax.lax.scan(body, h, xs)
            h = layernorm(h, lnl_w, lnl_b)
            return jnp.einsum('bld,vd->blv', h, Wout) + bout
        return _forward(x, Win, bin, ln1_w, ln1_b, phz_re, phz_im, lc_re, lc_im, sc_lin, ln2_w, ln2_b, W1, b1, W2, b2, lnl_w, lnl_b, Wout, bout)

    def _L1_ffn_ref(x, W, bias, A, Bf, coeffs, scales):
        import jax, jax.numpy as jnp
        import numpy as np
        out = jnp.einsum('bsd,od->bso', x, W) + bias
        xa = jnp.einsum('bsd,erd->ebsr', x, A)
        w = coeffs * scales
        upd = jnp.einsum('ebsr,eor,e->bso', xa, Bf, w)
        return out + upd
    x = L0_attn_x
    xn = _layernorm(x, axis=-1)
    s = _L0_attn_ref(xn, L0_attn_w_gate, L0_attn_w_up, L0_attn_w_down)
    g = _silu(_L0_ffn_ref(xn, L0_ffn_weight, L0_ffn_bias))
    x = x + s * g
    xn = _layernorm(x, axis=-1)
    s = _L1_attn_ref(xn, L1_attn_Win, L1_attn_bin, L1_attn_ln1_w, L1_attn_ln1_b, L1_attn_phz_re, L1_attn_phz_im, L1_attn_lc_re, L1_attn_lc_im, L1_attn_sc_lin, L1_attn_ln2_w, L1_attn_ln2_b, L1_attn_W1, L1_attn_b1, L1_attn_W2, L1_attn_b2, L1_attn_lnl_w, L1_attn_lnl_b, L1_attn_Wout, L1_attn_bout)
    g = _silu(_L1_ffn_ref(xn, L1_ffn_W, L1_ffn_bias, L1_ffn_A, L1_ffn_Bf, L1_ffn_coeffs, L1_ffn_scales))
    x = x + s * g
    return x

_drawn_inputs = setup_inputs


def setup_inputs(seed=0):
    import zlib

    import numpy as np

    out = dict(_drawn_inputs(seed))
    spreads = {'L0_ffn_bias': (0.0, 0.8),
     'L1_attn_bin': (0.0, 0.643),
     'L1_attn_ln1_w': (1.0, 0.591),
     'L1_attn_ln1_b': (0.0, 0.67),
     'L1_attn_sc_lin': (1.0, 0.6),
     'L1_attn_ln2_w': (1.0, 0.6),
     'L1_attn_ln2_b': (0.0, 0.8),
     'L1_attn_b1': (0.0, 0.8),
     'L1_attn_b2': (0.0, 0.8),
     'L1_attn_lnl_w': (1.0, 0.6),
     'L1_attn_lnl_b': (0.0, 0.635),
     'L1_attn_bout': (0.0, 0.591),
     'L1_ffn_scales': (0.5, 0.6)}
    factors = {'L1_attn_lc_re': 8.0,
     'L1_attn_lc_im': 8.0,
     'L1_ffn_bias': 8.0,
     'L1_ffn_A': 3.618,
     'L1_ffn_Bf': 3.619,
     'L1_ffn_coeffs': 8.0}
    for name, (base, spread) in spreads.items():
        noise = np.random.default_rng([zlib.crc32(name.encode()), seed]).standard_normal(out[name].shape)
        drawn = base * np.exp(spread * noise) if base else spread * noise
        out[name] = jnp.asarray(drawn.astype(out[name].dtype))
    for name, factor in factors.items():
        out[name] = (out[name] * factor).astype(out[name].dtype)
    return out
```

```python
from contextlib import ExitStack

import concourse.bass as bass
from concourse import mybir

F32 = mybir.dt.float32
F32R = mybir.dt.float32r
I32 = mybir.dt.int32
I8 = mybir.dt.int8
ALU = mybir.AluOpType
ACT = mybir.ActivationFunctionType
AX_X = mybir.AxisListType.X
RADD = bass.bass_isa.ReduceOp.add

P = 128
EPS = 1e-5

TOKENS, HID, INNER = 2048, 512, 1376
KH = HID // P
TILES = TOKENS // P
PAIRS = TILES // 2
DROP = INNER // 2
NCOL = [(0, 512), (512, 1024), (1024, INNER)]
CHUNKS = -(-INNER // P)
PADDED = CHUNKS * P
GROUPS = [(0, 4), (4, 8), (8, CHUNKS)]
NG = len(GROUPS)
TERNARY = 0.7

STEPS = 8
LOW, HIGH = 0.6, 0.9
CANDS = STEPS + 1
ACT_COUNTS = STEPS + 2
PICKS = 12
N_CONST = 5 + STEPS + 2 + 8

BATCH, SEQ, DIM, DFF, DEPTH, VOCAB = 2, 1024, 64, 256, 4, 512
NB = 512
HALVES = SEQ // NB
COARSE = 32
EXPERTS, RANK = 16, 16
ER = EXPERTS * RANK
NPAR = 10
ROOT = 18
N_MK = 12
N_RAD = 7
N_SMALL = 18 + 2 * (2 + 5 * 15)
(C_L1W, C_L1B, C_PR, C_PI, C_LR, C_LI, C_SCL, C_L2W, C_L2B, C_B2) = range(NPAR)


def settled(engine, passed):
    engine.sem_inc(passed, 1)


def mixture_kernel(nc, x, wg_t, wu_t, wd_t, tern_w, ffn_bias, win_t, cols, last_cols, b1_cols,
                   w1_t, w2_t, wout_t, bout_cols, f1_w_t, f1_bias_cols, f1_a, f1_b_t,
                   f1_mix, out):
    x1_dram = nc.dram_tensor("x1_scratch", (TOKENS, HID), F32, kind="Internal").ap()
    pair_view = "(n t q) h -> q n t h"
    x_pairs = x.rearrange(pair_view, t=2, q=P)
    x1_pairs = x1_dram.rearrange(pair_view, t=2, q=P)

    with ExitStack() as ctx:
        def psum(name, shape):
            return ctx.enter_context(nc.psum_tensor(name, shape, F32))

        def sem(name):
            return ctx.enter_context(nc.semaphore(name))

        pool_passed, act_passed, dve_passed = sem("pool_passed"), sem("act_passed"), sem("dve_passed")

        ps_a = psum("ps_a", [P, 3, NB])
        ps_b = psum("ps_b", [P, 3, NB])
        ps_t = psum("ps_t", [P, 2, NB])

        with ExitStack() as actx:
            def sb(name, shape, dt=F32):
                return actx.enter_context(nc.sbuf_tensor(name, shape, dt))

            wg_hi = sb("wg_hi", [P, KH, INNER], F32R)
            wg_lo = sb("wg_lo", [P, KH, INNER], F32R)
            wu_hi = sb("wu_hi", [P, KH, INNER], F32R)
            wu_lo = sb("wu_lo", [P, KH, INNER], F32R)
            wd_hi = sb("wd_hi", [P, CHUNKS, HID], F32R)
            wd_lo = sb("wd_lo", [P, CHUNKS, HID], F32R)
            q_t = sb("q_t", [P, KH, HID], F32R)
            s_buf = sb("s_buf", [P, 2, INNER])
            k_buf = sb("k_buf", [P, 2, INNER])
            m_buf = sb("m_buf", [P, 2, PADDED])
            zt_hi = sb("zt_hi", [P, PADDED], F32R)
            zt_lo = sb("zt_lo", [P, PADDED], F32R)
            xin = sb("xin", [P, 2, HID])
            xres = sb("xres", [P, 2, HID])
            xt_hi = sb("xt_hi", [P, 2, HID], F32R)
            xt_lo = sb("xt_lo", [P, 2, HID], F32R)
            gate2 = sb("gate2", [P, 2, HID])
            bias_b = sb("bias_b", [P, HID])
            junk_d = sb("junk_d", [P, INNER], I8)
            junk_a = sb("junk_a", [P, INNER], I8)
            ident = sb("ident", [P, P])
            powers = sb("powers", [P, STEPS + 2, 2])
            widths = sb("widths", [P, STEPS + 2, 2])
            iota8 = sb("iota8", [P, 2, 8])
            mag_sum = sb("mag_sum", [P, 2])
            cand = sb("cand", [P, 2])
            cand_low = sb("cand_low", [P, 2])
            rise = sb("rise", [P, 2])
            below = sb("below", [P, 2])
            at_most = sb("at_most", [P, 2])
            rank = sb("rank", [P, 2])
            top8 = sb("top8", [P, 2, 8])
            pick = sb("pick", [P, 2, 8])
            tau = sb("tau", [P, 2])
            above = sb("above", [P, 2])
            bad = sb("bad", [P, 2])
            bad_all = sb("bad_all", [P, 2])
            bad_int = sb("bad_int", [P, 2], I32)
            bit = sb("bit", [P, 2], I32)
            lo_bits = sb("lo_bits", [P, 2], I32)
            cand_bits = sb("cand_bits", [P, 2], I32)
            set_bits = sb("set_bits", [P, 2], I32)
            stats = sb("stats", [P, 2, 6])
            mv = sb("mv", [P, 2, 2])
            var_eps = sb("var_eps", [P, 2])
            rstd = sb("rstd", [P, 2])
            expo = sb("expo", [P, 2])
            one = sb("one", [P, 1])
            mags, thr, thr_neg = (pick[:].rearrange("p t e -> p (t e)")[:, i * KH:(i + 1) * KH] for i in range(3))

            c_const = sem("c_const")
            x_in = sem("x_in")
            x_res = sem("x_res")
            bias_in = sem("bias_in")
            tern_in = sem("tern_in")
            w_in = [sem(f"w_in{i}") for i in range(4)]
            w_hi = sem("w_hi")
            w_lo = sem("w_lo")
            t_mag = sem("t_mag")
            t_thr = sem("t_thr")
            t_neg = sem("t_neg")
            t_q = sem("t_q")
            t_tr = sem("t_tr")
            t_cp = sem("t_cp")
            ln_st = sem("ln_st")
            ln_mv = sem("ln_mv")
            ln_ve = sem("ln_ve")
            ln_rs = sem("ln_rs")
            xn_ready = sem("xn_ready")
            xt_psum = sem("xt_psum")
            xt_h = sem("xt_h")
            xt_l = sem("xt_l")
            gate_done = sem("gate_done")
            up_done = sem("up_done")
            s_ready = sem("s_ready")
            k_ready = sem("k_ready")
            z_ready = sem("z_ready")
            wid_ready = sem("wid_ready")
            cand_ready = sem("cand_ready")
            candlow_ready = sem("candlow_ready")
            rise_ready = sem("rise_ready")
            cnt_dve = sem("cnt_dve")
            cnt_act = sem("cnt_act")
            small_ready = sem("small_ready")
            top_ready = sem("top_ready")
            picked = sem("picked")
            bad_sum = sem("bad_sum")
            mask_ready = sem("mask_ready")
            zt_psum = sem("zt_psum")
            zt_h = sem("zt_h")
            zt_l = sem("zt_l")
            down_done = sem("down_done")
            down_out = sem("down_out")
            x1_ready = sem("x1_ready")
            x1_out = sem("x1_out")
            q_done = sem("q_done")
            q_biased = sem("q_biased")
            g_ready = sem("g_ready")

            units = []
            for w, hi, lo in ((wg_t, wg_hi, wg_lo), (wu_t, wu_hi, wu_lo)):
                for k in range(KH):
                    units.append((w[k * P:(k + 1) * P, :], P, hi[:, k, :], lo[:, k, :], None))
            N_GU = len(units)
            for c in range(0, CHUNKS - 1, 2):
                units.append((wd_t[c * P:(c + 2) * P, :].rearrange("(c p) n -> p c n", c=2), P,
                              wd_hi[:, c:c + 2, :], wd_lo[:, c:c + 2, :], 2))
            last_rows = INNER - (CHUNKS - 1) * P
            units.append((wd_t[(CHUNKS - 1) * P:INNER, :], last_rows,
                          wd_hi[0:last_rows, CHUNKS - 1, :], wd_lo[0:last_rows, CHUNKS - 1, :], None))

            def slot_of(u):
                return u % 4 if u < N_GU else u % 2

            def slot_ap(u):
                _, rows, hi, _, parts = units[u]
                buf = (m_buf[:, 0, :], m_buf[:, 1, :], k_buf[:, 0, :], k_buf[:, 1, :])[slot_of(u)]
                n = HID * (parts or 1) if u >= N_GU else INNER
                ap = buf[0:rows, 0:n]
                return ap.rearrange("p (c n) -> p c n", c=parts) if parts else ap

            def loads_before(u):
                return sum(slot_of(v) == slot_of(u) for v in range(u + 1))

            block_a = actx.enter_context(nc.Block())

            def col(ap, n):
                return ap.rearrange("p (t o) -> p t o", o=1).to_broadcast([P, 2, n])

            @block_a.sync
            def _(sp):
                def load_x(dst, done, p):
                    sp.dma_start(dst[:].rearrange("q (n t) h -> q n t h", n=1),
                                 x_pairs[:, bass.ds(p, 1), :, :]).then_inc(done, 16)

                load_x(xin, x_in, 0)
                for t in range(2):
                    sp.dma_start(s_buf[:, t, 0:2 * HID].rearrange("p (k n) -> p k n", k=2),
                                 tern_w[2 * P * t:2 * P * (t + 1), :].rearrange("(k p) n -> p k n", p=P)
                                 ).then_inc(tern_in, 16)
                for u in range(len(units)):
                    prev = [v for v in range(u) if slot_of(v) == slot_of(u)]
                    if prev:
                        sp.wait_ge(w_lo, prev[-1] + 1)
                        sp.wait_ge(w_hi, prev[-1] + 1)
                    sp.dma_start(slot_ap(u), units[u][0]).then_inc(w_in[slot_of(u)], 16)
                    if u == 3:
                        sp.dma_start(bias_b[:], ffn_bias.partition_broadcast(P)).then_inc(bias_in, 16)
                sp.wait_ge(xt_psum, 2)
                load_x(xin, x_in, 1)

                def pair(p, ahead):
                    if ahead:
                        sp.wait_ge(xt_psum, 2 * p + 2)
                        load_x(xin, x_in, p + 1)
                    sp.wait_ge(x1_out, 16 * (p - 1))
                    load_x(xres, x_res, p - 1)
                    sp.wait_ge(x1_ready, 2 * p)
                    sp.dma_start(x1_pairs[:, bass.ds(p - 1, 1), :, :],
                                 xres[:].rearrange("q (n t) h -> q n t h", n=1)).then_inc(x1_out, 16)

                with sp.Fori(1, PAIRS - 1) as p:
                    pair(p, True)
                pair(PAIRS - 1, False)
                pair(PAIRS, False)
                sp.wait_ge(x1_out, 16 * PAIRS)

            @block_a.gpsimd
            def _(pool):
                pool.memset(ident[:], 0.0).then_inc(c_const, 1)
                pool.wait_ge(c_const, 1)
                pool.affine_select(out=ident[:], in_=ident[:], compare_op=ALU.not_equal, fill=1.0, base=0,
                                   pattern=[[-1, P]], channel_multiplier=1).then_inc(c_const, 1)
                pool.memset(expo[:], -0.5).then_inc(c_const, 1)
                pool.memset(one[:], 1.0).then_inc(c_const, 1)
                pool.memset(m_buf[:, :, INNER:PADDED], 0.0).then_inc(c_const, 1)
                for j in range(STEPS + 2):
                    pool.memset(powers[:, j, :], (HIGH - LOW) / INNER / 2 ** j).then_inc(c_const, 1)
                for j in range(8):
                    pool.memset(iota8[:, :, j:j + 1], float(j)).then_inc(c_const, 1)
                pool.wait_ge(c_const, N_CONST)

                def root(p):
                    pool.wait_ge(ln_ve, p + 1)
                    pool.tensor_tensor(rstd[:], var_eps[:], expo[:], ALU.pow).then_inc(ln_rs, 1)

                def residual(p):
                    for t in range(2):
                        if t == 0:
                            pool.wait_ge(x_res, 16 * p)
                        pool.wait_ge(down_out, 2 * (p - 1) + t + 1)
                        pool.tensor_tensor(xres[:, t, :], xres[:, t, :], gate2[:, t, :],
                                           ALU.add).then_inc(x1_ready, 1)

                def check_sum(p):
                    pool.wait_ge(picked, PICKS * p + PICKS - 1)
                    settled(pool, pool_passed)
                    pool.partition_all_reduce(bad_all[:], bad[:], P, RADD).then_inc(bad_sum, 1)

                root(0)
                root(1)
                check_sum(0)
                with pool.Fori(1, PAIRS - 1) as p:
                    root(p + 1)
                    residual(p)
                    check_sum(p)
                residual(PAIRS - 1)
                check_sum(PAIRS - 1)
                residual(PAIRS)

            @block_a.scalar
            def _(act):
                def split_hi(u):
                    act.wait_ge(w_in[slot_of(u)], 16 * loads_before(u))
                    act.activation(units[u][2], slot_ap(u), ACT.Copy).then_inc(w_hi, 1)

                def xt_high(p, t):
                    act.wait_ge(xt_psum, 2 * p + t + 1)
                    act.activation(xt_hi[:, t, :], ps_t[:, t, :], ACT.Copy).then_inc(xt_h, 1)

                act.wait_ge(tern_in, 32)
                for k in range(KH):
                    if k:
                        act.wait_ge(t_mag, k)
                    act.activation(junk_a[:, 0:HID], s_buf[:, k // 2, (k % 2) * HID:(k % 2 + 1) * HID],
                                   ACT.Abs, accum_out=mags[:, k:k + 1]).then_inc(t_mag, 1)
                for t in range(2):
                    xt_high(0, t)
                for u in range(N_GU):
                    split_hi(u)

                def silu_keys(p, t, wait_free):
                    act.wait_ge(gate_done, 2 * p + t + 1)
                    if not wait_free:
                        act.wait_ge(w_lo, N_GU)
                    if wait_free:
                        act.wait_ge(mask_ready, 2 * p + t - 1)
                    act.activation(s_buf[:, t, :], ps_a[:].rearrange("p a n -> p (a n)")[:, 0:INNER],
                                   ACT.Silu).then_inc(s_ready, 1)
                    act.wait_ge(s_ready, 2 * p + t + 1)
                    act.activation(k_buf[:, t, :], s_buf[:, t, :], ACT.Abs,
                                   accum_out=mag_sum[:, t:t + 1]).then_inc(k_ready, 1)

                def count_b(p, n):
                    act.wait_ge(cand_ready, CANDS * p + n + 1)
                    act.activation(junk_a[:], k_buf[:, 1, :], ACT.Sign, bias=cand[:, 1:2], scale=-1.0,
                                   accum_out=below[:, 1:2]).then_inc(cnt_act, 1)

                def count_last(p):
                    act.wait_ge(cand_ready, CANDS * p + STEPS + 1)
                    for t in range(2):
                        act.wait_ge(cnt_act, ACT_COUNTS * p + STEPS + t)
                        act.activation(junk_a[:], k_buf[:, t, :], ACT.Sign, bias=cand[:, t:t + 1], scale=-1.0,
                                       accum_out=at_most[:, t:t + 1]).then_inc(cnt_act, 1)

                def zt_high(p, i):
                    n = 2 * NG * (p - 1) + i
                    c0, c1 = GROUPS[i % NG]
                    act.wait_ge(zt_psum, n + 1)
                    if not (isinstance(n, int) and n < NG):
                        act.wait_ge(down_done, n - NG + 1)
                    act.activation(zt_hi[:, c0 * P:c1 * P], ps_t[:, i % 2, 0:(c1 - c0) * P],
                                   ACT.Copy).then_inc(zt_h, 1)

                def gate_silu(p):
                    for t in range(2):
                        act.wait_ge(q_biased, 2 * p + t + 1)
                        act.activation(gate2[:, t, :], gate2[:, t, :], ACT.Silu).then_inc(g_ready, 1)

                def pair(p, back, ahead, first=False):
                    for t in range(2):
                        silu_keys(p, t, not first)
                    if first:
                        for u in range(N_GU, len(units)):
                            split_hi(u)
                    count_b(p, 0)
                    count_b(p, 1)
                    if back:
                        zt_high(p, 0)
                        zt_high(p, 1)
                    for i in range(2, 6):
                        count_b(p, i)
                        if back:
                            zt_high(p, i)
                    count_b(p, 6)
                    count_b(p, 7)
                    count_last(p)
                    if ahead:
                        for t in range(2):
                            xt_high(p + 1, t)
                    gate_silu(p)

                pair(0, False, True, first=True)
                pair(1, True, True)
                with act.Fori(2, PAIRS - 1) as p:
                    pair(p, True, True)
                pair(PAIRS - 1, True, False)
                for i in range(2 * NG):
                    zt_high(PAIRS, i)

            @block_a.vector
            def _(dve):
                def split_lo(u):
                    dve.wait_ge(w_hi, u + 1)
                    dve.tensor_tensor(units[u][3], slot_ap(u), units[u][2].bitcast(F32),
                                      ALU.subtract).then_inc(w_lo, 1)

                def xt_low(p, t):
                    dve.wait_ge(xt_h, 2 * p + t + 1)
                    dve.tensor_tensor(xt_lo[:, t, :], ps_t[:, t, :], xt_hi[:, t, :].bitcast(F32),
                                      ALU.subtract).then_inc(xt_l, 1)

                def norm_stats(p):
                    dve.wait_ge(x_in, 16 * (p + 1))
                    for t in range(2):
                        dve.bn_stats(stats[:, t, :], xin[:, t, :]).then_inc(ln_st, 1)
                    for t in range(2):
                        dve.wait_ge(ln_st, 2 * p + t + 1)
                        settled(dve, dve_passed)
                        dve.bn_aggr(mv[:, t, :], stats[:, t, :]).then_inc(ln_mv, 1)
                    dve.wait_ge(ln_mv, 2 * p + 2)
                    dve.tensor_scalar(var_eps[:], mv[:, :, 1], EPS, None, ALU.add).then_inc(ln_ve, 1)

                def norm_apply(p):
                    dve.wait_ge(ln_rs, p + 1)
                    for t in range(2):
                        dve.tensor_scalar(xin[:, t, :], xin[:, t, :], mv[:, t, 0:1], rstd[:, t:t + 1],
                                          ALU.subtract, ALU.mult).then_inc(xn_ready, 1)

                norm_stats(0)
                norm_apply(0)
                for k in range(KH):
                    dve.wait_ge(t_mag, k + 1)
                    dve.tensor_scalar(thr[:, k:k + 1], mags[:, k:k + 1], 1.0 / HID, TERNARY,
                                      ALU.mult, ALU.mult).then_inc(t_thr, 1)
                    dve.wait_ge(t_thr, 2 * k + 1)
                    dve.tensor_scalar(thr_neg[:, k:k + 1], thr[:, k:k + 1], -1.0, None,
                                      ALU.mult).then_inc(t_thr, 1)
                    w = s_buf[:, k // 2, (k % 2) * HID:(k % 2 + 1) * HID]
                    neg = gate2[:, k % 2, :]
                    dve.wait_ge(t_thr, 2 * k + 2)
                    if k >= 2:
                        dve.wait_ge(t_q, k - 1)
                    dve.tensor_scalar(neg, w, thr_neg[:, k:k + 1], None, ALU.is_lt).then_inc(t_neg, 1)
                    dve.wait_ge(t_neg, k + 1)
                    dve.scalar_tensor_tensor(out=w, in0=w, scalar=thr[:, k:k + 1], in1=neg,
                                             op0=ALU.is_gt, op1=ALU.subtract).then_inc(t_q, 1)
                for t in range(2):
                    xt_low(0, t)
                for k in range(KH):
                    dve.wait_ge(t_tr, k + 1)
                    dve.tensor_copy(q_t[:, k, :], ps_b[:, k % 3, :]).then_inc(t_cp, 1)
                for u in range(N_GU):
                    split_lo(u)

                def product(p, t):
                    dve.wait_ge(up_done, 2 * p + t + 1)
                    dve.wait_ge(k_ready, 2 * p + t + 1)
                    dve.tensor_tensor(s_buf[:, t, :], s_buf[:, t, :],
                                      ps_b[:].rearrange("p a n -> p (a n)")[:, 0:INNER],
                                      ALU.mult).then_inc(z_ready, 1)

                def bracket(p):
                    dve.wait_ge(k_ready, 2 * p + 2)
                    dve.tensor_tensor(widths[:], powers[:],
                                      mag_sum[:].rearrange("p (o t) -> p o t", o=1).to_broadcast(
                                          [P, STEPS + 2, 2]), ALU.mult).then_inc(wid_ready, 1)
                    dve.tensor_scalar(cand[:], mag_sum[:], (LOW + HIGH) / 2 / INNER, None,
                                      ALU.mult).then_inc(cand_ready, 1)

                def halve(p, n):
                    dve.wait_ge(cand_ready, CANDS * p + n + 1)
                    if n == 0:
                        dve.wait_ge(wid_ready, p + 1)
                    if n < STEPS - 1:
                        dve.tensor_tensor(cand_low[:], cand[:], widths[:, n + 2, :],
                                          ALU.subtract).then_inc(candlow_ready, 1)
                    else:
                        dve.tensor_copy(cand_low[:], cand[:]).then_inc(candlow_ready, 1)
                    dve.tensor_scalar(junk_d[:], k_buf[:, 0, :], cand[:, 0:1], -float(DROP),
                                      ALU.is_lt, ALU.add, accum_out=below[:, 0:1]).then_inc(cnt_dve, 1)
                    dve.wait_ge(cnt_dve, STEPS * p + n + 1)
                    dve.wait_ge(cnt_act, ACT_COUNTS * p + n + 1)
                    dve.scalar_tensor_tensor(out=rise[:], in0=below[:], scalar=0.0, in1=widths[:, n + 1, :],
                                             op0=ALU.is_lt, op1=ALU.mult).then_inc(rise_ready, 1)
                    dve.wait_ge(rise_ready, STEPS * p + n + 1)
                    dve.wait_ge(candlow_ready, STEPS * p + n + 1)
                    dve.tensor_tensor(cand[:], cand_low[:], rise[:], ALU.add).then_inc(cand_ready, 1)

                def largest_under(p, t, back):
                    dve.wait_ge(cand_ready, CANDS * p + STEPS + 1)
                    if back:
                        dve.wait_ge(zt_psum, 2 * NG * (p - 1) + NG * (t + 1))
                    dve.scalar_tensor_tensor(out=m_buf[:, t, 0:INNER], in0=k_buf[:, t, :],
                                             scalar=cand[:, t:t + 1], in1=k_buf[:, t, :],
                                             op0=ALU.is_le, op1=ALU.mult).then_inc(small_ready, 1)
                    dve.wait_ge(small_ready, 2 * p + t + 1)
                    settled(dve, dve_passed)
                    dve.max(top8[:, t, :], m_buf[:, t, 0:INNER]).then_inc(top_ready, 1)

                def choose(p):
                    done = [PICKS * p]

                    def step(ins):
                        done[0] = done[0] + 1
                        ins.then_inc(picked, 1)
                        dve.wait_ge(picked, done[0])

                    dve.wait_ge(cnt_act, ACT_COUNTS * (p + 1))
                    dve.wait_ge(top_ready, 2 * p + 2)
                    step(dve.tensor_scalar(rank[:], at_most[:], 0.5, 0.25, ALU.mult, ALU.add))
                    step(dve.tensor_tensor(pick[:], iota8[:], col(rank[:], 8), ALU.subtract))
                    step(dve.tensor_tensor(pick[:], pick[:], pick[:], ALU.mult))
                    step(dve.scalar_tensor_tensor(out=pick[:], in0=pick[:], scalar=0.1, in1=top8[:],
                                                  op0=ALU.is_lt, op1=ALU.mult))
                    step(dve.tensor_reduce(tau[:], pick[:], AX_X, ALU.add))
                    step(dve.tensor_tensor(pick[:], top8[:], col(tau[:], 8), ALU.is_gt))
                    step(dve.tensor_reduce(above[:], pick[:], AX_X, ALU.add))
                    step(dve.tensor_tensor(above[:], above[:], rank[:], ALU.subtract))
                    step(dve.tensor_tensor(above[:], above[:], above[:], ALU.mult))
                    step(dve.tensor_scalar(bad[:], tau[:], 0.0, None, ALU.is_le))
                    step(dve.scalar_tensor_tensor(out=bad[:], in0=above[:], scalar=0.1, in1=bad[:],
                                                  op0=ALU.is_gt, op1=ALU.max))
                    dve.wait_ge(bad_sum, p + 1)
                    step(dve.tensor_tensor(bad_int[:, 0:1], bad_all[:, 0:1], bad_all[:, 1:2], ALU.add))
                    settled(dve, dve_passed)
                    failed = dve.value_load(bad_int[0:1, 0:1], min_val=0, max_val=2 * P)
                    with dve.If(failed > 0):
                        exact_choice()

                def exact_choice():
                    dve.memset(lo_bits[:], 0)
                    dve.memset(bit[:], 1 << 30)
                    dve.drain()
                    with dve.Fori(0, 31):
                        dve.tensor_tensor(cand_bits[:], lo_bits[:], bit[:], ALU.bitwise_or)
                        dve.drain()
                        for t in range(2):
                            dve.tensor_scalar(junk_d[:], k_buf[:, t, :], cand_bits[:, t:t + 1].bitcast(F32),
                                              -float(DROP), ALU.is_lt, ALU.add, accum_out=above[:, t:t + 1])
                            dve.drain()
                        dve.scalar_tensor_tensor(out=set_bits[:], in0=above[:], scalar=0.0, in1=bit[:],
                                                 op0=ALU.is_lt, op1=ALU.mult)
                        dve.drain()
                        dve.tensor_tensor(lo_bits[:], lo_bits[:], set_bits[:], ALU.bitwise_or)
                        dve.tensor_scalar(bit[:], bit[:], 1, None, ALU.logical_shift_right)
                        dve.drain()
                    dve.tensor_copy(tau[:], lo_bits[:].bitcast(F32))
                    dve.drain()
                    for t in range(2):
                        keys, tau_t = k_buf[:, t, :], tau[:, t:t + 1]
                        equal, seen = m_buf[:, 0, 0:INNER], m_buf[:, 1, 0:INNER]
                        dve.tensor_scalar(junk_d[:], keys, tau_t, -float(DROP), ALU.is_lt, ALU.add,
                                          accum_out=above[:, t:t + 1])
                        dve.tensor_scalar(equal, keys, tau_t, None, ALU.is_equal)
                        dve.drain()
                        dve.tensor_scalar(above[:, t:t + 1], above[:, t:t + 1], -1.0, None, ALU.mult)
                        dve.tensor_tensor_scan(seen, one[:].to_broadcast([P, INNER]), equal, 0.0,
                                               ALU.mult, ALU.add)
                        dve.drain()
                        dve.scalar_tensor_tensor(out=seen, in0=seen, scalar=above[:, t:t + 1], in1=equal,
                                                 op0=ALU.is_gt, op1=ALU.mult)
                        dve.drain()
                        dve.scalar_tensor_tensor(out=keys, in0=seen, scalar=3.0e38, in1=keys,
                                                 op0=ALU.mult, op1=ALU.max)
                        dve.drain()

                def mask(p):
                    for t in range(2):
                        dve.wait_ge(z_ready, 2 * p + t + 1)
                        dve.scalar_tensor_tensor(out=m_buf[:, t, 0:INNER], in0=k_buf[:, t, :],
                                                 scalar=tau[:, t:t + 1], in1=s_buf[:, t, :],
                                                 op0=ALU.is_gt, op1=ALU.mult).then_inc(mask_ready, 1)

                def zt_low(p, i):
                    n = 2 * NG * (p - 1) + i
                    c0, c1 = GROUPS[i % NG]
                    dve.wait_ge(zt_h, n + 1)
                    dve.tensor_tensor(zt_lo[:, c0 * P:c1 * P], ps_t[:, i % 2, 0:(c1 - c0) * P],
                                      zt_hi[:, c0 * P:c1 * P].bitcast(F32), ALU.subtract).then_inc(zt_l, 1)

                def down_gate(p, t):
                    dve.wait_ge(down_done, 2 * NG * (p - 1) + NG * (t + 1))
                    dve.wait_ge(g_ready, 2 * (p - 1) + t + 1)
                    dve.tensor_tensor(gate2[:, t, :], ps_a[:, t, :], gate2[:, t, :],
                                      ALU.mult).then_inc(down_out, 1)

                def q_bias(p, t, back):
                    dve.wait_ge(q_done, 2 * p + t + 1)
                    if back:
                        dve.wait_ge(x1_ready, 2 * (p - 1) + t + 1)
                    dve.tensor_tensor(gate2[:, t, :], ps_b[:, t, :], bias_b[:], ALU.add).then_inc(q_biased, 1)

                def pair(p, back, ahead, first=False):
                    product(p, 0)
                    if first:
                        for u in range(N_GU, len(units)):
                            split_lo(u)
                    if ahead:
                        norm_stats(p + 1)
                    bracket(p)
                    halve(p, 0)
                    halve(p, 1)
                    product(p, 1)
                    if back:
                        zt_low(p, 0)
                        zt_low(p, 1)
                    if ahead:
                        norm_apply(p + 1)
                    for i in range(2, 6):
                        halve(p, i)
                        if back:
                            zt_low(p, i)
                    if back:
                        down_gate(p, 0)
                    halve(p, 6)
                    halve(p, 7)
                    if back:
                        down_gate(p, 1)
                    largest_under(p, 0, back)
                    if ahead:
                        for t in range(2):
                            xt_low(p + 1, t)
                    largest_under(p, 1, back)
                    if first:
                        dve.wait_ge(bias_in, 16)
                    for t in range(2):
                        q_bias(p, t, back)
                    choose(p)
                    mask(p)

                pair(0, False, True, first=True)
                pair(1, True, True)
                with dve.Fori(2, PAIRS - 1) as p:
                    pair(p, True, True)
                pair(PAIRS - 1, True, False)
                for i in range(2 * NG):
                    zt_low(PAIRS, i)
                for t in range(2):
                    down_gate(PAIRS, t)

            @block_a.tensor
            def _(pe):
                def x_transpose(p, t):
                    pe.wait_ge(xn_ready, 2 * p + t + 1)
                    for k in range(KH):
                        last = pe.transpose(ps_t[:, t, k * P:(k + 1) * P], xin[:, t, k * P:(k + 1) * P], ident[:])
                    last.then_inc(xt_psum, 1)

                def project(p, t, hi, lo, bank, done, unit0):
                    for k in range(KH):
                        if isinstance(p, int) and p == 0 and t == 0:
                            pe.wait_ge(w_lo, unit0 + k + 1)
                        xh, xl = xt_hi[:, t, k * P:(k + 1) * P], xt_lo[:, t, k * P:(k + 1) * P]
                        for n, (xs, ws) in enumerate(((xh, hi), (xh, lo), (xl, hi))):
                            for c, (c0, c1) in enumerate(NCOL):
                                last = pe.matmul(bank[:, c, 0:c1 - c0], xs, ws[:, k, c0:c1],
                                                 start=(k == 0 and n == 0), stop=(k == KH - 1 and n == 2))
                    last.then_inc(done, 1)

                def zt_transpose(p, i):
                    n = 2 * NG * (p - 1) + i
                    t, (c0, c1) = i // NG, GROUPS[i % NG]
                    pe.wait_ge(mask_ready, 2 * (p - 1) + t + 1)
                    if not (isinstance(n, int) and n < 2):
                        pe.wait_ge(zt_l, n - 1)
                    for c in range(c0, c1):
                        last = pe.transpose(ps_t[:, i % 2, (c - c0) * P:(c - c0 + 1) * P],
                                            m_buf[:, t, c * P:(c + 1) * P], ident[:])
                    last.then_inc(zt_psum, 1)

                def down(p, i):
                    t, (c0, c1) = i // NG, GROUPS[i % NG]
                    pe.wait_ge(zt_l, 2 * NG * (p - 1) + i + 1)
                    if isinstance(p, int) and p == 1:
                        pe.wait_ge(w_lo, len(units))
                    for c in range(c0, c1):
                        rows = min(P, INNER - c * P)
                        zh = zt_hi[0:rows, c * P:(c + 1) * P]
                        zl = zt_lo[0:rows, c * P:(c + 1) * P]
                        for n, (zs, ws) in enumerate(((zh, wd_hi), (zh, wd_lo), (zl, wd_hi))):
                            last = pe.matmul(ps_a[:, t, :], zs, ws[0:rows, c, :],
                                             start=(c == 0 and n == 0), stop=(c == CHUNKS - 1 and n == 2))
                    last.then_inc(down_done, 1)

                def ternary(p, t):
                    for k in range(KH):
                        for n, xs in enumerate((xt_hi, xt_lo)):
                            last = pe.matmul(ps_b[:, t, :], xs[:, t, k * P:(k + 1) * P], q_t[:, k, :],
                                             start=(k == 0 and n == 0), stop=(k == KH - 1 and n == 1))
                    last.then_inc(q_done, 1)

                def back_half(p):
                    order = [("T", 0), ("T", 1), ("D", 0)]
                    for i in range(2, 2 * NG):
                        order += [("T", i), ("D", i - 1)]
                    order.append(("D", 2 * NG - 1))
                    for kind, i in order:
                        (zt_transpose if kind == "T" else down)(p, i)

                def pair(p, back, ahead):
                    for t in range(2):
                        pe.wait_ge(xt_l, 2 * p + t + 1)
                        if t == 1:
                            pe.wait_ge(s_ready, 2 * p + 1)
                        elif not (isinstance(p, int) and p < 2):
                            pe.wait_ge(down_out, 2 * (p - 1))
                        project(p, t, wg_hi, wg_lo, ps_a, gate_done, 0)
                        if t == 1:
                            pe.wait_ge(z_ready, 2 * p + 1)
                        elif not (isinstance(p, int) and p == 0):
                            pe.wait_ge(q_biased, 2 * p)
                        project(p, t, wu_hi, wu_lo, ps_b, up_done, KH)
                    if back:
                        pe.wait_ge(s_ready, 2 * p + 2)
                        back_half(p)
                    for t in range(2):
                        if t == 0:
                            pe.wait_ge(z_ready, 2 * p + 2)
                        ternary(p, t)
                        if ahead:
                            x_transpose(p + 1, t)

                pe.wait_ge(c_const, 2)
                for t in range(2):
                    x_transpose(0, t)
                for k in range(KH):
                    pe.wait_ge(t_q, KH)
                    if k == 3:
                        pe.wait_ge(t_cp, 1)
                    for o in range(KH):
                        last = pe.transpose(ps_b[:, k % 3, o * P:(o + 1) * P],
                                            s_buf[:, o // 2, (o % 2) * HID + k * P:(o % 2) * HID + (k + 1) * P],
                                            ident[:])
                    last.then_inc(t_tr, 1)
                pe.wait_ge(t_cp, KH)
                pair(0, False, True)
                pair(1, True, True)
                with pe.Fori(2, PAIRS - 1) as p:
                    pair(p, True, True)
                pair(PAIRS - 1, True, False)
                back_half(PAIRS)

        with ExitStack() as bctx:
            def sb(name, shape, dt=F32):
                return bctx.enter_context(nc.sbuf_tensor(name, shape, dt))

            x1 = sb("x1", [P, TILES, HID])
            work = sb("work", [P, 4 * SEQ])
            xn = work[:].rearrange("p (t n) -> p t n", n=HID)
            w_re, w_im, u_re, u_im = (work[:, j * SEQ:(j + 1) * SEQ] for j in range(4))
            xt = sb("xt", [P, KH, TOKENS])
            weff = sb("weff", [P, KH, HID])
            g2 = sb("g2", [P, VOCAB // P, TOKENS])
            fold = sb("fold", [P, 8, HID])
            f_a, f_b, f_wt = fold[:, 0:2, :], fold[:, 2:4, :], fold[:, 4:8, :]
            hs, res = fold[:, 0:4, :], fold[:, 4:8, :]
            f_w = sb("f_w", [P, 2, ER // P])
            f_bias = sb("f_bias", [P, VOCAB // P])
            bout_c = sb("bout_c", [P, VOCAB // P])
            win = sb("win", [P, BATCH, KH, P])
            par = sb("par", [P, DEPTH * NPAR])
            par_last = sb("par_last", [P, 3])
            b1_c = sb("b1_c", [P, DEPTH * 2])
            w1 = sb("w1", [P, DFF])
            w2 = sb("w2", [P, BATCH, 2, P])
            wout = sb("wout", [P, VOCAB])
            ident2 = sb("ident2", [P, P])
            center = sb("center", [P, P])
            means = sb("means", [P, 2])
            expo2 = sb("expo2", [P, 16])
            stats2 = sb("stats2", [P, TILES, 6])
            mv2 = sb("mv2", [P, TILES, 2])
            ve2 = sb("ve2", [P, TILES])
            rs2 = sb("rs2", [P, TILES])
            h = sb("h", [P, SEQ])
            y = sb("y", [P, SEQ])
            xc = sb("xc", [P, SEQ])
            sq = sb("sq", [P, SEQ])
            lnv = sb("lnv", [P, HALVES, 8])
            lnr = sb("lnr", [P, HALVES, 8])
            rot_c = sb("rot_c", [P, DEPTH, SEQ])
            rot_s = sb("rot_s", [P, DEPTH, SEQ])
            small = sb("small", [P, 4, DEPTH, COARSE])
            tmp = sb("tmp", [P, 4, DEPTH, COARSE // 2])
            tbig = sb("tbig", [P, SEQ])
            e_re = sb("e_re", [P, DEPTH])
            e_im = sb("e_im", [P, DEPTH])
            e_t = sb("e_t", [P, 4, DEPTH])
            e_s = sb("e_s", [P, 4])
            rad = sb("rad", [P, DEPTH])
            rho = sb("rho", [P, DEPTH])
            u0 = sb("u0", [P, 2, DEPTH])

            x1_in = [sem(f"x1_in{i}") for i in range(4)]
            par_in = sem("par_in")
            win_in = sem("win_in")
            f_in = sem("f_in")
            last_in = sem("last_in")
            lay_in = sem("lay_in")
            mk = sem("mk")
            st2 = sem("st2")
            mv2_s = sem("mv2_s")
            ve2_s = sem("ve2_s")
            rs2_s = sem("rs2_s")
            xn_s = sem("xn_s")
            xt_ps = sem("xt_ps")
            xt_a = sem("xt_a")
            xt_v = sem("xt_v")
            h_ps = sem("h_ps")
            h_ready = sem("h_ready")
            fold_w = sem("fold_w")
            fold_b = sem("fold_b")
            full = sem("full")
            free = sem("free")
            tb = sem("tb")
            rho_s = sem("rho_s")
            ln_cent = sem("ln_cent")
            ln_xc = sem("ln_xc")
            ln_sq = sem("ln_sq")
            ln_var = sem("ln_var")
            ln_v = sem("ln_v")
            ln_r = sem("ln_r")
            ln_bc = sem("ln_bc")
            ln_y = sem("ln_y")
            ln_o = sem("ln_o")
            cv_wr = sem("cv_wr")
            cv_wi = sem("cv_wi")
            cv_ur = sem("cv_ur")
            cv_ui = sem("cv_ui")
            cv_a = sem("cv_a")
            cv_b = sem("cv_b")
            cv_ab = sem("cv_ab")
            ff_2 = sem("ff_2")
            r_ready = sem("r_ready")
            o_ps = sem("o_ps")
            o_ready = sem("o_ready")
            o_out = sem("o_out")

            bank1 = [ps_a[:, 0, :], ps_a[:, 1, :]]
            bank2 = [ps_a[:, 2, :], ps_b[:, 0, :]]
            bankv = [ps_b[:, 1, :], ps_b[:, 2, :]]
            bankx = [ps_t[:, 0, :], ps_t[:, 1, :]]
            obank = bank1 + bank2
            ORDER = [0, 2, 1, 3]
            FOLD = KH
            UNITS = 4 + 2 * 4

            def use(l, k):
                return FOLD + UNITS * l + k

            def cs(c):
                return slice(c * NB, (c + 1) * NB)

            def pcol(l, j):
                return par[:, bass.ds(NPAR * l + j, 1)]

            block_b = bctx.enter_context(nc.Block())

            @block_b.sync
            def _(sp):
                def both(dst, src, done):
                    for b in range(BATCH):
                        sp.dma_start(dst[b * DIM:(b + 1) * DIM, :], src).then_inc(done, 16)

                def x1_group(g):
                    sp.dma_start(x1[:, 4 * g:4 * g + 4, :],
                                 x1_dram[4 * g * P:4 * (g + 1) * P, :].rearrange("(t q) h -> q t h", q=P)
                                 ).then_inc(x1_in[g], 16)

                x1_group(0)
                both(par, cols, par_in)
                both(par_last, last_cols, par_in)
                sp.dma_start(b1_c[:], b1_cols).then_inc(par_in, 16)
                x1_group(2)
                sp.wait_ge(mk, N_MK)
                for b in range(BATCH):
                    sp.dma_start(win[:, b, :, b * DIM:(b + 1) * DIM],
                                 win_t.rearrange("(k p) d -> p k d", p=P)).then_inc(win_in, 16)
                x1_group(1)
                x1_group(3)
                sp.dma_start(f_a, f1_a.rearrange("(k p) n -> p k n", p=P)).then_inc(f_in, 16)
                sp.dma_start(f_b, f1_b_t.rearrange("(k p) n -> p k n", p=P)).then_inc(f_in, 16)
                sp.dma_start(f_w[:], f1_mix).then_inc(f_in, 16)
                sp.dma_start(f_wt, f1_w_t.rearrange("(k p) n -> p k n", p=P)).then_inc(f_in, 16)
                sp.dma_start(f_bias[:], f1_bias_cols).then_inc(last_in, 16)
                sp.dma_start(bout_c[:], bout_cols).then_inc(last_in, 16)
                both(wout, wout_t, last_in)
                with sp.Fori(0, DEPTH) as l:
                    sp.wait_ge(ff_2, 2 * l)
                    for b in range(BATCH):
                        sp.dma_start(w1[b * DIM:(b + 1) * DIM, :].rearrange("p (o n) -> p o n", o=1),
                                     w1_t[bass.ds(l, 1), :, :].rearrange("o p n -> p o n")).then_inc(lay_in, 16)
                        sp.dma_start(w2[:, b, :, b * DIM:(b + 1) * DIM],
                                     w2_t[bass.ds(l, 1), :, :].rearrange("o (m p) d -> p (o m) d", p=P)
                                     ).then_inc(lay_in, 16)
                for t in range(TILES):
                    sp.wait_ge(o_ready, t + 1)
                    sp.dma_start(out[t * P:(t + 1) * P, :], x1[:, t, :]).then_inc(o_out, 16)
                sp.wait_ge(o_out, 16 * TILES)

            @block_b.gpsimd
            def _(pool):
                made = [0]

                def make(ins):
                    made[0] += 1
                    ins.then_inc(mk, 1)
                    pool.wait_ge(mk, made[0])

                make(pool.memset(win[:], 0.0))
                make(pool.memset(w2[:], 0.0))
                make(pool.memset(expo2[:], -0.5))
                make(pool.memset(ident2[:], 0.0))
                make(pool.affine_select(out=ident2[:], in_=ident2[:], compare_op=ALU.not_equal, fill=1.0,
                                        base=0, pattern=[[-1, P]], channel_multiplier=1))
                make(pool.memset(center[:], 0.0))
                make(pool.memset(means[:], 0.0))
                for b in range(BATCH):
                    half = slice(b * DIM, (b + 1) * DIM)
                    make(pool.memset(center[half, half], -1.0 / DIM))
                    make(pool.memset(means[half, b:b + 1], 1.0 / DIM))
                make(pool.tensor_tensor(center[:], center[:], ident2[:], ALU.add))
                assert made[0] == N_MK

                n = [0]

                def step(ins):
                    n[0] += 1
                    ins.then_inc(tb, 1)
                    pool.wait_ge(tb, n[0])

                def tt(o, a, b, op):
                    step(pool.tensor_tensor(o, a, b, op))

                pool.wait_ge(par_in, 16 * 5)
                pv = par[:].rearrange("p (l j) -> p l j", j=NPAR)
                re, im, lr, li = (pv[:, :, j] for j in (C_PR, C_PI, C_LR, C_LI))
                t0, t1, t2, t3 = (e_t[:, j, :] for j in range(4))
                tt(t0, re, re, ALU.mult)
                tt(t1, im, im, ALU.mult)
                tt(t0, t0, t1, ALU.add)
                step(pool.tensor_scalar(t1, t0, 1.0e-37, None, ALU.is_lt))
                step(pool.tensor_scalar(t0, t0, 1.0e-37, None, ALU.max))
                step(pool.memset(rad[:], 0.5))
                tt(rad[:], t0, rad[:], ALU.pow)
                tt(t2, t0, expo2[:, 0:DEPTH], ALU.pow)
                tt(e_re[:], re, t2, ALU.mult)
                tt(e_im[:], im, t2, ALU.mult)
                tt(e_re[:], e_re[:], t1, ALU.add)
                tt(t0, lr, e_re[:], ALU.mult)
                tt(t1, li, e_im[:], ALU.mult)
                tt(u0[:, 0, :], t0, t1, ALU.subtract)
                tt(t0, lr, e_im[:], ALU.mult)
                tt(t1, li, e_re[:], ALU.mult)
                tt(t0, t0, t1, ALU.add)
                step(pool.tensor_scalar(u0[:, 1, :], t0, -1.0, None, ALU.mult))

                for base in (0, 2):
                    sr, si = small[:, base, :, :], small[:, base + 1, :, :]
                    step(pool.memset(sr[:, :, 0:1], 1.0))
                    step(pool.memset(si[:, :, 0:1], 0.0))
                    w = 1
                    while w < COARSE:
                        br = e_re[:].rearrange("p (l o) -> p l o", o=1).to_broadcast([P, DEPTH, w])
                        bi = e_im[:].rearrange("p (l o) -> p l o", o=1).to_broadcast([P, DEPTH, w])
                        q = [tmp[:, j, :, 0:w] for j in range(4)]
                        tt(q[0], sr[:, :, 0:w], br, ALU.mult)
                        tt(q[1], si[:, :, 0:w], bi, ALU.mult)
                        tt(q[2], sr[:, :, 0:w], bi, ALU.mult)
                        tt(q[3], si[:, :, 0:w], br, ALU.mult)
                        tt(sr[:, :, w:2 * w], q[0], q[1], ALU.subtract)
                        tt(si[:, :, w:2 * w], q[2], q[3], ALU.add)
                        tt(t0, e_re[:], e_re[:], ALU.mult)
                        tt(t1, e_im[:], e_im[:], ALU.mult)
                        tt(t2, e_re[:], e_im[:], ALU.mult)
                        tt(e_re[:], t0, t1, ALU.subtract)
                        tt(e_im[:], t2, t2, ALU.add)
                        tt(t0, t0, t1, ALU.add)
                        step(pool.tensor_scalar(t0, t0, -1.0, 2.0, ALU.mult, ALU.add))
                        tt(e_re[:], e_re[:], t0, ALU.mult)
                        tt(e_im[:], e_im[:], t0, ALU.mult)
                        w *= 2

                def tables(l, first):
                    done = [first]

                    def big(o, a, b, op):
                        done[0] = done[0] + 1
                        settled(pool, pool_passed)
                        pool.tensor_tensor(o, a, b, op).then_inc(tb, 1)
                        pool.wait_ge(tb, done[0])

                    def part(j, fine):
                        s = small[:, j, bass.ds(l, 1), :]
                        s = s.rearrange("p o n -> p o n" if fine else "p o n -> p n o")
                        return s.to_broadcast([P, COARSE, COARSE])

                    fr, fi, cr, ci = part(0, True), part(1, True), part(2, False), part(3, False)
                    grid = "p o (a b) -> p (o a) b"
                    co = rot_c[:, bass.ds(l, 1), :].rearrange(grid, b=COARSE)
                    si = rot_s[:, bass.ds(l, 1), :].rearrange(grid, b=COARSE)
                    t = tbig[:].rearrange("p (a b) -> p a b", b=COARSE)
                    big(t, ci, fi, ALU.mult)
                    big(co, cr, fr, ALU.mult)
                    big(co, co, t, ALU.subtract)
                    big(t, ci, fr, ALU.mult)
                    big(si, cr, fi, ALU.mult)
                    big(si, si, t, ALU.add)

                def roots(q):
                    for c in range(HALVES):
                        pool.wait_ge(ln_v, 2 * q + c + 1)
                        pool.tensor_tensor(lnr[:, c, :], lnv[:, c, :], expo2[:, 0:8], ALU.pow).then_inc(ln_r, 1)

                def conv(l):
                    sin = [rot_s[:, bass.ds(l, 1), cs(c)] for c in range(HALVES)]
                    for c in range(HALVES):
                        pool.wait_ge(ln_o, 4 * l + c + 1)
                        settled(pool, pool_passed)
                        pool.tensor_tensor(w_im[:, cs(c)].rearrange("p (o n) -> p o n", o=1),
                                           y[:, cs(c)].rearrange("p (o n) -> p o n", o=1), sin[c],
                                           ALU.mult).then_inc(cv_wi, 1)
                    for c in range(HALVES):
                        pool.wait_ge(cv_ui, 2 * l + c + 1)
                        settled(pool, pool_passed)
                        pool.tensor_tensor(w_im[:, cs(c)].rearrange("p (o n) -> p o n", o=1),
                                           u_im[:, cs(c)].rearrange("p (o n) -> p o n", o=1), sin[c],
                                           ALU.mult).then_inc(cv_b, 1)

                assert n[0] == N_SMALL
                tables(0, N_SMALL)
                with pool.Fori(0, DEPTH - 1) as l:
                    roots(2 * l)
                    conv(l)
                    roots(2 * l + 1)
                    tables(l + 1, 6 * l + 6 + N_SMALL)
                roots(2 * DEPTH - 2)
                conv(DEPTH - 1)
                roots(2 * DEPTH - 1)
                roots(2 * DEPTH)

            @block_b.scalar
            def _(act):
                act.wait_ge(tb, N_RAD)
                act.activation(rho[:], rad[:], ACT.Tanh).then_inc(rho_s, 1)
                for i in range(0, TILES, 2):
                    t = 4 * ORDER[i // 4] + i % 4
                    act.wait_ge(xt_ps, i + 1)
                    act.activation(xt[:, :, t * P:(t + 1) * P],
                                   bankx[0].rearrange("p (k n) -> p k n", k=KH), ACT.Copy).then_inc(xt_a, 1)

                def ln_squares(q):
                    for c in range(HALVES):
                        act.wait_ge(ln_xc, 2 * q + c + 1)
                        act.activation(sq[:, cs(c)], xc[:, cs(c)], ACT.Square).then_inc(ln_sq, 1)

                def ln_out(q, dst, func, w, b):
                    for c in range(HALVES):
                        act.wait_ge(ln_y, 2 * q + c + 1)
                        settled(act, act_passed)
                        act.activation(dst[:, cs(c)], xc[:, cs(c)], func, scale=w, bias=b).then_inc(ln_o, 1)

                def gates(l, ks):
                    for k in ks:
                        act.wait_ge(full, use(l, k) + 1)
                        settled(act, act_passed)
                        act.activation(g2[:, k, bass.ds(NB * l, NB)], bankx[k % 2], ACT.Silu,
                                       bias=f_bias[:, k:k + 1]).then_inc(free, 1)

                act.wait_ge(par_in, 16 * 5)
                act.wait_ge(last_in, 64)
                with act.Fori(0, DEPTH) as l:
                    ln_squares(2 * l)
                    ln_out(2 * l, y, ACT.Silu, pcol(l, C_L1W), pcol(l, C_L1B))
                    gates(l, (0, 1, 2))
                    ln_squares(2 * l + 1)
                    gates(l, (3,))
                    ln_out(2 * l + 1, y, ACT.Identity, pcol(l, C_L2W), pcol(l, C_L2B))
                    for c in range(HALVES):
                        for u in range(4):
                            act.wait_ge(full, use(l, 4 + 4 * c + u) + 1)
                            if c == 1 and u == 0:
                                act.wait_ge(ff_2, 2 * l + 1)
                            settled(act, act_passed)
                            act.activation(hs[:, u, :], bankx[u % 2], ACT.Silu,
                                           bias=b1_c[:, bass.ds(2 * l + u % 2, 1)]).then_inc(free, 1)
                q = 2 * DEPTH
                ln_squares(q)
                ln_out(q, y, ACT.Identity, par_last[:, 0:1], par_last[:, 1:2])

            @block_b.vector
            def _(dve):
                for i in range(4):
                    g = ORDER[i]
                    dve.wait_ge(x1_in[g], 16)
                    for j in range(4):
                        dve.bn_stats(stats2[:, 4 * g + j, :], x1[:, 4 * g + j, :]).then_inc(st2, 1)
                    for j in range(4):
                        dve.wait_ge(st2, 4 * i + j + 1)
                        dve.bn_aggr(mv2[:, 4 * g + j, :], stats2[:, 4 * g + j, :]).then_inc(mv2_s, 1)
                    v, r = ve2[:, 4 * g:4 * g + 4], rs2[:, 4 * g:4 * g + 4]
                    dve.wait_ge(mv2_s, 4 * i + 4)
                    done = [ROOT * i]

                    def step(ins):
                        done[0] += 1
                        ins.then_inc(rs2_s, 1)
                        dve.wait_ge(rs2_s, done[0])

                    step(dve.tensor_scalar(v, mv2[:, 4 * g:4 * g + 4, 1], EPS, None, ALU.add))
                    step(dve.tensor_scalar(r.bitcast(I32), v.bitcast(I32), -0.5, float(0x5F3759DF),
                                           ALU.mult, ALU.add))
                    s = e_s[:]
                    for _ in range(4):
                        step(dve.tensor_tensor(s, r, r, ALU.mult))
                        step(dve.tensor_tensor(s, s, v, ALU.mult))
                        step(dve.tensor_scalar(s, s, -0.5, 1.5, ALU.mult, ALU.add))
                        step(dve.tensor_tensor(r, r, s, ALU.mult))
                    for j in range(4):
                        t = 4 * g + j
                        if i >= 2:
                            dve.wait_ge(xt_ps, 4 * (i - 2) + j + 1)
                        dve.tensor_scalar(xn[:, 4 * (i % 2) + j, :], x1[:, t, :], mv2[:, t, 0:1], rs2[:, t:t + 1],
                                          ALU.subtract, ALU.mult).then_inc(xn_s, 1)
                    for j in (1, 3):
                        t = 4 * g + j
                        dve.wait_ge(xt_ps, 4 * i + j + 1)
                        dve.tensor_copy(xt[:, :, t * P:(t + 1) * P],
                                        bankx[1].rearrange("p (k n) -> p k n", k=KH)).then_inc(xt_v, 1)
                    if i % 2:
                        c = i // 2
                        dve.wait_ge(h_ps, c + 1)
                        if i == 1:
                            dve.wait_ge(par_in, 16 * 5)
                        dve.tensor_scalar(h[:, cs(c)], bank1[c], par_last[:, 2:3], None,
                                          ALU.add).then_inc(h_ready, 1)

                dve.wait_ge(f_in, 16 * 4)
                dve.tensor_tensor(f_w[:, 0, :], f_w[:, 0, :], f_w[:, 1, :], ALU.mult).then_inc(fold_w, 1)
                dve.wait_ge(fold_w, 1)
                for k in range(ER // P):
                    dve.tensor_scalar(f_b[:, k, :], f_b[:, k, :], f_w[:, 0, k:k + 1], None,
                                      ALU.mult).then_inc(fold_b, 1)
                for k in range(KH):
                    dve.wait_ge(full, k + 1)
                    dve.tensor_tensor(weff[:, k, :], bankx[k % 2], f_wt[:, k, :], ALU.add).then_inc(free, 1)

                def ln(q):
                    for c in range(HALVES):
                        dve.wait_ge(ln_cent, 2 * q + c + 1)
                        dve.tensor_copy(xc[:, cs(c)], bank1[c]).then_inc(ln_xc, 1)
                    for c in range(HALVES):
                        dve.wait_ge(ln_var, 2 * q + c + 1)
                        dve.tensor_scalar(lnv[:, c, :], bankv[c][:, 0:8], EPS, None, ALU.add).then_inc(ln_v, 1)
                    for c in range(HALVES):
                        dve.wait_ge(ln_bc, 2 * q + c + 1)
                        dve.wait_ge(ln_xc, 2 * q + c + 1)
                        dve.tensor_tensor(xc[:, cs(c)], xc[:, cs(c)], bank2[c], ALU.mult).then_inc(ln_y, 1)

                def conv(l):
                    def one(ap):
                        return ap.rearrange("p (o n) -> p o n", o=1)

                    cos = [rot_c[:, bass.ds(l, 1), cs(c)] for c in range(HALVES)]
                    decay = rho[:, bass.ds(l, 1)].to_broadcast([P, NB])
                    dve.wait_ge(tb, N_SMALL + 6 * l + 6)
                    dve.wait_ge(rho_s, 1)
                    for c in range(HALVES):
                        dve.wait_ge(ln_o, 4 * l + c + 1)
                        dve.tensor_tensor(one(w_re[:, cs(c)]), one(y[:, cs(c)]), cos[c],
                                          ALU.mult).then_inc(cv_wr, 1)
                    for name, w, u, done in (("re", w_re, u_re, cv_ur), ("im", w_im, u_im, cv_ui)):
                        for c in range(HALVES):
                            dve.wait_ge(cv_wr if name == "re" else cv_wi, 2 * l + c + 1)
                            if c == 0:
                                first = u0[:, 0 if name == "re" else 1, bass.ds(l, 1)]
                            else:
                                dve.wait_ge(done, 2 * l + 1)
                                first = u[:, NB - 1:NB]
                            dve.tensor_tensor_scan(u[:, cs(c)], decay, w[:, cs(c)], first,
                                                   ALU.mult, ALU.add).then_inc(done, 1)
                    for c in range(HALVES):
                        dve.wait_ge(cv_ur, 2 * l + c + 1)
                        dve.tensor_tensor(one(w_re[:, cs(c)]), one(u_re[:, cs(c)]), cos[c],
                                          ALU.mult).then_inc(cv_a, 1)
                    for c in range(HALVES):
                        dve.wait_ge(cv_a, 2 * l + c + 1)
                        dve.wait_ge(cv_b, 2 * l + c + 1)
                        dve.tensor_tensor(w_re[:, cs(c)], w_re[:, cs(c)], w_im[:, cs(c)], ALU.add).then_inc(cv_ab, 1)
                        dve.wait_ge(cv_ab, 2 * l + c + 1)
                        dve.scalar_tensor_tensor(out=h[:, cs(c)], in0=w_re[:, cs(c)], scalar=pcol(l, C_SCL),
                                                 in1=h[:, cs(c)], op0=ALU.mult, op1=ALU.add).then_inc(h_ready, 1)

                with dve.Fori(0, DEPTH) as l:
                    ln(2 * l)
                    conv(l)
                    ln(2 * l + 1)
                    for c in range(HALVES):
                        dve.wait_ge(ff_2, 2 * l + c + 1)
                        dve.scalar_tensor_tensor(out=h[:, cs(c)], in0=bank1[c], scalar=pcol(l, C_B2),
                                                 in1=h[:, cs(c)], op0=ALU.add, op1=ALU.add).then_inc(h_ready, 1)
                ln(2 * DEPTH)

                def outer(g):
                    b, c = g // HALVES, g % HALVES
                    for k in range(VOCAB // P):
                        dve.wait_ge(full, use(DEPTH, 4 * g + k) + 1)
                        if g:
                            dve.wait_ge(o_ps, 4 * g)
                        dve.scalar_tensor_tensor(out=res[:, k, :], in0=bankx[k % 2], scalar=bout_c[:, k:k + 1],
                                                 in1=g2[:, k, g * NB:(g + 1) * NB], op0=ALU.add,
                                                 op1=ALU.mult).then_inc(free, 1)

                def inner(g):
                    for j in range(4):
                        t = 4 * g + j
                        dve.wait_ge(o_ps, t + 1)
                        dve.tensor_tensor(x1[:, t, :], obank[j], x1[:, t, :], ALU.add).then_inc(o_ready, 1)

                for g in range(4):
                    outer(g)
                    inner(g)

            @block_b.tensor
            def _(pe):
                pe.wait_ge(mk, N_MK)
                for i in range(TILES):
                    pe.wait_ge(xn_s, i + 1)
                    if i >= 2:
                        pe.wait_ge(xt_v if i % 2 else xt_a, i // 2)
                    for k in range(KH):
                        last = pe.transpose(bankx[i % 2][:, k * P:(k + 1) * P], xn[:, i % 8, k * P:(k + 1) * P],
                                            ident2[:])
                    last.then_inc(xt_ps, 1)
                    if i % 8 == 7:
                        c = i // 8
                        pe.wait_ge(win_in, 32)
                        pe.wait_ge(xt_a, 4 * c + 4)
                        pe.wait_ge(xt_v, 4 * c + 4)
                        for b in range(BATCH):
                            for k in range(KH):
                                last = pe.matmul(bank1[c], win[:, b, k, :],
                                                 xt[:, k, b * SEQ + c * NB:b * SEQ + (c + 1) * NB],
                                                 start=(b == 0 and k == 0), stop=(b == 1 and k == KH - 1))
                        last.then_inc(h_ps, 1)
                pe.wait_ge(fold_b, ER // P)
                for k in range(KH):
                    if k >= 2:
                        pe.wait_ge(free, k - 1)
                    for e in range(ER // P):
                        last = pe.matmul(bankx[k % 2], f_a[:, e, k * P:(k + 1) * P], f_b[:, e, :],
                                         start=(e == 0), stop=(e == ER // P - 1))
                    last.then_inc(full, 1)

                def ln_center(q):
                    for c in range(HALVES):
                        pe.wait_ge(h_ready, 2 * q + c + 1)
                        pe.matmul(bank1[c], center[:], h[:, cs(c)], start=True, stop=True).then_inc(ln_cent, 1)

                def ln_variance(q):
                    for c in range(HALVES):
                        pe.wait_ge(ln_sq, 2 * q + c + 1)
                        for j in range(4):
                            last = pe.matmul(bankv[c][:, 2 * j:2 * j + 2],
                                             sq[:, c * NB + j * P:c * NB + (j + 1) * P], means[:],
                                             start=True, stop=True)
                        last.then_inc(ln_var, 1)

                def ln_spread(q):
                    for c in range(HALVES):
                        pe.wait_ge(ln_r, 2 * q + c + 1)
                        for j in range(4):
                            for b in range(BATCH):
                                last = pe.matmul(bank2[c][b * DIM:(b + 1) * DIM, j * P:(j + 1) * P],
                                                 lnr[:, c, 2 * j + b:2 * j + b + 1].to_broadcast([P, DIM]),
                                                 ident2[:], start=True, stop=True)
                        last.then_inc(ln_bc, 1)

                def gate_unit(l, k):
                    pe.wait_ge(free, use(l, k) - 1)
                    for n in range(KH):
                        last = pe.matmul(bankx[k % 2], weff[:, n, k * P:(k + 1) * P],
                                         xt[:, n, bass.ds(NB * l, NB)], start=(n == 0), stop=(n == KH - 1))
                    last.then_inc(full, 1)

                def up_unit(l, c, u):
                    b, m = u // 2, u % 2
                    pe.wait_ge(free, use(l, 4 + 4 * c + u) - 1)
                    half = slice(b * DIM, (b + 1) * DIM)
                    pe.matmul(bankx[u % 2], w1[half, m * P:(m + 1) * P], y[half, cs(c)],
                              start=True, stop=True).then_inc(full, 1)

                def down_unit(l, c, u):
                    b, m = u // 2, u % 2
                    pe.wait_ge(free, use(l, 4 + 4 * c + u) + 1)
                    last = pe.matmul(bank1[c], w2[:, b, m, :], hs[:, u, :], start=(u == 0), stop=(u == 3))
                    if u == 3:
                        last.then_inc(ff_2, 1)

                with pe.Fori(0, DEPTH) as l:
                    ln_center(2 * l)
                    ln_variance(2 * l)
                    ln_spread(2 * l)
                    for k in (0, 1, 2):
                        gate_unit(l, k)
                    ln_center(2 * l + 1)
                    gate_unit(l, 3)
                    ln_variance(2 * l + 1)
                    ln_spread(2 * l + 1)
                    pe.wait_ge(lay_in, 64 * l + 64)
                    for c in range(HALVES):
                        pe.wait_ge(ln_o, 4 * l + 2 + c + 1)
                        up_unit(l, c, 0)
                        up_unit(l, c, 1)
                        down_unit(l, c, 0)
                        up_unit(l, c, 2)
                        down_unit(l, c, 1)
                        up_unit(l, c, 3)
                        down_unit(l, c, 2)
                        down_unit(l, c, 3)
                q = 2 * DEPTH
                ln_center(q)
                ln_variance(q)
                ln_spread(q)

                def out_unit(g, k):
                    b, c = g // HALVES, g % HALVES
                    if k == 0:
                        pe.wait_ge(ln_o, 2 * q + c + 1)
                    pe.wait_ge(free, use(DEPTH, 4 * g + k) - 1)
                    half = slice(b * DIM, (b + 1) * DIM)
                    pe.matmul(bankx[k % 2], wout[half, k * P:(k + 1) * P], y[half, cs(c)],
                              start=True, stop=True).then_inc(full, 1)

                def out_tile(g, j):
                    t = 4 * g + j
                    if j == 0:
                        pe.wait_ge(free, use(DEPTH, 4 * g + 3) + 1)
                    if t >= 4:
                        pe.wait_ge(o_ready, t - 3)
                    for k in range(VOCAB // P):
                        last = pe.transpose(obank[j][:, k * P:(k + 1) * P], res[:, k, j * P:(j + 1) * P], ident2[:])
                    last.then_inc(o_ps, 1)

                for g in range(4):
                    for k in range(4):
                        out_unit(g, k)
                    for j in range(4):
                        out_tile(g, j)


def _program(nc, args, out):
    mixture_kernel(nc, *args, out)


def kernel(**inputs):
    import numpy as np
    import concourse.bacc as bacc
    from concourse.bass_utils import run_bass_kernel_spmd

    a = {k: np.asarray(v) for k, v in inputs.items()}

    def t(name):
        return np.ascontiguousarray(a[name].T)

    def l1(name):
        return a["L1_attn_" + name]

    per_layer = ["ln1_w", "ln1_b", "phz_re", "phz_im", "lc_re", "lc_im", "sc_lin", "ln2_w", "ln2_b", "b2"]
    data = {
        "x": a["L0_attn_x"].reshape(TOKENS, HID),
        "wg_t": t("L0_attn_w_gate"), "wu_t": t("L0_attn_w_up"), "wd_t": t("L0_attn_w_down"),
        "tern_w": a["L0_ffn_weight"], "ffn_bias": a["L0_ffn_bias"],
        "win_t": t("L1_attn_Win"),
        "cols": np.stack([l1(n) for n in per_layer], axis=1).transpose(2, 0, 1).reshape(DIM, DEPTH * NPAR),
        "last_cols": np.stack([l1("lnl_w"), l1("lnl_b"), l1("bin")], axis=1),
        "b1_cols": l1("b1").reshape(DEPTH * DFF // P, P).T,
        "w1_t": l1("W1").transpose(0, 2, 1), "w2_t": l1("W2").transpose(0, 2, 1),
        "wout_t": t("L1_attn_Wout"), "bout_cols": l1("bout").reshape(VOCAB // P, P).T,
        "f1_w_t": t("L1_ffn_W"), "f1_bias_cols": a["L1_ffn_bias"].reshape(HID // P, P).T,
        "f1_a": a["L1_ffn_A"].reshape(ER, HID),
        "f1_b_t": a["L1_ffn_Bf"].transpose(0, 2, 1).reshape(ER, HID),
        "f1_mix": np.stack([np.repeat(a["L1_ffn_" + n], RANK).reshape(ER // P, P) for n in ("coeffs", "scales")])
        .transpose(2, 0, 1),
    }
    nc = bacc.Bacc("TRN2", target_bir_lowering=False, num_devices=1)
    arrays, args = {}, []
    for name, value in data.items():
        value = np.ascontiguousarray(value)
        arrays["in_" + name] = value
        args.append(nc.dram_tensor("in_" + name, value.shape, mybir.dt.from_np(value.dtype),
                                   kind="ExternalInput").ap())
    out = nc.dram_tensor("out_0", (TOKENS, HID), F32, kind="ExternalOutput").ap()
    _program(nc, args, out)
    r = run_bass_kernel_spmd(nc, [arrays], core_ids=[0])
    return r.results[0]["out_0"].reshape(2, TOKENS // 2, HID)
```

```python
from contextlib import ExitStack

import concourse.bass as bass
from concourse import mybir

F32 = mybir.dt.float32
F32R = mybir.dt.float32r
I32 = mybir.dt.int32
I8 = mybir.dt.int8
ALU = mybir.AluOpType
ACT = mybir.ActivationFunctionType
AX_X = mybir.AxisListType.X
RADD = bass.bass_isa.ReduceOp.add

P = 128
EPS = 1e-5

TOKENS, HID, INNER = 2048, 512, 1376
KH = HID // P
TILES = TOKENS // P
PAIRS = TILES // 2
DROP = INNER // 2
NCOL = [(0, 512), (512, 1024), (1024, INNER)]
CHUNKS = -(-INNER // P)
PADDED = CHUNKS * P
GROUPS = [(0, 4), (4, 8), (8, CHUNKS)]
NG = len(GROUPS)
TERNARY = 0.7

STEPS = 8
LOW, HIGH = 0.6, 0.9
CANDS = STEPS + 1
ACT_COUNTS = STEPS + 2
PICKS = 12
N_CONST = 5 + STEPS + 2 + 8

BATCH, SEQ, DIM, DFF, DEPTH, VOCAB = 2, 1024, 64, 256, 4, 512
NB = 512
HALVES = SEQ // NB
COARSE = 32
EXPERTS, RANK = 16, 16
ER = EXPERTS * RANK
NPAR = 10
ROOT = 18
N_MK = 11
N_RAD = 9
N_START = N_RAD + 10
N_POWERS = 2 + 5 * 15
N_SMALL = N_START + 2 * N_POWERS
(C_L1W, C_L1B, C_PR, C_PI, C_LR, C_LI, C_SCL, C_L2W, C_L2B, C_B2) = range(NPAR)


def settled(engine, passed):
    engine.sem_inc(passed, 1)


def mixture_kernel(nc, x, wg_t, wu_t, wd_t, tern_w, ffn_bias, win_t, cols, last_cols, b1_cols,
                   w1_t, w2_t, wout_t, bout_cols, f1_w_t, f1_bias_cols, f1_a, f1_b_t,
                   f1_mix, out):
    x1_dram = nc.dram_tensor("x1_scratch", (TOKENS, HID), F32, kind="Internal").ap()
    pair_view = "(n t q) h -> q n t h"
    x_pairs = x.rearrange(pair_view, t=2, q=P)
    x1_pairs = x1_dram.rearrange(pair_view, t=2, q=P)

    with ExitStack() as ctx:
        def psum(name, shape):
            return ctx.enter_context(nc.psum_tensor(name, shape, F32))

        def sem(name):
            return ctx.enter_context(nc.semaphore(name))

        pool_passed, act_passed, dve_passed = sem("pool_passed"), sem("act_passed"), sem("dve_passed")

        ps_a = psum("ps_a", [P, 3, NB])
        ps_b = psum("ps_b", [P, 3, NB])
        ps_t = psum("ps_t", [P, 2, NB])

        N_W = KH * INNER
        with ExitStack() as wctx:
            wg_hi, wg_lo, wu_hi, wu_lo = (
                wctx.enter_context(nc.sbuf_tensor(name, [P, KH, INNER], F32R))
                for name in ("wg_hi", "wg_lo", "wu_hi", "wu_lo"))
        arena = ctx.enter_context(nc.sbuf_tensor("arena", [P, 4 * N_W], F32))
        cursor = [0]

        def over_weights(*shape):
            n = 1
            for d in shape:
                n *= d
            ap = arena[:, cursor[0]:cursor[0] + n]
            cursor[0] += n
            assert cursor[0] <= 4 * N_W
            if len(shape) == 1:
                return ap
            return ap.rearrange("p (a b) -> p a b", b=shape[1]) if len(shape) == 2 else \
                ap.rearrange("p (a b c) -> p a b c", b=shape[1], c=shape[2])

        x1 = over_weights(TILES, HID)
        fold = over_weights(8, HID)
        f_a, f_b, f_wt = fold[:, 0:2, :], fold[:, 2:4, :], fold[:, 4:8, :]
        hs, res = fold[:, 0:4, :], fold[:, 4:8, :]
        work = over_weights(4 * SEQ)
        xn = work.rearrange("p (t n) -> p t n", n=HID)
        w_re, w_im, u_re, u_im = (work[:, j * SEQ:(j + 1) * SEQ] for j in range(4))
        weff = over_weights(KH, HID)
        win = over_weights(BATCH, KH, P)
        f_w = over_weights(2, ER // P)
        stats2 = over_weights(TILES, 6)
        mv2 = over_weights(TILES, 2)
        ve2 = over_weights(TILES)
        rs2 = over_weights(TILES)
        e_s = over_weights(TILES)
        par = over_weights(DEPTH * NPAR)
        par_last = over_weights(3)
        small = over_weights(4, DEPTH * COARSE).rearrange("p j (l n) -> p j l n", n=COARSE)
        tmp = over_weights(4, DEPTH * COARSE // 2).rearrange("p j (l n) -> p j l n", n=COARSE // 2)
        e_c = over_weights(2, DEPTH)
        e_t = over_weights(4, DEPTH)
        rad = over_weights(DEPTH)
        u0 = over_weights(2, DEPTH)

        x1_in = [sem(f"x1_in{i}") for i in range(4)]
        win_in = sem("win_in")
        win_zero = sem("win_zero")
        f_in = sem("f_in")
        fold_w = sem("fold_w")
        fold_b = sem("fold_b")
        full = sem("full")
        free = sem("free")
        st2 = sem("st2")
        mv2_s = sem("mv2_s")
        rs2_s = sem("rs2_s")
        xn_s = sem("xn_s")
        par_in = sem("par_in")
        tb = sem("tb")
        ORDER = [0, 2, 1, 3]
        bankf = [ps_a[:, 2, :], ps_b[:, 2, :]]

        def load_x1_group(sp, g):
            sp.dma_start(x1[:, 4 * g:4 * g + 4, :],
                         x1_dram[4 * g * P:4 * (g + 1) * P, :].rearrange("(t q) h -> q t h", q=P)
                         ).then_inc(x1_in[g], 16)

        def norm2_stats(dve, i):
            dve.wait_ge(x1_in[ORDER[i]], 16)
            for j in range(4):
                dve.bn_stats(stats2[:, 4 * i + j, :], x1[:, 4 * ORDER[i] + j, :]).then_inc(st2, 1)
            for j in range(4):
                dve.wait_ge(st2, 4 * i + j + 1)
                dve.bn_aggr(mv2[:, 4 * i + j, :], stats2[:, 4 * i + j, :]).then_inc(mv2_s, 1)

        def norm2_root(dve, n, i0, i1):
            w = slice(4 * i0, 4 * i1)
            v, r, s = ve2[:, w], rs2[:, w], e_s[:, w]
            done = [ROOT * n]

            def step(ins):
                done[0] += 1
                ins.then_inc(rs2_s, 1)
                dve.wait_ge(rs2_s, done[0])

            dve.wait_ge(mv2_s, 4 * i1)
            step(dve.tensor_scalar(v, mv2[:, w, 1], EPS, None, ALU.add))
            step(dve.tensor_scalar(r.bitcast(I32), v.bitcast(I32), -0.5, float(0x5F3759DF),
                                   ALU.mult, ALU.add))
            for _ in range(4):
                step(dve.tensor_tensor(s, r, r, ALU.mult))
                step(dve.tensor_tensor(s, s, v, ALU.mult))
                step(dve.tensor_scalar(s, s, -0.5, 1.5, ALU.mult, ALU.add))
                step(dve.tensor_tensor(r, r, s, ALU.mult))

        def norm2_apply(dve, i):
            for j in range(4):
                m = 4 * i + j
                dve.tensor_scalar(xn[:, m % 8, :], x1[:, 4 * ORDER[i] + j, :], mv2[:, m, 0:1], rs2[:, m:m + 1],
                                  ALU.subtract, ALU.mult).then_inc(xn_s, 1)

        def tables_start(pool):
            pool.wait_ge(par_in, 16 * 4)
            pv = par.rearrange("p (l j) -> p l j", j=NPAR)
            re, im, lr, li = (pv[:, :, j] for j in (C_PR, C_PI, C_LR, C_LI))
            t0, t1, t2, t3 = (e_t[:, j, :] for j in range(4))
            e_re, e_im = e_c[:, 0, :], e_c[:, 1, :]
            n = [0]

            def run(*instructions):
                n[0] += len(instructions)
                for ins in instructions:
                    ins.then_inc(tb, 1)
                pool.wait_ge(tb, n[0])

            def tt(o, a, b, op):
                return pool.tensor_tensor(o, a, b, op)

            run(tt(t0, re, re, ALU.mult), tt(t1, im, im, ALU.mult), pool.memset(rad, 0.5),
                pool.memset(t3, -0.5))
            run(tt(t0, t0, t1, ALU.add))
            run(pool.tensor_scalar(t1, t0, 1.0e-37, None, ALU.is_lt))
            run(pool.tensor_scalar(t0, t0, 1.0e-37, None, ALU.max))
            run(tt(rad, t0, rad, ALU.pow), tt(t2, t0, t3, ALU.pow))
            assert n[0] == N_RAD
            run(tt(e_re, re, t2, ALU.mult), tt(e_im, im, t2, ALU.mult))
            run(tt(e_re, e_re, t1, ALU.add))
            run(tt(t0, lr, e_re, ALU.mult), tt(t1, li, e_im, ALU.mult),
                tt(t2, lr, e_im, ALU.mult), tt(t3, li, e_re, ALU.mult))
            run(tt(u0[:, 0, :], t0, t1, ALU.subtract), tt(t2, t2, t3, ALU.add))
            run(pool.tensor_scalar(u0[:, 1, :], t2, -1.0, None, ALU.mult))
            assert n[0] == N_START

        def tables_powers(pool, half):
            n = [N_START + half * N_POWERS]

            def run(*instructions):
                n[0] += len(instructions)
                for ins in instructions:
                    ins.then_inc(tb, 1)
                pool.wait_ge(tb, n[0])

            def tt(o, a, b, op):
                return pool.tensor_tensor(o, a, b, op)

            z = small[:, 2 * half:2 * half + 2, :, :]
            t0, t1, t2, t3 = (e_t[:, j, :] for j in range(4))
            e_re, e_im = e_c[:, 0, :], e_c[:, 1, :]
            run(pool.memset(z[:, 0, :, 0:1], 1.0), pool.memset(z[:, 1, :, 0:1], 0.0))
            w = 1
            while w < COARSE:
                br, bi = (e.rearrange("p (l o) -> p l o", o=1).to_broadcast([P, DEPTH, w]) for e in (e_re, e_im))
                q = [tmp[:, j, :, 0:w] for j in range(4)]
                zr, zi = z[:, 0, :, 0:w], z[:, 1, :, 0:w]
                run(tt(q[0], zr, br, ALU.mult), tt(q[1], zi, bi, ALU.mult),
                    tt(q[2], zr, bi, ALU.mult), tt(q[3], zi, br, ALU.mult),
                    tt(t0, e_re, e_re, ALU.mult), tt(t1, e_im, e_im, ALU.mult), tt(t2, e_re, e_im, ALU.mult))
                run(tt(z[:, 0, :, w:2 * w], q[0], q[1], ALU.subtract),
                    tt(z[:, 1, :, w:2 * w], q[2], q[3], ALU.add),
                    tt(e_re, t0, t1, ALU.subtract), tt(e_im, t2, t2, ALU.add), tt(t3, t0, t1, ALU.add))
                run(pool.tensor_scalar(t3, t3, -1.0, 2.0, ALU.mult, ALU.add))
                run(tt(e_re, e_re, t3, ALU.mult), tt(e_im, e_im, t3, ALU.mult))
                w *= 2
            assert n[0] == N_START + (half + 1) * N_POWERS

        with ExitStack() as actx:
            def sb(name, shape, dt=F32):
                return actx.enter_context(nc.sbuf_tensor(name, shape, dt))

            wd_hi = sb("wd_hi", [P, CHUNKS, HID], F32R)
            wd_lo = sb("wd_lo", [P, CHUNKS, HID], F32R)
            q_t = sb("q_t", [P, KH, HID], F32R)
            s_buf = sb("s_buf", [P, 2, INNER])
            k_buf = sb("k_buf", [P, 2, INNER])
            m_buf = sb("m_buf", [P, 2, PADDED])
            zt_hi = sb("zt_hi", [P, PADDED], F32R)
            zt_lo = sb("zt_lo", [P, PADDED], F32R)
            xin = sb("xin", [P, 2, HID])
            xres = sb("xres", [P, 2, HID])
            xt_hi = sb("xt_hi", [P, 2, HID], F32R)
            xt_lo = sb("xt_lo", [P, 2, HID], F32R)
            gate2 = sb("gate2", [P, 2, HID])
            bias_b = sb("bias_b", [P, HID])
            junk_d = sb("junk_d", [P, INNER], I8)
            junk_a = sb("junk_a", [P, INNER], I8)
            ident = sb("ident", [P, P])
            powers = sb("powers", [P, STEPS + 2, 2])
            widths = sb("widths", [P, STEPS + 2, 2])
            iota8 = sb("iota8", [P, 2, 8])
            mag_sum = sb("mag_sum", [P, 2])
            cand = sb("cand", [P, 2])
            cand_low = sb("cand_low", [P, 2])
            rise = sb("rise", [P, 2])
            below = sb("below", [P, 2])
            at_most = sb("at_most", [P, 2])
            rank = sb("rank", [P, 2])
            top8 = sb("top8", [P, 2, 8])
            pick = sb("pick", [P, 2, 8])
            tau = sb("tau", [P, 2])
            above = sb("above", [P, 2])
            bad = sb("bad", [P, 2])
            bad_all = sb("bad_all", [P, 2])
            bad_int = sb("bad_int", [P, 2], I32)
            bit = sb("bit", [P, 2], I32)
            lo_bits = sb("lo_bits", [P, 2], I32)
            cand_bits = sb("cand_bits", [P, 2], I32)
            set_bits = sb("set_bits", [P, 2], I32)
            stats = sb("stats", [P, 2, 6])
            mv = sb("mv", [P, 2, 2])
            var_eps = sb("var_eps", [P, 2])
            rstd = sb("rstd", [P, 2])
            expo = sb("expo", [P, 2])
            one = sb("one", [P, 1])
            mags, thr, thr_neg = (pick[:].rearrange("p t e -> p (t e)")[:, i * KH:(i + 1) * KH] for i in range(3))

            c_const = sem("c_const")
            x_in = sem("x_in")
            x_res = sem("x_res")
            bias_in = sem("bias_in")
            tern_in = sem("tern_in")
            w_in = [sem(f"w_in{i}") for i in range(4)]
            w_hi = sem("w_hi")
            w_lo = sem("w_lo")
            t_mag = sem("t_mag")
            t_thr = sem("t_thr")
            t_neg = sem("t_neg")
            t_q = sem("t_q")
            t_tr = sem("t_tr")
            t_cp = sem("t_cp")
            ln_st = sem("ln_st")
            ln_mv = sem("ln_mv")
            ln_ve = sem("ln_ve")
            ln_rs = sem("ln_rs")
            xn_ready = sem("xn_ready")
            xt_psum = sem("xt_psum")
            xt_h = sem("xt_h")
            xt_l = sem("xt_l")
            gate_done = sem("gate_done")
            up_done = sem("up_done")
            s_ready = sem("s_ready")
            k_ready = sem("k_ready")
            z_ready = sem("z_ready")
            wid_ready = sem("wid_ready")
            cand_ready = sem("cand_ready")
            candlow_ready = sem("candlow_ready")
            rise_ready = sem("rise_ready")
            cnt_dve = sem("cnt_dve")
            cnt_act = sem("cnt_act")
            small_ready = sem("small_ready")
            top_ready = sem("top_ready")
            picked = sem("picked")
            bad_sum = sem("bad_sum")
            mask_ready = sem("mask_ready")
            zt_psum = sem("zt_psum")
            zt_h = sem("zt_h")
            zt_l = sem("zt_l")
            down_done = sem("down_done")
            down_out = sem("down_out")
            x1_ready = sem("x1_ready")
            x1_out = sem("x1_out")
            q_done = sem("q_done")
            q_biased = sem("q_biased")
            g_ready = sem("g_ready")

            units = []
            for w, hi, lo in ((wg_t, wg_hi, wg_lo), (wu_t, wu_hi, wu_lo)):
                for k in range(KH):
                    units.append((w[k * P:(k + 1) * P, :], P, hi[:, k, :], lo[:, k, :], None))
            N_GU = len(units)
            for c in range(0, CHUNKS - 1, 2):
                units.append((wd_t[c * P:(c + 2) * P, :].rearrange("(c p) n -> p c n", c=2), P,
                              wd_hi[:, c:c + 2, :], wd_lo[:, c:c + 2, :], 2))
            last_rows = INNER - (CHUNKS - 1) * P
            units.append((wd_t[(CHUNKS - 1) * P:INNER, :], last_rows,
                          wd_hi[0:last_rows, CHUNKS - 1, :], wd_lo[0:last_rows, CHUNKS - 1, :], None))

            def slot_of(u):
                return u % 4 if u < N_GU else u % 2

            def slot_ap(u):
                _, rows, hi, _, parts = units[u]
                buf = (m_buf[:, 0, :], m_buf[:, 1, :], k_buf[:, 0, :], k_buf[:, 1, :])[slot_of(u)]
                n = HID * (parts or 1) if u >= N_GU else INNER
                ap = buf[0:rows, 0:n]
                return ap.rearrange("p (c n) -> p c n", c=parts) if parts else ap

            def loads_before(u):
                return sum(slot_of(v) == slot_of(u) for v in range(u + 1))

            block_a = actx.enter_context(nc.Block())

            def col(ap, n):
                return ap.rearrange("p (t o) -> p t o", o=1).to_broadcast([P, 2, n])

            @block_a.sync
            def _(sp):
                def load_x(dst, done, p):
                    sp.dma_start(dst[:].rearrange("q (n t) h -> q n t h", n=1),
                                 x_pairs[:, bass.ds(p, 1), :, :]).then_inc(done, 16)

                load_x(xin, x_in, 0)
                for t in range(2):
                    sp.dma_start(s_buf[:, t, 0:2 * HID].rearrange("p (k n) -> p k n", k=2),
                                 tern_w[2 * P * t:2 * P * (t + 1), :].rearrange("(k p) n -> p k n", p=P)
                                 ).then_inc(tern_in, 16)
                for u in range(len(units)):
                    prev = [v for v in range(u) if slot_of(v) == slot_of(u)]
                    if prev:
                        sp.wait_ge(w_lo, prev[-1] + 1)
                        sp.wait_ge(w_hi, prev[-1] + 1)
                    sp.dma_start(slot_ap(u), units[u][0]).then_inc(w_in[slot_of(u)], 16)
                    if u == 3:
                        sp.dma_start(bias_b[:], ffn_bias.partition_broadcast(P)).then_inc(bias_in, 16)
                sp.wait_ge(xt_psum, 2)
                load_x(xin, x_in, 1)

                def second_layer():
                    sp.wait_ge(up_done, TILES)
                    for b in range(BATCH):
                        for dst, src in ((par, cols), (par_last, last_cols)):
                            sp.dma_start(dst[b * DIM:(b + 1) * DIM, :], src).then_inc(par_in, 16)
                    sp.dma_start(f_w, f1_mix).then_inc(f_in, 16)
                    sp.dma_start(f_b, f1_b_t.rearrange("(k p) n -> p k n", p=P)).then_inc(f_in, 16)
                    sp.dma_start(f_a, f1_a.rearrange("(k p) n -> p k n", p=P)).then_inc(f_in, 16)
                    sp.dma_start(f_wt, f1_w_t.rearrange("(k p) n -> p k n", p=P)).then_inc(f_in, 16)
                    for i in range(3):
                        load_x1_group(sp, ORDER[i])
                    sp.wait_ge(win_zero, 1)
                    for b in range(BATCH):
                        sp.dma_start(win[:, b, :, b * DIM:(b + 1) * DIM],
                                     win_t.rearrange("(k p) d -> p k d", p=P)).then_inc(win_in, 16)

                def pair(p, ahead, last=False):
                    if ahead:
                        sp.wait_ge(xt_psum, 2 * p + 2)
                        load_x(xin, x_in, p + 1)
                    sp.wait_ge(x1_out, 16 * (p - 1))
                    load_x(xres, x_res, p - 1)
                    if last:
                        second_layer()
                    sp.wait_ge(x1_ready, 2 * p)
                    sp.dma_start(x1_pairs[:, bass.ds(p - 1, 1), :, :],
                                 xres[:].rearrange("q (n t) h -> q n t h", n=1)).then_inc(x1_out, 16)

                with sp.Fori(1, PAIRS - 1) as p:
                    pair(p, True)
                pair(PAIRS - 1, False, last=True)
                pair(PAIRS, False)
                sp.wait_ge(x1_out, 16 * PAIRS)

            @block_a.gpsimd
            def _(pool):
                pool.memset(ident[:], 0.0).then_inc(c_const, 1)
                pool.wait_ge(c_const, 1)
                pool.affine_select(out=ident[:], in_=ident[:], compare_op=ALU.not_equal, fill=1.0, base=0,
                                   pattern=[[-1, P]], channel_multiplier=1).then_inc(c_const, 1)
                pool.memset(expo[:], -0.5).then_inc(c_const, 1)
                pool.memset(one[:], 1.0).then_inc(c_const, 1)
                pool.memset(m_buf[:, :, INNER:PADDED], 0.0).then_inc(c_const, 1)
                for j in range(STEPS + 2):
                    pool.memset(powers[:, j, :], (HIGH - LOW) / INNER / 2 ** j).then_inc(c_const, 1)
                for j in range(8):
                    pool.memset(iota8[:, :, j:j + 1], float(j)).then_inc(c_const, 1)
                pool.wait_ge(c_const, N_CONST)

                def root(p):
                    pool.wait_ge(ln_ve, p + 1)
                    pool.tensor_tensor(rstd[:], var_eps[:], expo[:], ALU.pow).then_inc(ln_rs, 1)

                def residual(p):
                    for t in range(2):
                        if t == 0:
                            pool.wait_ge(x_res, 16 * p)
                        pool.wait_ge(down_out, 2 * (p - 1) + t + 1)
                        pool.tensor_tensor(xres[:, t, :], xres[:, t, :], gate2[:, t, :],
                                           ALU.add).then_inc(x1_ready, 1)

                def check_sum(p):
                    pool.wait_ge(picked, PICKS * p + PICKS - 1)
                    settled(pool, pool_passed)
                    pool.partition_all_reduce(bad_all[:], bad[:], P, RADD).then_inc(bad_sum, 1)

                root(0)
                root(1)
                check_sum(0)
                with pool.Fori(1, PAIRS - 1) as p:
                    root(p + 1)
                    residual(p)
                    check_sum(p)
                pool.wait_ge(up_done, TILES)
                pool.memset(win, 0.0).then_inc(win_zero, 1)
                tables_start(pool)
                pool.wait_ge(f_in, 16 * 4)
                pool.tensor_tensor(f_w[:, 0, :], f_w[:, 0, :], f_w[:, 1, :], ALU.mult).then_inc(fold_w, 1)
                pool.wait_ge(fold_w, 1)
                for k in range(ER // P):
                    pool.tensor_scalar(f_b[:, k, :], f_b[:, k, :], f_w[:, 0, k:k + 1], 0.0,
                                       ALU.mult, ALU.add).then_inc(fold_b, 1)
                residual(PAIRS - 1)
                check_sum(PAIRS - 1)
                tables_powers(pool, 0)
                residual(PAIRS)

            @block_a.scalar
            def _(act):
                def split_hi(u):
                    act.wait_ge(w_in[slot_of(u)], 16 * loads_before(u))
                    act.activation(units[u][2], slot_ap(u), ACT.Copy).then_inc(w_hi, 1)

                def xt_high(p, t):
                    act.wait_ge(xt_psum, 2 * p + t + 1)
                    act.activation(xt_hi[:, t, :], ps_t[:, t, :], ACT.Copy).then_inc(xt_h, 1)

                act.wait_ge(tern_in, 32)
                for k in range(KH):
                    if k:
                        act.wait_ge(t_mag, k)
                    act.activation(junk_a[:, 0:HID], s_buf[:, k // 2, (k % 2) * HID:(k % 2 + 1) * HID],
                                   ACT.Abs, accum_out=mags[:, k:k + 1]).then_inc(t_mag, 1)
                for t in range(2):
                    xt_high(0, t)
                for u in range(N_GU):
                    split_hi(u)

                def silu_keys(p, t, wait_free):
                    act.wait_ge(gate_done, 2 * p + t + 1)
                    if not wait_free:
                        act.wait_ge(w_lo, N_GU)
                    if wait_free:
                        act.wait_ge(mask_ready, 2 * p + t - 1)
                    act.activation(s_buf[:, t, :], ps_a[:].rearrange("p a n -> p (a n)")[:, 0:INNER],
                                   ACT.Silu).then_inc(s_ready, 1)
                    act.wait_ge(s_ready, 2 * p + t + 1)
                    act.activation(k_buf[:, t, :], s_buf[:, t, :], ACT.Abs,
                                   accum_out=mag_sum[:, t:t + 1]).then_inc(k_ready, 1)

                def count_b(p, n):
                    act.wait_ge(cand_ready, CANDS * p + n + 1)
                    act.activation(junk_a[:], k_buf[:, 1, :], ACT.Sign, bias=cand[:, 1:2], scale=-1.0,
                                   accum_out=below[:, 1:2]).then_inc(cnt_act, 1)

                def count_last(p):
                    act.wait_ge(cand_ready, CANDS * p + STEPS + 1)
                    for t in range(2):
                        act.wait_ge(cnt_act, ACT_COUNTS * p + STEPS + t)
                        act.activation(junk_a[:], k_buf[:, t, :], ACT.Sign, bias=cand[:, t:t + 1], scale=-1.0,
                                       accum_out=at_most[:, t:t + 1]).then_inc(cnt_act, 1)

                def zt_high(p, i):
                    n = 2 * NG * (p - 1) + i
                    c0, c1 = GROUPS[i % NG]
                    act.wait_ge(zt_psum, n + 1)
                    if not (isinstance(n, int) and n < NG):
                        act.wait_ge(down_done, n - NG + 1)
                    act.activation(zt_hi[:, c0 * P:c1 * P], ps_t[:, i % 2, 0:(c1 - c0) * P],
                                   ACT.Copy).then_inc(zt_h, 1)

                def gate_silu(p):
                    for t in range(2):
                        act.wait_ge(q_biased, 2 * p + t + 1)
                        act.activation(gate2[:, t, :], gate2[:, t, :], ACT.Silu).then_inc(g_ready, 1)

                def pair(p, back, ahead, first=False):
                    for t in range(2):
                        silu_keys(p, t, not first)
                    if first:
                        for u in range(N_GU, len(units)):
                            split_hi(u)
                    count_b(p, 0)
                    count_b(p, 1)
                    if back:
                        zt_high(p, 0)
                        zt_high(p, 1)
                    for i in range(2, 6):
                        count_b(p, i)
                        if back:
                            zt_high(p, i)
                    count_b(p, 6)
                    count_b(p, 7)
                    count_last(p)
                    if ahead:
                        for t in range(2):
                            xt_high(p + 1, t)
                    gate_silu(p)

                pair(0, False, True, first=True)
                pair(1, True, True)
                with act.Fori(2, PAIRS - 1) as p:
                    pair(p, True, True)
                pair(PAIRS - 1, True, False)
                for k in range(KH):
                    act.wait_ge(full, k + 1)
                    act.activation(weff[:, k, :], bankf[k % 2], ACT.Copy).then_inc(free, 1)
                for i in range(2 * NG):
                    zt_high(PAIRS, i)

            @block_a.vector
            def _(dve):
                def split_lo(u):
                    dve.wait_ge(w_hi, u + 1)
                    dve.tensor_tensor(units[u][3], slot_ap(u), units[u][2].bitcast(F32),
                                      ALU.subtract).then_inc(w_lo, 1)

                def xt_low(p, t):
                    dve.wait_ge(xt_h, 2 * p + t + 1)
                    dve.tensor_tensor(xt_lo[:, t, :], ps_t[:, t, :], xt_hi[:, t, :].bitcast(F32),
                                      ALU.subtract).then_inc(xt_l, 1)

                def norm_stats(p):
                    dve.wait_ge(x_in, 16 * (p + 1))
                    for t in range(2):
                        dve.bn_stats(stats[:, t, :], xin[:, t, :]).then_inc(ln_st, 1)
                    for t in range(2):
                        dve.wait_ge(ln_st, 2 * p + t + 1)
                        settled(dve, dve_passed)
                        dve.bn_aggr(mv[:, t, :], stats[:, t, :]).then_inc(ln_mv, 1)
                    dve.wait_ge(ln_mv, 2 * p + 2)
                    dve.tensor_scalar(var_eps[:], mv[:, :, 1], EPS, None, ALU.add).then_inc(ln_ve, 1)

                def norm_apply(p):
                    dve.wait_ge(ln_rs, p + 1)
                    for t in range(2):
                        dve.tensor_scalar(xin[:, t, :], xin[:, t, :], mv[:, t, 0:1], rstd[:, t:t + 1],
                                          ALU.subtract, ALU.mult).then_inc(xn_ready, 1)

                norm_stats(0)
                norm_apply(0)
                for k in range(KH):
                    dve.wait_ge(t_mag, k + 1)
                    dve.tensor_scalar(thr[:, k:k + 1], mags[:, k:k + 1], 1.0 / HID, TERNARY,
                                      ALU.mult, ALU.mult).then_inc(t_thr, 1)
                    dve.wait_ge(t_thr, 2 * k + 1)
                    dve.tensor_scalar(thr_neg[:, k:k + 1], thr[:, k:k + 1], -1.0, None,
                                      ALU.mult).then_inc(t_thr, 1)
                    w = s_buf[:, k // 2, (k % 2) * HID:(k % 2 + 1) * HID]
                    neg = gate2[:, k % 2, :]
                    dve.wait_ge(t_thr, 2 * k + 2)
                    if k >= 2:
                        dve.wait_ge(t_q, k - 1)
                    dve.tensor_scalar(neg, w, thr_neg[:, k:k + 1], None, ALU.is_lt).then_inc(t_neg, 1)
                    dve.wait_ge(t_neg, k + 1)
                    dve.scalar_tensor_tensor(out=w, in0=w, scalar=thr[:, k:k + 1], in1=neg,
                                             op0=ALU.is_gt, op1=ALU.subtract).then_inc(t_q, 1)
                for t in range(2):
                    xt_low(0, t)
                for k in range(KH):
                    dve.wait_ge(t_tr, k + 1)
                    dve.tensor_copy(q_t[:, k, :], ps_b[:, k % 3, :]).then_inc(t_cp, 1)
                for u in range(N_GU):
                    split_lo(u)

                def product(p, t):
                    dve.wait_ge(up_done, 2 * p + t + 1)
                    dve.wait_ge(k_ready, 2 * p + t + 1)
                    dve.tensor_tensor(s_buf[:, t, :], s_buf[:, t, :],
                                      ps_b[:].rearrange("p a n -> p (a n)")[:, 0:INNER],
                                      ALU.mult).then_inc(z_ready, 1)

                def bracket(p):
                    dve.wait_ge(k_ready, 2 * p + 2)
                    dve.tensor_tensor(widths[:], powers[:],
                                      mag_sum[:].rearrange("p (o t) -> p o t", o=1).to_broadcast(
                                          [P, STEPS + 2, 2]), ALU.mult).then_inc(wid_ready, 1)
                    dve.tensor_scalar(cand[:], mag_sum[:], (LOW + HIGH) / 2 / INNER, None,
                                      ALU.mult).then_inc(cand_ready, 1)

                def halve(p, n):
                    dve.wait_ge(cand_ready, CANDS * p + n + 1)
                    if n == 0:
                        dve.wait_ge(wid_ready, p + 1)
                    if n < STEPS - 1:
                        dve.tensor_tensor(cand_low[:], cand[:], widths[:, n + 2, :],
                                          ALU.subtract).then_inc(candlow_ready, 1)
                    else:
                        dve.tensor_copy(cand_low[:], cand[:]).then_inc(candlow_ready, 1)
                    dve.tensor_scalar(junk_d[:], k_buf[:, 0, :], cand[:, 0:1], -float(DROP),
                                      ALU.is_lt, ALU.add, accum_out=below[:, 0:1]).then_inc(cnt_dve, 1)
                    dve.wait_ge(cnt_dve, STEPS * p + n + 1)
                    dve.wait_ge(cnt_act, ACT_COUNTS * p + n + 1)
                    dve.scalar_tensor_tensor(out=rise[:], in0=below[:], scalar=0.0, in1=widths[:, n + 1, :],
                                             op0=ALU.is_lt, op1=ALU.mult).then_inc(rise_ready, 1)
                    dve.wait_ge(rise_ready, STEPS * p + n + 1)
                    dve.wait_ge(candlow_ready, STEPS * p + n + 1)
                    dve.tensor_tensor(cand[:], cand_low[:], rise[:], ALU.add).then_inc(cand_ready, 1)

                def largest_under(p, t, back):
                    dve.wait_ge(cand_ready, CANDS * p + STEPS + 1)
                    if back:
                        dve.wait_ge(zt_psum, 2 * NG * (p - 1) + NG * (t + 1))
                    dve.scalar_tensor_tensor(out=m_buf[:, t, 0:INNER], in0=k_buf[:, t, :],
                                             scalar=cand[:, t:t + 1], in1=k_buf[:, t, :],
                                             op0=ALU.is_le, op1=ALU.mult).then_inc(small_ready, 1)
                    dve.wait_ge(small_ready, 2 * p + t + 1)
                    settled(dve, dve_passed)
                    dve.max(top8[:, t, :], m_buf[:, t, 0:INNER]).then_inc(top_ready, 1)

                def choose(p):
                    done = [PICKS * p]

                    def step(ins):
                        done[0] = done[0] + 1
                        ins.then_inc(picked, 1)
                        dve.wait_ge(picked, done[0])

                    dve.wait_ge(cnt_act, ACT_COUNTS * (p + 1))
                    dve.wait_ge(top_ready, 2 * p + 2)
                    step(dve.tensor_scalar(rank[:], at_most[:], 0.5, 0.25, ALU.mult, ALU.add))
                    step(dve.tensor_tensor(pick[:], iota8[:], col(rank[:], 8), ALU.subtract))
                    step(dve.tensor_tensor(pick[:], pick[:], pick[:], ALU.mult))
                    step(dve.scalar_tensor_tensor(out=pick[:], in0=pick[:], scalar=0.1, in1=top8[:],
                                                  op0=ALU.is_lt, op1=ALU.mult))
                    step(dve.tensor_reduce(tau[:], pick[:], AX_X, ALU.add))
                    step(dve.tensor_tensor(pick[:], top8[:], col(tau[:], 8), ALU.is_gt))
                    step(dve.tensor_reduce(above[:], pick[:], AX_X, ALU.add))
                    step(dve.tensor_tensor(above[:], above[:], rank[:], ALU.subtract))
                    step(dve.tensor_tensor(above[:], above[:], above[:], ALU.mult))
                    step(dve.tensor_scalar(bad[:], tau[:], 0.0, None, ALU.is_le))
                    step(dve.scalar_tensor_tensor(out=bad[:], in0=above[:], scalar=0.1, in1=bad[:],
                                                  op0=ALU.is_gt, op1=ALU.max))
                    dve.wait_ge(bad_sum, p + 1)
                    step(dve.tensor_tensor(bad_int[:, 0:1], bad_all[:, 0:1], bad_all[:, 1:2], ALU.add))
                    settled(dve, dve_passed)
                    failed = dve.value_load(bad_int[0:1, 0:1], min_val=0, max_val=2 * P)
                    with dve.If(failed > 0):
                        exact_choice()

                def exact_choice():
                    dve.memset(lo_bits[:], 0)
                    dve.memset(bit[:], 1 << 30)
                    dve.drain()
                    with dve.Fori(0, 31):
                        dve.tensor_tensor(cand_bits[:], lo_bits[:], bit[:], ALU.bitwise_or)
                        dve.drain()
                        for t in range(2):
                            dve.tensor_scalar(junk_d[:], k_buf[:, t, :], cand_bits[:, t:t + 1].bitcast(F32),
                                              -float(DROP), ALU.is_lt, ALU.add, accum_out=above[:, t:t + 1])
                            dve.drain()
                        dve.scalar_tensor_tensor(out=set_bits[:], in0=above[:], scalar=0.0, in1=bit[:],
                                                 op0=ALU.is_lt, op1=ALU.mult)
                        dve.drain()
                        dve.tensor_tensor(lo_bits[:], lo_bits[:], set_bits[:], ALU.bitwise_or)
                        dve.tensor_scalar(bit[:], bit[:], 1, None, ALU.logical_shift_right)
                        dve.drain()
                    dve.tensor_copy(tau[:], lo_bits[:].bitcast(F32))
                    dve.drain()
                    for t in range(2):
                        keys, tau_t = k_buf[:, t, :], tau[:, t:t + 1]
                        equal, seen = m_buf[:, 0, 0:INNER], m_buf[:, 1, 0:INNER]
                        dve.tensor_scalar(junk_d[:], keys, tau_t, -float(DROP), ALU.is_lt, ALU.add,
                                          accum_out=above[:, t:t + 1])
                        dve.tensor_scalar(equal, keys, tau_t, None, ALU.is_equal)
                        dve.drain()
                        dve.tensor_scalar(above[:, t:t + 1], above[:, t:t + 1], -1.0, None, ALU.mult)
                        dve.tensor_tensor_scan(seen, one[:].to_broadcast([P, INNER]), equal, 0.0,
                                               ALU.mult, ALU.add)
                        dve.drain()
                        dve.scalar_tensor_tensor(out=seen, in0=seen, scalar=above[:, t:t + 1], in1=equal,
                                                 op0=ALU.is_gt, op1=ALU.mult)
                        dve.drain()
                        dve.scalar_tensor_tensor(out=keys, in0=seen, scalar=3.0e38, in1=keys,
                                                 op0=ALU.mult, op1=ALU.max)
                        dve.drain()

                def mask(p):
                    for t in range(2):
                        dve.wait_ge(z_ready, 2 * p + t + 1)
                        dve.scalar_tensor_tensor(out=m_buf[:, t, 0:INNER], in0=k_buf[:, t, :],
                                                 scalar=tau[:, t:t + 1], in1=s_buf[:, t, :],
                                                 op0=ALU.is_gt, op1=ALU.mult).then_inc(mask_ready, 1)

                def zt_low(p, i):
                    n = 2 * NG * (p - 1) + i
                    c0, c1 = GROUPS[i % NG]
                    dve.wait_ge(zt_h, n + 1)
                    dve.tensor_tensor(zt_lo[:, c0 * P:c1 * P], ps_t[:, i % 2, 0:(c1 - c0) * P],
                                      zt_hi[:, c0 * P:c1 * P].bitcast(F32), ALU.subtract).then_inc(zt_l, 1)

                def down_gate(p, t):
                    dve.wait_ge(down_done, 2 * NG * (p - 1) + NG * (t + 1))
                    dve.wait_ge(g_ready, 2 * (p - 1) + t + 1)
                    dve.tensor_tensor(gate2[:, t, :], ps_a[:, t, :], gate2[:, t, :],
                                      ALU.mult).then_inc(down_out, 1)

                def q_bias(p, t, back):
                    dve.wait_ge(q_done, 2 * p + t + 1)
                    if back:
                        dve.wait_ge(x1_ready, 2 * (p - 1) + t + 1)
                    dve.tensor_tensor(gate2[:, t, :], ps_b[:, t, :], bias_b[:], ALU.add).then_inc(q_biased, 1)

                def pair(p, back, ahead, first=False):
                    product(p, 0)
                    if first:
                        for u in range(N_GU, len(units)):
                            split_lo(u)
                    if ahead:
                        norm_stats(p + 1)
                    bracket(p)
                    halve(p, 0)
                    halve(p, 1)
                    product(p, 1)
                    if back:
                        zt_low(p, 0)
                        zt_low(p, 1)
                    if ahead:
                        norm_apply(p + 1)
                    for i in range(2, 6):
                        halve(p, i)
                        if back:
                            zt_low(p, i)
                    if back:
                        down_gate(p, 0)
                    halve(p, 6)
                    halve(p, 7)
                    if back:
                        down_gate(p, 1)
                    largest_under(p, 0, back)
                    if ahead:
                        for t in range(2):
                            xt_low(p + 1, t)
                    largest_under(p, 1, back)
                    if first:
                        dve.wait_ge(bias_in, 16)
                    for t in range(2):
                        q_bias(p, t, back)
                    choose(p)
                    mask(p)

                pair(0, False, True, first=True)
                pair(1, True, True)
                with dve.Fori(2, PAIRS - 1) as p:
                    pair(p, True, True)
                pair(PAIRS - 1, True, False)
                for i in range(2 * NG):
                    zt_low(PAIRS, i)
                    if i in (0, 1, 5):
                        norm2_stats(dve, min(i, 2))
                    elif i == 2:
                        norm2_root(dve, 0, 0, 2)
                    else:
                        norm2_apply(dve, i - 3)
                for t in range(2):
                    down_gate(PAIRS, t)

            @block_a.tensor
            def _(pe):
                def x_transpose(p, t):
                    pe.wait_ge(xn_ready, 2 * p + t + 1)
                    for k in range(KH):
                        last = pe.transpose(ps_t[:, t, k * P:(k + 1) * P], xin[:, t, k * P:(k + 1) * P], ident[:])
                    last.then_inc(xt_psum, 1)

                def project(p, t, hi, lo, bank, done, unit0):
                    for k in range(KH):
                        if isinstance(p, int) and p == 0 and t == 0:
                            pe.wait_ge(w_lo, unit0 + k + 1)
                        xh, xl = xt_hi[:, t, k * P:(k + 1) * P], xt_lo[:, t, k * P:(k + 1) * P]
                        for n, (xs, ws) in enumerate(((xh, hi), (xh, lo), (xl, hi))):
                            for c, (c0, c1) in enumerate(NCOL):
                                last = pe.matmul(bank[:, c, 0:c1 - c0], xs, ws[:, k, c0:c1],
                                                 start=(k == 0 and n == 0), stop=(k == KH - 1 and n == 2))
                    last.then_inc(done, 1)

                def zt_transpose(p, i):
                    n = 2 * NG * (p - 1) + i
                    t, (c0, c1) = i // NG, GROUPS[i % NG]
                    pe.wait_ge(mask_ready, 2 * (p - 1) + t + 1)
                    if not (isinstance(n, int) and n < 2):
                        pe.wait_ge(zt_l, n - 1)
                    for c in range(c0, c1):
                        last = pe.transpose(ps_t[:, i % 2, (c - c0) * P:(c - c0 + 1) * P],
                                            m_buf[:, t, c * P:(c + 1) * P], ident[:])
                    last.then_inc(zt_psum, 1)

                def down(p, i):
                    t, (c0, c1) = i // NG, GROUPS[i % NG]
                    pe.wait_ge(zt_l, 2 * NG * (p - 1) + i + 1)
                    if isinstance(p, int) and p == 1:
                        pe.wait_ge(w_lo, len(units))
                    for c in range(c0, c1):
                        rows = min(P, INNER - c * P)
                        zh = zt_hi[0:rows, c * P:(c + 1) * P]
                        zl = zt_lo[0:rows, c * P:(c + 1) * P]
                        for n, (zs, ws) in enumerate(((zh, wd_hi), (zh, wd_lo), (zl, wd_hi))):
                            last = pe.matmul(ps_a[:, t, :], zs, ws[0:rows, c, :],
                                             start=(c == 0 and n == 0), stop=(c == CHUNKS - 1 and n == 2))
                    last.then_inc(down_done, 1)

                def ternary(p, t):
                    for k in range(KH):
                        for n, xs in enumerate((xt_hi, xt_lo)):
                            last = pe.matmul(ps_b[:, t, :], xs[:, t, k * P:(k + 1) * P], q_t[:, k, :],
                                             start=(k == 0 and n == 0), stop=(k == KH - 1 and n == 1))
                    last.then_inc(q_done, 1)

                def back_half(p):
                    order = [("T", 0), ("T", 1), ("D", 0)]
                    for i in range(2, 2 * NG):
                        order += [("T", i), ("D", i - 1)]
                    order.append(("D", 2 * NG - 1))
                    for kind, i in order:
                        (zt_transpose if kind == "T" else down)(p, i)

                def pair(p, back, ahead):
                    for t in range(2):
                        pe.wait_ge(xt_l, 2 * p + t + 1)
                        if t == 1:
                            pe.wait_ge(s_ready, 2 * p + 1)
                        elif not (isinstance(p, int) and p < 2):
                            pe.wait_ge(down_out, 2 * (p - 1))
                        project(p, t, wg_hi, wg_lo, ps_a, gate_done, 0)
                        if t == 1:
                            pe.wait_ge(z_ready, 2 * p + 1)
                        elif not (isinstance(p, int) and p == 0):
                            pe.wait_ge(q_biased, 2 * p)
                        project(p, t, wu_hi, wu_lo, ps_b, up_done, KH)
                    if back:
                        pe.wait_ge(s_ready, 2 * p + 2)
                        back_half(p)
                    for t in range(2):
                        if t == 0:
                            pe.wait_ge(z_ready, 2 * p + 2)
                        ternary(p, t)
                        if ahead:
                            x_transpose(p + 1, t)

                pe.wait_ge(c_const, 2)
                for t in range(2):
                    x_transpose(0, t)
                for k in range(KH):
                    pe.wait_ge(t_q, KH)
                    if k == 3:
                        pe.wait_ge(t_cp, 1)
                    for o in range(KH):
                        last = pe.transpose(ps_b[:, k % 3, o * P:(o + 1) * P],
                                            s_buf[:, o // 2, (o % 2) * HID + k * P:(o % 2) * HID + (k + 1) * P],
                                            ident[:])
                    last.then_inc(t_tr, 1)
                pe.wait_ge(t_cp, KH)
                pair(0, False, True)
                pair(1, True, True)
                with pe.Fori(2, PAIRS - 1) as p:
                    pair(p, True, True)
                pair(PAIRS - 1, True, False)
                pe.wait_ge(fold_b, ER // P)
                for k in range(KH):
                    if k >= 2:
                        pe.wait_ge(free, k - 1)
                    for e in range(ER // P):
                        pe.matmul(bankf[k % 2], f_a[:, e, k * P:(k + 1) * P], f_b[:, e, :],
                                  start=(e == 0), stop=False)
                    pe.matmul(bankf[k % 2], ident[:], f_wt[:, k, :], start=False, stop=True).then_inc(full, 1)
                back_half(PAIRS)

        with ExitStack() as bctx:
            def sb(name, shape, dt=F32):
                return bctx.enter_context(nc.sbuf_tensor(name, shape, dt))

            xt = sb("xt", [P, KH, TOKENS])
            g2 = sb("g2", [P, VOCAB // P, TOKENS])
            f_bias = sb("f_bias", [P, VOCAB // P])
            bout_c = sb("bout_c", [P, VOCAB // P])
            b1_c = sb("b1_c", [P, DEPTH * 2])
            w1 = sb("w1", [P, DFF])
            w2 = sb("w2", [P, BATCH, 2, P])
            wout = sb("wout", [P, VOCAB])
            ident2 = sb("ident2", [P, P])
            center = sb("center", [P, P])
            means = sb("means", [P, 2])
            expo2 = sb("expo2", [P, 16])
            h = over_weights(SEQ)
            y = sb("y", [P, SEQ])
            xc = sb("xc", [P, SEQ])
            sq = sb("sq", [P, SEQ])
            lnv = sb("lnv", [P, HALVES, 8])
            lnr = sb("lnr", [P, HALVES, 8])
            rot_c = sb("rot_c", [P, DEPTH, SEQ])
            rot_s = sb("rot_s", [P, DEPTH, SEQ])
            tbig = sb("tbig", [P, SEQ])
            rho = sb("rho", [P, DEPTH])

            last_in = sem("last_in")
            lay_in = sem("lay_in")
            mk = sem("mk")
            xt_ps = sem("xt_ps")
            xt_a = sem("xt_a")
            xt_v = sem("xt_v")
            h_ps = sem("h_ps")
            h_ready = sem("h_ready")
            rho_s = sem("rho_s")
            ln_cent = sem("ln_cent")
            ln_xc = sem("ln_xc")
            ln_sq = sem("ln_sq")
            ln_var = sem("ln_var")
            ln_v = sem("ln_v")
            ln_r = sem("ln_r")
            ln_w = sem("ln_w")
            ln_bc = sem("ln_bc")
            ln_y = sem("ln_y")
            ln_o = sem("ln_o")
            cv_wr = sem("cv_wr")
            cv_wi = sem("cv_wi")
            cv_ur = sem("cv_ur")
            cv_ui = sem("cv_ui")
            cv_a = sem("cv_a")
            cv_b = sem("cv_b")
            cv_ab = sem("cv_ab")
            ff_2 = sem("ff_2")
            r_ready = sem("r_ready")
            o_ps = sem("o_ps")
            o_ready = sem("o_ready")
            o_out = sem("o_out")

            bank1 = [ps_a[:, 0, :], ps_a[:, 1, :]]
            bank2 = [ps_a[:, 2, :], ps_b[:, 0, :]]
            bankv = [ps_b[:, 1, :], ps_b[:, 2, :]]
            bankx = [ps_t[:, 0, :], ps_t[:, 1, :]]
            obank = bank1 + bank2
            FOLD = KH
            UNITS = 4 + 2 * 4

            def use(l, k):
                return FOLD + UNITS * l + k

            def cs(c):
                return slice(c * NB, (c + 1) * NB)

            def pcol(l, j):
                return par[:, bass.ds(NPAR * l + j, 1)]

            block_b = bctx.enter_context(nc.Block())

            @block_b.sync
            def _(sp):
                def both(dst, src, done):
                    for b in range(BATCH):
                        sp.dma_start(dst[b * DIM:(b + 1) * DIM, :], src).then_inc(done, 16)

                load_x1_group(sp, ORDER[3])
                sp.dma_start(b1_c[:], b1_cols).then_inc(last_in, 16)
                sp.dma_start(f_bias[:], f1_bias_cols).then_inc(last_in, 16)
                sp.dma_start(bout_c[:], bout_cols).then_inc(last_in, 16)
                both(wout, wout_t, last_in)
                sp.wait_ge(mk, N_MK)
                with sp.Fori(0, DEPTH) as l:
                    sp.wait_ge(ff_2, 2 * l)
                    for b in range(BATCH):
                        sp.dma_start(w1[b * DIM:(b + 1) * DIM, :].rearrange("p (o n) -> p o n", o=1),
                                     w1_t[bass.ds(l, 1), :, :].rearrange("o p n -> p o n")).then_inc(lay_in, 16)
                        sp.dma_start(w2[:, b, :, b * DIM:(b + 1) * DIM],
                                     w2_t[bass.ds(l, 1), :, :].rearrange("o (m p) d -> p (o m) d", p=P)
                                     ).then_inc(lay_in, 16)
                for t in range(TILES):
                    sp.wait_ge(o_ready, t + 1)
                    sp.dma_start(out[t * P:(t + 1) * P, :], x1[:, t, :]).then_inc(o_out, 16)
                sp.wait_ge(o_out, 16 * TILES)

            @block_b.gpsimd
            def _(pool):
                made = [0]

                def make(ins):
                    made[0] += 1
                    ins.then_inc(mk, 1)
                    pool.wait_ge(mk, made[0])

                make(pool.memset(ident2[:], 0.0))
                make(pool.affine_select(out=ident2[:], in_=ident2[:], compare_op=ALU.not_equal, fill=1.0,
                                        base=0, pattern=[[-1, P]], channel_multiplier=1))
                make(pool.memset(w2[:], 0.0))
                make(pool.memset(expo2[:], -0.5))
                make(pool.memset(center[:], 0.0))
                make(pool.memset(means[:], 0.0))
                for b in range(BATCH):
                    half = slice(b * DIM, (b + 1) * DIM)
                    make(pool.memset(center[half, half], -1.0 / DIM))
                    make(pool.memset(means[half, b:b + 1], 1.0 / DIM))
                make(pool.tensor_tensor(center[:], center[:], ident2[:], ALU.add))
                assert made[0] == N_MK

                tables_powers(pool, 1)

                def tables(l, first):
                    done = [first]

                    def big(o, a, b, op):
                        done[0] = done[0] + 1
                        settled(pool, pool_passed)
                        pool.tensor_tensor(o, a, b, op).then_inc(tb, 1)
                        pool.wait_ge(tb, done[0])

                    def part(j, fine):
                        s = small[:, j, bass.ds(l, 1), :]
                        s = s.rearrange("p o n -> p o n" if fine else "p o n -> p n o")
                        return s.to_broadcast([P, COARSE, COARSE])

                    fr, fi, cr, ci = part(0, True), part(1, True), part(2, False), part(3, False)
                    grid = "p o (a b) -> p (o a) b"
                    co = rot_c[:, bass.ds(l, 1), :].rearrange(grid, b=COARSE)
                    si = rot_s[:, bass.ds(l, 1), :].rearrange(grid, b=COARSE)
                    t = tbig[:].rearrange("p (a b) -> p a b", b=COARSE)
                    big(t, ci, fi, ALU.mult)
                    big(co, cr, fr, ALU.mult)
                    big(co, co, t, ALU.subtract)
                    big(t, ci, fr, ALU.mult)
                    big(si, cr, fi, ALU.mult)
                    big(si, si, t, ALU.add)

                def roots(q):
                    for c in range(HALVES):
                        pool.wait_ge(ln_v, 2 * q + c + 1)
                        pool.tensor_tensor(lnr[:, c, :], lnv[:, c, :], expo2[:, 0:8], ALU.pow).then_inc(ln_r, 1)

                def conv(l):
                    sin = [rot_s[:, bass.ds(l, 1), cs(c)] for c in range(HALVES)]
                    for c in range(HALVES):
                        pool.wait_ge(ln_o, 4 * l + c + 1)
                        settled(pool, pool_passed)
                        pool.tensor_tensor(w_im[:, cs(c)].rearrange("p (o n) -> p o n", o=1),
                                           y[:, cs(c)].rearrange("p (o n) -> p o n", o=1), sin[c],
                                           ALU.mult).then_inc(cv_wi, 1)
                    for c in range(HALVES):
                        pool.wait_ge(cv_ui, 2 * l + c + 1)
                        settled(pool, pool_passed)
                        pool.tensor_tensor(w_im[:, cs(c)].rearrange("p (o n) -> p o n", o=1),
                                           u_im[:, cs(c)].rearrange("p (o n) -> p o n", o=1), sin[c],
                                           ALU.mult).then_inc(cv_b, 1)

                tables(0, N_SMALL)
                with pool.Fori(0, DEPTH - 1) as l:
                    roots(2 * l)
                    conv(l)
                    roots(2 * l + 1)
                    tables(l + 1, 6 * l + 6 + N_SMALL)
                roots(2 * DEPTH - 2)
                conv(DEPTH - 1)
                roots(2 * DEPTH - 1)
                roots(2 * DEPTH)

            @block_b.scalar
            def _(act):
                act.wait_ge(tb, N_RAD)
                act.activation(rho[:], rad, ACT.Tanh).then_inc(rho_s, 1)
                for i in range(0, TILES, 2):
                    t = 4 * ORDER[i // 4] + i % 4
                    act.wait_ge(xt_ps, i + 1)
                    act.activation(xt[:, :, t * P:(t + 1) * P],
                                   bankx[0].rearrange("p (k n) -> p k n", k=KH), ACT.Copy).then_inc(xt_a, 1)

                def ln_squares(q):
                    for c in range(HALVES):
                        act.wait_ge(ln_xc, 2 * q + c + 1)
                        act.activation(sq[:, cs(c)], xc[:, cs(c)], ACT.Square).then_inc(ln_sq, 1)

                def ln_out(q, dst, func, w, b):
                    for c in range(HALVES):
                        act.wait_ge(ln_y, 2 * q + c + 1)
                        settled(act, act_passed)
                        act.activation(dst[:, cs(c)], xc[:, cs(c)], func, scale=w, bias=b).then_inc(ln_o, 1)

                def gates(l, ks):
                    for k in ks:
                        act.wait_ge(full, use(l, k) + 1)
                        settled(act, act_passed)
                        act.activation(g2[:, k, bass.ds(NB * l, NB)], bankx[k % 2], ACT.Silu,
                                       bias=f_bias[:, k:k + 1]).then_inc(free, 1)

                act.wait_ge(par_in, 16 * 4)
                act.wait_ge(last_in, 16 * 5)
                with act.Fori(0, DEPTH) as l:
                    ln_squares(2 * l)
                    ln_out(2 * l, y, ACT.Silu, pcol(l, C_L1W), pcol(l, C_L1B))
                    gates(l, (0, 1, 2))
                    ln_squares(2 * l + 1)
                    gates(l, (3,))
                    ln_out(2 * l + 1, y, ACT.Identity, pcol(l, C_L2W), pcol(l, C_L2B))
                    for c in range(HALVES):
                        for u in range(4):
                            act.wait_ge(full, use(l, 4 + 4 * c + u) + 1)
                            if c == 1 and u == 0:
                                act.wait_ge(ff_2, 2 * l + 1)
                            settled(act, act_passed)
                            act.activation(hs[:, u, :], bankx[u % 2], ACT.Silu,
                                           bias=b1_c[:, bass.ds(2 * l + u % 2, 1)]).then_inc(free, 1)
                q = 2 * DEPTH
                ln_squares(q)
                ln_out(q, y, ACT.Identity, par_last[:, 0:1], par_last[:, 1:2])

            @block_b.vector
            def _(dve):
                def xt_odd(i):
                    for j in (1, 3):
                        t = 4 * ORDER[i] + j
                        dve.wait_ge(xt_ps, 4 * i + j + 1)
                        dve.tensor_copy(xt[:, :, t * P:(t + 1) * P],
                                        bankx[1].rearrange("p (k n) -> p k n", k=KH)).then_inc(xt_v, 1)

                def h_in(c):
                    dve.wait_ge(h_ps, c + 1)
                    if c == 0:
                        dve.wait_ge(par_in, 16 * 4)
                    dve.tensor_scalar(h[:, cs(c)], bank1[c], par_last[:, 2:3], None, ALU.add).then_inc(h_ready, 1)

                xt_odd(0)
                norm2_root(dve, 1, 2, 3)
                norm2_apply(dve, 2)
                norm2_stats(dve, 3)
                norm2_root(dve, 2, 3, 4)
                xt_odd(1)
                norm2_apply(dve, 3)
                h_in(0)
                xt_odd(2)
                xt_odd(3)
                h_in(1)

                def ln(q):
                    for c in range(HALVES):
                        dve.wait_ge(ln_cent, 2 * q + c + 1)
                        dve.tensor_copy(xc[:, cs(c)], bank1[c]).then_inc(ln_xc, 1)
                    for c in range(HALVES):
                        dve.wait_ge(ln_var, 2 * q + c + 1)
                        dve.tensor_scalar(lnv[:, c, :], bankv[c][:, 0:8], EPS, None, ALU.add).then_inc(ln_v, 1)
                    for c in range(HALVES):
                        dve.wait_ge(ln_r, 2 * q + c + 1)
                        dve.tensor_copy(sq[:, cs(c)].rearrange("p (t d) -> p t d", d=DIM),
                                        lnr[:, c, :].rearrange("p (t o) -> p t o", o=1).to_broadcast([P, 8, DIM])
                                        ).then_inc(ln_w, 1)
                    for c in range(HALVES):
                        dve.wait_ge(ln_bc, 2 * q + c + 1)
                        dve.wait_ge(ln_xc, 2 * q + c + 1)
                        dve.tensor_tensor(xc[:, cs(c)], xc[:, cs(c)], bank2[c], ALU.mult).then_inc(ln_y, 1)

                def conv(l):
                    def one(ap):
                        return ap.rearrange("p (o n) -> p o n", o=1)

                    cos = [rot_c[:, bass.ds(l, 1), cs(c)] for c in range(HALVES)]
                    decay = rho[:, bass.ds(l, 1)].to_broadcast([P, NB])
                    dve.wait_ge(tb, N_SMALL + 6 * l + 6)
                    dve.wait_ge(rho_s, 1)
                    for c in range(HALVES):
                        dve.wait_ge(ln_o, 4 * l + c + 1)
                        dve.tensor_tensor(one(w_re[:, cs(c)]), one(y[:, cs(c)]), cos[c],
                                          ALU.mult).then_inc(cv_wr, 1)
                    for name, w, u, done in (("re", w_re, u_re, cv_ur), ("im", w_im, u_im, cv_ui)):
                        for c in range(HALVES):
                            dve.wait_ge(cv_wr if name == "re" else cv_wi, 2 * l + c + 1)
                            if c == 0:
                                first = u0[:, 0 if name == "re" else 1, bass.ds(l, 1)]
                            else:
                                dve.wait_ge(done, 2 * l + 1)
                                first = u[:, NB - 1:NB]
                            dve.tensor_tensor_scan(u[:, cs(c)], decay, w[:, cs(c)], first,
                                                   ALU.mult, ALU.add).then_inc(done, 1)
                    for c in range(HALVES):
                        dve.wait_ge(cv_ur, 2 * l + c + 1)
                        dve.tensor_tensor(one(w_re[:, cs(c)]), one(u_re[:, cs(c)]), cos[c],
                                          ALU.mult).then_inc(cv_a, 1)
                    for c in range(HALVES):
                        dve.wait_ge(cv_a, 2 * l + c + 1)
                        dve.wait_ge(cv_b, 2 * l + c + 1)
                        dve.tensor_tensor(w_re[:, cs(c)], w_re[:, cs(c)], w_im[:, cs(c)], ALU.add).then_inc(cv_ab, 1)
                        dve.wait_ge(cv_ab, 2 * l + c + 1)
                        dve.scalar_tensor_tensor(out=h[:, cs(c)], in0=w_re[:, cs(c)], scalar=pcol(l, C_SCL),
                                                 in1=h[:, cs(c)], op0=ALU.mult, op1=ALU.add).then_inc(h_ready, 1)

                with dve.Fori(0, DEPTH) as l:
                    ln(2 * l)
                    conv(l)
                    ln(2 * l + 1)
                    for c in range(HALVES):
                        dve.wait_ge(ff_2, 2 * l + c + 1)
                        dve.scalar_tensor_tensor(out=h[:, cs(c)], in0=bank1[c], scalar=pcol(l, C_B2),
                                                 in1=h[:, cs(c)], op0=ALU.add, op1=ALU.add).then_inc(h_ready, 1)
                ln(2 * DEPTH)

                def outer(g):
                    b, c = g // HALVES, g % HALVES
                    for k in range(VOCAB // P):
                        dve.wait_ge(full, use(DEPTH, 4 * g + k) + 1)
                        if g:
                            dve.wait_ge(o_ps, 4 * g)
                        dve.scalar_tensor_tensor(out=res[:, k, :], in0=bankx[k % 2], scalar=bout_c[:, k:k + 1],
                                                 in1=g2[:, k, g * NB:(g + 1) * NB], op0=ALU.add,
                                                 op1=ALU.mult).then_inc(free, 1)

                def inner(g):
                    for j in range(4):
                        t = 4 * g + j
                        dve.wait_ge(o_ps, t + 1)
                        dve.tensor_tensor(x1[:, t, :], obank[j], x1[:, t, :], ALU.add).then_inc(o_ready, 1)

                for g in range(4):
                    outer(g)
                    inner(g)

            @block_b.tensor
            def _(pe):
                pe.wait_ge(mk, 2)
                for i in range(TILES):
                    pe.wait_ge(xn_s, i + 1)
                    if i >= 2:
                        pe.wait_ge(xt_v if i % 2 else xt_a, i // 2)
                    for k in range(KH):
                        last = pe.transpose(bankx[i % 2][:, k * P:(k + 1) * P], xn[:, i % 8, k * P:(k + 1) * P],
                                            ident2[:])
                    last.then_inc(xt_ps, 1)
                    if i % 8 == 7:
                        c = i // 8
                        pe.wait_ge(win_in, 32)
                        pe.wait_ge(xt_a, 4 * c + 4)
                        pe.wait_ge(xt_v, 4 * c + 4)
                        for b in range(BATCH):
                            for k in range(KH):
                                last = pe.matmul(bank1[c], win[:, b, k, :],
                                                 xt[:, k, b * SEQ + c * NB:b * SEQ + (c + 1) * NB],
                                                 start=(b == 0 and k == 0), stop=(b == 1 and k == KH - 1))
                        last.then_inc(h_ps, 1)
                pe.wait_ge(mk, N_MK)

                def layer_norm(q, l=None, i=0):
                    for c in range(HALVES):
                        pe.wait_ge(h_ready, 2 * q + c + 1)
                        pe.matmul(bank1[c], center[:], h[:, cs(c)], start=True, stop=True).then_inc(ln_cent, 1)
                    if l is not None:
                        gate_step(l, i)
                    for c in range(HALVES):
                        pe.wait_ge(ln_sq, 2 * q + c + 1)
                        for j in range(4):
                            last = pe.matmul(bankv[c][:, 2 * j:2 * j + 2],
                                             sq[:, c * NB + j * P:c * NB + (j + 1) * P], means[:],
                                             start=True, stop=True)
                        last.then_inc(ln_var, 1)
                    if l is not None:
                        gate_step(l, i + 1)
                        gate_step(l, i + 2)
                    for c in range(HALVES):
                        pe.wait_ge(ln_w, 2 * q + c + 1)
                        for j in range(4):
                            last = pe.transpose(bank2[c][:, j * P:(j + 1) * P],
                                                sq[:, c * NB + j * P:c * NB + (j + 1) * P], ident2[:])
                        last.then_inc(ln_bc, 1)

                def gate_step(l, i):
                    k, n = i // KH, i % KH
                    if n == 0:
                        pe.wait_ge(free, use(l, k) - 1)
                    last = pe.matmul(bankx[k % 2], weff[:, n, k * P:(k + 1) * P],
                                     xt[:, n, bass.ds(NB * l, NB)], start=(n == 0), stop=(n == KH - 1))
                    if n == KH - 1:
                        last.then_inc(full, 1)

                def up_unit(l, c, u):
                    b, m = u // 2, u % 2
                    pe.wait_ge(free, use(l, 4 + 4 * c + u) - 1)
                    half = slice(b * DIM, (b + 1) * DIM)
                    pe.matmul(bankx[u % 2], w1[half, m * P:(m + 1) * P], y[half, cs(c)],
                              start=True, stop=True).then_inc(full, 1)

                def down_unit(l, c, u):
                    b, m = u // 2, u % 2
                    pe.wait_ge(free, use(l, 4 + 4 * c + u) + 1)
                    last = pe.matmul(bank1[c], w2[:, b, m, :], hs[:, u, :], start=(u == 0), stop=(u == 3))
                    if u == 3:
                        last.then_inc(ff_2, 1)

                with pe.Fori(0, DEPTH) as l:
                    layer_norm(2 * l, l, 0)
                    for i in range(3, 13):
                        gate_step(l, i)
                    layer_norm(2 * l + 1, l, 13)
                    pe.wait_ge(lay_in, 64 * l + 64)
                    for c in range(HALVES):
                        pe.wait_ge(ln_o, 4 * l + 2 + c + 1)
                        up_unit(l, c, 0)
                        up_unit(l, c, 1)
                        down_unit(l, c, 0)
                        up_unit(l, c, 2)
                        down_unit(l, c, 1)
                        up_unit(l, c, 3)
                        down_unit(l, c, 2)
                        down_unit(l, c, 3)
                q = 2 * DEPTH
                layer_norm(q)

                def out_unit(g, k):
                    b, c = g // HALVES, g % HALVES
                    if k == 0:
                        pe.wait_ge(ln_o, 2 * q + c + 1)
                    pe.wait_ge(free, use(DEPTH, 4 * g + k) - 1)
                    half = slice(b * DIM, (b + 1) * DIM)
                    pe.matmul(bankx[k % 2], wout[half, k * P:(k + 1) * P], y[half, cs(c)],
                              start=True, stop=True).then_inc(full, 1)

                def out_tile(g, j):
                    t = 4 * g + j
                    if j == 0:
                        pe.wait_ge(free, use(DEPTH, 4 * g + 3) + 1)
                    if t >= 4:
                        pe.wait_ge(o_ready, t - 3)
                    for k in range(VOCAB // P):
                        last = pe.transpose(obank[j][:, k * P:(k + 1) * P], res[:, k, j * P:(j + 1) * P], ident2[:])
                    last.then_inc(o_ps, 1)

                for g in range(4):
                    for k in range(4):
                        out_unit(g, k)
                    for j in range(4):
                        out_tile(g, j)


def _program(nc, args, out):
    mixture_kernel(nc, *args, out)


def layout(**inputs):
    import numpy as np

    a = {k: np.asarray(v) for k, v in inputs.items()}

    def t(name):
        return np.ascontiguousarray(a[name].T)

    def l1(name):
        return a["L1_attn_" + name]

    per_layer = ["ln1_w", "ln1_b", "phz_re", "phz_im", "lc_re", "lc_im", "sc_lin", "ln2_w", "ln2_b", "b2"]
    data = {
        "x": a["L0_attn_x"].reshape(TOKENS, HID),
        "wg_t": t("L0_attn_w_gate"), "wu_t": t("L0_attn_w_up"), "wd_t": t("L0_attn_w_down"),
        "tern_w": a["L0_ffn_weight"], "ffn_bias": a["L0_ffn_bias"],
        "win_t": t("L1_attn_Win"),
        "cols": np.stack([l1(n) for n in per_layer], axis=1).transpose(2, 0, 1).reshape(DIM, DEPTH * NPAR),
        "last_cols": np.stack([l1("lnl_w"), l1("lnl_b"), l1("bin")], axis=1),
        "b1_cols": l1("b1").reshape(DEPTH * DFF // P, P).T,
        "w1_t": l1("W1").transpose(0, 2, 1), "w2_t": l1("W2").transpose(0, 2, 1),
        "wout_t": t("L1_attn_Wout"), "bout_cols": l1("bout").reshape(VOCAB // P, P).T,
        "f1_w_t": t("L1_ffn_W"), "f1_bias_cols": a["L1_ffn_bias"].reshape(HID // P, P).T,
        "f1_a": a["L1_ffn_A"].reshape(ER, HID),
        "f1_b_t": a["L1_ffn_Bf"].transpose(0, 2, 1).reshape(ER, HID),
        "f1_mix": np.stack([np.repeat(a["L1_ffn_" + n], RANK).reshape(ER // P, P) for n in ("coeffs", "scales")])
        .transpose(2, 0, 1),
    }
    return {name: np.ascontiguousarray(value) for name, value in data.items()}


def kernel(**inputs):
    import concourse.bacc as bacc
    from concourse.bass_utils import run_bass_kernel_spmd

    nc = bacc.Bacc("TRN2", target_bir_lowering=False, num_devices=1)
    arrays, args = {}, []
    for name, value in layout(**inputs).items():
        arrays["in_" + name] = value
        args.append(nc.dram_tensor("in_" + name, value.shape, mybir.dt.from_np(value.dtype),
                                   kind="ExternalInput").ap())
    out = nc.dram_tensor("out_0", (TOKENS, HID), F32, kind="ExternalOutput").ap()
    _program(nc, args, out)
    r = run_bass_kernel_spmd(nc, [arrays], core_ids=[0])
    return r.results[0]["out_0"].reshape(2, TOKENS // 2, HID)
```

```python
from contextlib import ExitStack

import concourse.bass as bass
from concourse import mybir

F32 = mybir.dt.float32
F32R = mybir.dt.float32r
I32 = mybir.dt.int32
I8 = mybir.dt.int8
ALU = mybir.AluOpType
ACT = mybir.ActivationFunctionType
AX_X = mybir.AxisListType.X
RADD = bass.bass_isa.ReduceOp.add

P = 128
EPS = 1e-5

TOKENS, HID, INNER = 2048, 512, 1376
KH = HID // P
TILES = TOKENS // P
PAIRS = TILES // 2
STORED = PAIRS - 2
DROP = INNER // 2
NCOL = [(0, 512), (512, 1024), (1024, INNER)]
CHUNKS = -(-INNER // P)
PADDED = CHUNKS * P
GROUPS = [(0, 4), (4, 8), (8, CHUNKS)]
NG = len(GROUPS)
TERNARY = 0.7

STEPS = 8
LOW, HIGH = 0.6, 0.9
CANDS = STEPS + 1
ACT_COUNTS = STEPS + 2
PICKS = 12
N_CONST = 5 + STEPS + 2 + 8

BATCH, SEQ, DIM, DFF, DEPTH, VOCAB = 2, 1024, 64, 256, 4, 512
NB = 512
HALVES = SEQ // NB
DOUBLINGS = 5
COARSE = 2 ** DOUBLINGS
EXPERTS, RANK = 16, 16
ER = EXPERTS * RANK
(C_L1W, C_L1B, C_PR, C_PI, C_LR, C_LI, C_SCL, C_L2W, C_L2B, C_B2) = range(10)
NPAR = 10
ROOT = 11
N_MK = 11
N_RAD = 9
N_START = N_RAD + 10
N_DOUBLING = 15
N_POWERS = 2 + DOUBLINGS * N_DOUBLING
N_SMALL = N_START + 2 * N_POWERS
GATES = (1, 2, 1, 7, 1, 2, 2)


def settled(engine, passed):
    engine.sem_inc(passed, 1)


def mixture_kernel(nc, x, wg_t, wu_t, wd_t, tern_w, ffn_bias, win_t, cols, last_cols, b1_cols,
                   w1_t, w2_t, wout_t, bout, f1_w_t, f1_bias, f1_a, f1_b_t,
                   f1_mix, out):
    x1_dram = nc.dram_tensor("x1_scratch", (2 * STORED * P, HID), F32, kind="Internal").ap()
    pair_view = "(n t q) h -> q n t h"
    x_pairs = x.rearrange(pair_view, t=2, q=P)
    x1_pairs = x1_dram.rearrange(pair_view, t=2, q=P)

    with ExitStack() as ctx:
        def psum(name, shape):
            return ctx.enter_context(nc.psum_tensor(name, shape, F32))

        def sem(name):
            return ctx.enter_context(nc.semaphore(name))

        pool_passed, act_passed, dve_passed = sem("pool_passed"), sem("act_passed"), sem("dve_passed")

        ps_a = psum("ps_a", [P, 3, NB])
        ps_b = psum("ps_b", [P, 3, NB])
        ps_t = psum("ps_t", [P, 2, NB])

        N_W = KH * INNER
        with ExitStack() as wctx:
            wg_hi, wg_lo, wu_hi, wu_lo = (
                wctx.enter_context(nc.sbuf_tensor(name, [P, KH, INNER], F32R))
                for name in ("wg_hi", "wg_lo", "wu_hi", "wu_lo"))
        arena = ctx.enter_context(nc.sbuf_tensor("arena", [P, 4 * N_W], F32))
        cursor = [0]

        ident = ctx.enter_context(nc.sbuf_tensor("ident", [P, P], F32))

        def over_weights(*shape):
            n = 1
            for d in shape:
                n *= d
            ap = arena[:, cursor[0]:cursor[0] + n]
            cursor[0] += n
            assert cursor[0] <= 4 * N_W
            if len(shape) == 1:
                return ap
            return ap.rearrange("p (a b) -> p a b", b=shape[1]) if len(shape) == 2 else \
                ap.rearrange("p (a b c) -> p a b c", b=shape[1], c=shape[2])

        x1 = over_weights(TILES, HID)
        fold = over_weights(8, HID)
        f_a, f_b, f_wt = fold[:, 0:2, :], fold[:, 2:4, :], fold[:, 4:8, :]
        hs, xt_now = fold[:, 0:4, :], fold[:, 4:8, :]
        work = over_weights(4 * SEQ)
        xn = work.rearrange("p (t n) -> p t n", n=HID)
        w_re, w_im, u_re, u_im = (work[:, j * SEQ:(j + 1) * SEQ] for j in range(4))
        sq = w_re
        weff = over_weights(KH, HID)
        win = over_weights(BATCH, KH, P)
        f_w = over_weights(2, ER // P)
        stats2 = over_weights(TILES, 6)
        mv2 = over_weights(TILES, 2)
        rs2 = over_weights(TILES)
        e_s = over_weights(TILES)
        par = over_weights(DEPTH * NPAR)
        par_last = over_weights(3)
        small = over_weights(4, DEPTH * COARSE).rearrange("p j (l n) -> p j l n", n=COARSE)
        tmp = over_weights(4, DEPTH * COARSE // 2).rearrange("p j (l n) -> p j l n", n=COARSE // 2)
        e_c = over_weights(2, DEPTH)
        e_t = over_weights(4, DEPTH)
        rad = over_weights(DEPTH)
        u0 = over_weights(2, DEPTH)

        x1_in = [sem(f"x1_in{i}") for i in range(3)]
        x1_ready = sem("x1_ready")
        win_in = sem("win_in")
        win_zero = sem("win_zero")
        f_in = sem("f_in")
        fold_w = sem("fold_w")
        fold_b = sem("fold_b")
        full = sem("full")
        free = sem("free")
        st2 = sem("st2")
        mv2_s = sem("mv2_s")
        rs2_s = sem("rs2_s")
        xn_s = sem("xn_s")
        par_in = sem("par_in")
        tb = sem("tb")
        ORDER = [0, 2, 1, 3]
        bankf = [ps_a[:, 2, :], ps_b[:, 2, :]]

        def load_x1_group(sp, g):
            sp.dma_start(x1[:, 4 * g:4 * g + 4, :],
                         x1_dram[4 * g * P:4 * (g + 1) * P, :].rearrange("(t q) h -> q t h", q=P)
                         ).then_inc(x1_in[g], 16)

        def norm2_stats(dve, i):
            if i < 3:
                dve.wait_ge(x1_in[ORDER[i]], 16)
            else:
                dve.wait_ge(x1_ready, TILES)
            for j in range(4):
                dve.bn_stats(stats2[:, 4 * i + j, :], x1[:, 4 * ORDER[i] + j, :]).then_inc(st2, 1)
            for j in range(4):
                dve.wait_ge(st2, 4 * i + j + 1)
                dve.bn_aggr(mv2[:, 4 * i + j, :], stats2[:, 4 * i + j, :]).then_inc(mv2_s, 1)

        def norm2_root(dve, n, i0, i1):
            w = slice(4 * i0, 4 * i1)
            v, r, s = mv2[:, w, 1], rs2[:, w], e_s[:, w]
            done = [ROOT * n]

            def step(ins):
                done[0] += 1
                ins.then_inc(rs2_s, 1)
                dve.wait_ge(rs2_s, done[0])

            dve.wait_ge(mv2_s, 4 * i1)
            step(dve.tensor_scalar(v, v, EPS, None, ALU.add))
            step(dve.tensor_scalar(r.bitcast(I32), v.bitcast(I32), -0.5, float(0x5F3759DF),
                                   ALU.mult, ALU.add))
            for _ in range(3):
                step(dve.tensor_tensor(s, r, r, ALU.mult))
                step(dve.scalar_tensor_tensor(out=s, in0=s, scalar=-0.5, in1=v, op0=ALU.mult, op1=ALU.mult))
                step(dve.scalar_tensor_tensor(out=r, in0=s, scalar=1.5, in1=r, op0=ALU.add, op1=ALU.mult))

        def norm2_apply(dve, i):
            for j in range(4):
                m = 4 * i + j
                dve.tensor_scalar(xn[:, m % 8, :], x1[:, 4 * ORDER[i] + j, :], mv2[:, m, 0:1], rs2[:, m:m + 1],
                                  ALU.subtract, ALU.mult).then_inc(xn_s, 1)

        def tables_start(pool):
            pool.wait_ge(par_in, 16 * 4)
            pv = par.rearrange("p (l j) -> p l j", j=NPAR)
            re, im, lr, li = (pv[:, :, j] for j in (C_PR, C_PI, C_LR, C_LI))
            t0, t1, t2, t3 = (e_t[:, j, :] for j in range(4))
            e_re, e_im = e_c[:, 0, :], e_c[:, 1, :]
            n = [0]

            def run(*instructions):
                n[0] += len(instructions)
                for ins in instructions:
                    ins.then_inc(tb, 1)
                pool.wait_ge(tb, n[0])

            def tt(o, a, b, op):
                return pool.tensor_tensor(o, a, b, op)

            run(tt(t0, re, re, ALU.mult), tt(t1, im, im, ALU.mult), pool.memset(rad, 0.5),
                pool.memset(t3, -0.5))
            run(tt(t0, t0, t1, ALU.add))
            run(pool.tensor_scalar(t1, t0, 1.0e-37, None, ALU.is_lt))
            run(pool.tensor_scalar(t0, t0, 1.0e-37, None, ALU.max))
            run(tt(rad, t0, rad, ALU.pow), tt(t2, t0, t3, ALU.pow))
            assert n[0] == N_RAD
            run(tt(e_re, re, t2, ALU.mult), tt(e_im, im, t2, ALU.mult))
            run(tt(e_re, e_re, t1, ALU.add))
            run(tt(t0, lr, e_re, ALU.mult), tt(t1, li, e_im, ALU.mult),
                tt(t2, lr, e_im, ALU.mult), tt(t3, li, e_re, ALU.mult))
            run(tt(u0[:, 0, :], t0, t1, ALU.subtract), tt(t2, t2, t3, ALU.add))
            run(pool.tensor_scalar(u0[:, 1, :], t2, -1.0, None, ALU.mult))
            assert n[0] == N_START

        def tables_powers(pool, half, first, last):
            n = [N_START + half * N_POWERS + (2 + N_DOUBLING * first if first else 0)]

            def run(*instructions):
                n[0] += len(instructions)
                for ins in instructions:
                    ins.then_inc(tb, 1)
                pool.wait_ge(tb, n[0])

            def tt(o, a, b, op):
                return pool.tensor_tensor(o, a, b, op)

            z = small[:, 2 * half:2 * half + 2, :, :]
            t0, t1, t2, t3 = (e_t[:, j, :] for j in range(4))
            e_re, e_im = e_c[:, 0, :], e_c[:, 1, :]
            if first == 0:
                run(pool.memset(z[:, 0, :, 0:1], 1.0), pool.memset(z[:, 1, :, 0:1], 0.0))
            for w in (2 ** j for j in range(first, last)):
                br, bi = (e.rearrange("p (l o) -> p l o", o=1).to_broadcast([P, DEPTH, w]) for e in (e_re, e_im))
                q = [tmp[:, j, :, 0:w] for j in range(4)]
                zr, zi = z[:, 0, :, 0:w], z[:, 1, :, 0:w]
                run(tt(q[0], zr, br, ALU.mult), tt(q[1], zi, bi, ALU.mult),
                    tt(q[2], zr, bi, ALU.mult), tt(q[3], zi, br, ALU.mult),
                    tt(t0, e_re, e_re, ALU.mult), tt(t1, e_im, e_im, ALU.mult), tt(t2, e_re, e_im, ALU.mult))
                run(tt(z[:, 0, :, w:2 * w], q[0], q[1], ALU.subtract),
                    tt(z[:, 1, :, w:2 * w], q[2], q[3], ALU.add),
                    tt(e_re, t0, t1, ALU.subtract), tt(e_im, t2, t2, ALU.add), tt(t3, t0, t1, ALU.add))
                run(pool.tensor_scalar(t3, t3, -1.0, 2.0, ALU.mult, ALU.add))
                run(tt(e_re, e_re, t3, ALU.mult), tt(e_im, e_im, t3, ALU.mult))
            assert n[0] == N_START + half * N_POWERS + 2 + N_DOUBLING * last

        with ExitStack() as actx:
            def sb(name, shape, dt=F32):
                return actx.enter_context(nc.sbuf_tensor(name, shape, dt))

            wd_hi = sb("wd_hi", [P, CHUNKS, HID], F32R)
            wd_lo = sb("wd_lo", [P, CHUNKS, HID], F32R)
            q_t = sb("q_t", [P, KH, HID], F32R)
            s_buf = sb("s_buf", [P, 2, INNER])
            k_buf = sb("k_buf", [P, 2, INNER])
            m_buf = sb("m_buf", [P, 2, PADDED])
            zt_hi = sb("zt_hi", [P, PADDED], F32R)
            zt_lo = sb("zt_lo", [P, PADDED], F32R)
            xin = sb("xin", [P, 2, HID])
            xres = sb("xres", [P, 2, HID])
            xt_hi = sb("xt_hi", [P, 2, HID], F32R)
            xt_lo = sb("xt_lo", [P, 2, HID], F32R)
            gate2 = sb("gate2", [P, 2, HID])
            bias_b = sb("bias_b", [P, HID])
            junk_d = sb("junk_d", [P, INNER], I8)
            junk_a = sb("junk_a", [P, INNER], I8)
            powers = sb("powers", [P, STEPS + 2, 2])
            widths = sb("widths", [P, STEPS + 2, 2])
            iota8 = sb("iota8", [P, 2, 8])
            mag_sum = sb("mag_sum", [P, 2])
            cand = sb("cand", [P, 2])
            cand_low = sb("cand_low", [P, 2])
            rise = sb("rise", [P, 2])
            below = sb("below", [P, 2])
            at_most = sb("at_most", [P, 2])
            rank = sb("rank", [P, 2])
            top8 = sb("top8", [P, 2, 8])
            pick = sb("pick", [P, 2, 8])
            tau = sb("tau", [P, 2])
            above = sb("above", [P, 2])
            bad = sb("bad", [P, 2])
            bad_all = sb("bad_all", [P, 2])
            bad_int = sb("bad_int", [P, 2], I32)
            bit = sb("bit", [P, 2], I32)
            lo_bits = sb("lo_bits", [P, 2], I32)
            cand_bits = sb("cand_bits", [P, 2], I32)
            set_bits = sb("set_bits", [P, 2], I32)
            stats = sb("stats", [P, 2, 6])
            mv = sb("mv", [P, 2, 2])
            var_eps = sb("var_eps", [P, 2])
            rstd = sb("rstd", [P, 2])
            expo = sb("expo", [P, 2])
            one = sb("one", [P, 1])
            mags, thr, thr_neg = (pick[:].rearrange("p t e -> p (t e)")[:, i * KH:(i + 1) * KH] for i in range(3))

            c_const = sem("c_const")
            x_in = sem("x_in")
            x_res = sem("x_res")
            bias_in = sem("bias_in")
            tern_in = sem("tern_in")
            w_in = [sem(f"w_in{i}") for i in range(5)]
            w_hi = sem("w_hi")
            w_lo = sem("w_lo")
            t_mag = sem("t_mag")
            t_thr = sem("t_thr")
            t_neg = sem("t_neg")
            t_q = sem("t_q")
            t_tr = sem("t_tr")
            t_cp = sem("t_cp")
            ln_st = sem("ln_st")
            ln_mv = sem("ln_mv")
            ln_ve = sem("ln_ve")
            ln_rs = sem("ln_rs")
            xn_ready = sem("xn_ready")
            xt_psum = sem("xt_psum")
            xt_h = sem("xt_h")
            xt_l = sem("xt_l")
            gate_done = sem("gate_done")
            up_done = sem("up_done")
            s_ready = sem("s_ready")
            k_ready = sem("k_ready")
            z_ready = sem("z_ready")
            wid_ready = sem("wid_ready")
            cand_ready = sem("cand_ready")
            candlow_ready = sem("candlow_ready")
            rise_ready = sem("rise_ready")
            cnt_dve = sem("cnt_dve")
            cnt_act = sem("cnt_act")
            small_ready = sem("small_ready")
            top_ready = sem("top_ready")
            picked = sem("picked")
            bad_sum = sem("bad_sum")
            mask_ready = sem("mask_ready")
            zt_psum = sem("zt_psum")
            zt_h = sem("zt_h")
            zt_l = sem("zt_l")
            down_done = sem("down_done")
            down_out = sem("down_out")
            x1_out = sem("x1_out")
            q_done = sem("q_done")
            q_biased = sem("q_biased")
            g_ready = sem("g_ready")

            units = []
            for w, hi, lo in ((wg_t, wg_hi, wg_lo), (wu_t, wu_hi, wu_lo)):
                for k in range(KH):
                    units.append((w[k * P:(k + 1) * P, :], P, hi[:, k, :], lo[:, k, :], None))
            N_GU = len(units)
            for c in range(0, CHUNKS - 1, 2):
                units.append((wd_t[c * P:(c + 2) * P, :].rearrange("(c p) n -> p c n", c=2), P,
                              wd_hi[:, c:c + 2, :], wd_lo[:, c:c + 2, :], 2))
            last_rows = INNER - (CHUNKS - 1) * P
            units.append((wd_t[(CHUNKS - 1) * P:INNER, :], last_rows,
                          wd_hi[0:last_rows, CHUNKS - 1, :], wd_lo[0:last_rows, CHUNKS - 1, :], None))

            def slot_of(u):
                return u % 4 if u < N_GU else (0, 1, 3, 4)[(u - N_GU) % 4]

            def slot_ap(u):
                _, rows, hi, _, parts = units[u]
                buf = (m_buf[:, 0, :], m_buf[:, 1, :], k_buf[:, 0, :], k_buf[:, 1, :],
                       s_buf[:, 1, :])[slot_of(u)]
                n = HID * (parts or 1) if u >= N_GU else INNER
                ap = buf[0:rows, 0:n]
                return ap.rearrange("p (c n) -> p c n", c=parts) if parts else ap

            def loads_before(u):
                return sum(slot_of(v) == slot_of(u) for v in range(u + 1))

            block_a = actx.enter_context(nc.Block())

            def col(ap, n):
                return ap.rearrange("p (t o) -> p t o", o=1).to_broadcast([P, 2, n])

            @block_a.sync
            def _(sp):
                def load_x(dst, done, p):
                    sp.dma_start(dst[:].rearrange("q (n t) h -> q n t h", n=1),
                                 x_pairs[:, bass.ds(p, 1), :, :]).then_inc(done, 16)

                load_x(xin, x_in, 0)
                for t in range(2):
                    sp.dma_start(s_buf[:, t, 0:2 * HID].rearrange("p (k n) -> p k n", k=2),
                                 tern_w[2 * P * t:2 * P * (t + 1), :].rearrange("(k p) n -> p k n", p=P)
                                 ).then_inc(tern_in, 16)
                for u in range(len(units)):
                    prev = [v for v in range(u) if slot_of(v) == slot_of(u)]
                    if prev:
                        sp.wait_ge(w_lo, prev[-1] + 1)
                        sp.wait_ge(w_hi, prev[-1] + 1)
                    elif slot_of(u) == 4:
                        sp.wait_ge(t_tr, KH)
                    sp.dma_start(slot_ap(u), units[u][0]).then_inc(w_in[slot_of(u)], 16)
                    if u == 3:
                        sp.dma_start(bias_b[:], ffn_bias.partition_broadcast(P)).then_inc(bias_in, 16)
                        sp.wait_ge(xt_psum, 2)
                        load_x(xin, x_in, 1)

                def second_layer():
                    sp.wait_ge(up_done, TILES)
                    for b in range(BATCH):
                        for dst, src in ((par, cols), (par_last, last_cols)):
                            sp.dma_start(dst[b * DIM:(b + 1) * DIM, :], src).then_inc(par_in, 16)
                    sp.dma_start(f_w, f1_mix).then_inc(f_in, 16)
                    sp.dma_start(f_b, f1_b_t.rearrange("(k p) n -> p k n", p=P)).then_inc(f_in, 16)
                    sp.dma_start(f_a, f1_a.rearrange("(k p) n -> p k n", p=P)).then_inc(f_in, 16)
                    sp.dma_start(f_wt, f1_w_t.rearrange("(k p) n -> p k n", p=P)).then_inc(f_in, 16)
                    for i in range(3):
                        load_x1_group(sp, ORDER[i])
                    sp.wait_ge(win_zero, 1)
                    for b in range(BATCH):
                        sp.dma_start(win[:, b, :, b * DIM:(b + 1) * DIM],
                                     win_t.rearrange("(k p) d -> p k d", p=P)).then_inc(win_in, 16)

                def pair(p, first=False):
                    sp.wait_ge(xt_psum, 2 * p + 2)
                    load_x(xin, x_in, p + 1)
                    if not first:
                        sp.wait_ge(x1_out, 16 * (p - 1))
                    load_x(xres, x_res, p - 1)
                    sp.wait_ge(x1_ready, 2 * p)
                    sp.dma_start(x1_pairs[:, bass.ds(p - 1, 1), :, :],
                                 xres[:].rearrange("q (n t) h -> q n t h", n=1)).then_inc(x1_out, 16)

                pair(1, first=True)
                with sp.Fori(2, PAIRS - 1) as p:
                    pair(p)
                sp.wait_ge(x1_out, 16 * STORED)
                load_x(xres, x_res, PAIRS - 2)
                second_layer()
                sp.wait_ge(x1_ready, 2 * (PAIRS - 1))
                load_x(xres, x_res, PAIRS - 1)
                sp.wait_ge(x_res, 16 * PAIRS)

            @block_a.gpsimd
            def _(pool):
                pool.memset(ident[:], 0.0).then_inc(c_const, 1)
                pool.wait_ge(c_const, 1)
                pool.affine_select(out=ident[:], in_=ident[:], compare_op=ALU.not_equal, fill=1.0, base=0,
                                   pattern=[[-1, P]], channel_multiplier=1).then_inc(c_const, 1)
                pool.memset(expo[:], -0.5).then_inc(c_const, 1)
                pool.memset(one[:], 1.0).then_inc(c_const, 1)
                pool.memset(m_buf[:, :, INNER:PADDED], 0.0).then_inc(c_const, 1)
                for j in range(STEPS + 2):
                    pool.memset(powers[:, j, :], (HIGH - LOW) / INNER / 2 ** j).then_inc(c_const, 1)
                for j in range(8):
                    pool.memset(iota8[:, :, j:j + 1], float(j)).then_inc(c_const, 1)
                pool.wait_ge(c_const, N_CONST)

                def root(p):
                    pool.wait_ge(ln_ve, p + 1)
                    pool.tensor_tensor(rstd[:], var_eps[:], expo[:], ALU.pow).then_inc(ln_rs, 1)

                def residual(p, resident=False):
                    for t in range(2):
                        if t == 0:
                            pool.wait_ge(x_res, 16 * p)
                        pool.wait_ge(down_out, 2 * (p - 1) + t + 1)
                        row = x1[:, 2 * (p - 1) + t, :] if resident else xres[:, t, :]
                        pool.tensor_tensor(row, xres[:, t, :], gate2[:, t, :], ALU.add).then_inc(x1_ready, 1)

                def check_sum(p):
                    pool.wait_ge(picked, PICKS * p + PICKS - 1)
                    settled(pool, pool_passed)
                    pool.partition_all_reduce(bad_all[:], bad[:], P, RADD).then_inc(bad_sum, 1)

                root(0)
                root(1)
                check_sum(0)
                with pool.Fori(1, PAIRS - 1) as p:
                    root(p + 1)
                    residual(p)
                    check_sum(p)
                pool.wait_ge(up_done, TILES)
                pool.memset(win, 0.0).then_inc(win_zero, 1)
                tables_start(pool)
                tables_powers(pool, 0, 0, 3)
                pool.wait_ge(f_in, 16 * 4)
                pool.tensor_tensor(f_w[:, 0, :], f_w[:, 0, :], f_w[:, 1, :], ALU.mult).then_inc(fold_w, 1)
                pool.wait_ge(fold_w, 1)
                for k in range(ER // P):
                    pool.tensor_scalar(f_b[:, k, :], f_b[:, k, :], f_w[:, 0, k:k + 1], 0.0,
                                       ALU.mult, ALU.add).then_inc(fold_b, 1)
                residual(PAIRS - 1, resident=True)
                check_sum(PAIRS - 1)
                tables_powers(pool, 0, 3, DOUBLINGS)
                tables_powers(pool, 1, 0, DOUBLINGS - 1)
                residual(PAIRS, resident=True)

            @block_a.scalar
            def _(act):
                def split_hi(u):
                    act.wait_ge(w_in[slot_of(u)], 16 * loads_before(u))
                    act.activation(units[u][2], slot_ap(u), ACT.Copy).then_inc(w_hi, 1)

                def xt_high(p, t):
                    act.wait_ge(xt_psum, 2 * p + t + 1)
                    act.activation(xt_hi[:, t, :], ps_t[:, t, :], ACT.Copy).then_inc(xt_h, 1)

                act.wait_ge(tern_in, 32)
                for k in range(KH):
                    if k:
                        act.wait_ge(t_mag, k)
                    act.activation(junk_a[:, 0:HID], s_buf[:, k // 2, (k % 2) * HID:(k % 2 + 1) * HID],
                                   ACT.Abs, accum_out=mags[:, k:k + 1]).then_inc(t_mag, 1)
                for t in range(2):
                    xt_high(0, t)
                for u in range(N_GU):
                    split_hi(u)

                def silu_keys(p, t, wait_free):
                    act.wait_ge(gate_done, 2 * p + t + 1)
                    if not wait_free:
                        act.wait_ge(w_lo, N_GU + 4 if t else N_GU)
                    if wait_free:
                        act.wait_ge(mask_ready, 2 * p + t - 1)
                    act.activation(s_buf[:, t, :], ps_a[:].rearrange("p a n -> p (a n)")[:, 0:INNER],
                                   ACT.Silu).then_inc(s_ready, 1)
                    act.wait_ge(s_ready, 2 * p + t + 1)
                    act.activation(k_buf[:, t, :], s_buf[:, t, :], ACT.Abs,
                                   accum_out=mag_sum[:, t:t + 1]).then_inc(k_ready, 1)

                def count_b(p, n):
                    act.wait_ge(cand_ready, CANDS * p + n + 1)
                    act.activation(junk_a[:], k_buf[:, 1, :], ACT.Sign, bias=cand[:, 1:2], scale=-1.0,
                                   accum_out=below[:, 1:2]).then_inc(cnt_act, 1)

                def count_last(p, ahead):
                    act.wait_ge(cand_ready, CANDS * p + STEPS + 1)
                    for t in range(2):
                        if ahead:
                            xt_high(p + 1, t)
                        act.wait_ge(cnt_act, ACT_COUNTS * p + STEPS + t)
                        act.activation(junk_a[:], k_buf[:, t, :], ACT.Sign, bias=cand[:, t:t + 1], scale=-1.0,
                                       accum_out=at_most[:, t:t + 1]).then_inc(cnt_act, 1)

                def zt_high(p, i):
                    n = 2 * NG * (p - 1) + i
                    c0, c1 = GROUPS[i % NG]
                    act.wait_ge(zt_psum, n + 1)
                    if not (isinstance(n, int) and n < NG):
                        act.wait_ge(down_done, n - NG + 1)
                    act.activation(zt_hi[:, c0 * P:c1 * P], ps_t[:, i % 2, 0:(c1 - c0) * P],
                                   ACT.Copy).then_inc(zt_h, 1)

                def gate_silu(p):
                    for t in range(2):
                        act.wait_ge(q_biased, 2 * p + t + 1)
                        act.activation(gate2[:, t, :], gate2[:, t, :], ACT.Silu).then_inc(g_ready, 1)

                def pair(p, back, ahead, first=False):
                    for t in range(2):
                        silu_keys(p, t, not first)
                        if first and t == 0:
                            for u in range(N_GU, len(units)):
                                split_hi(u)
                    count_b(p, 0)
                    if back:
                        zt_high(p, 0)
                    count_b(p, 1)
                    if first:
                        for t in range(2):
                            xt_high(p + 1, t)
                    if back:
                        zt_high(p, 1)
                    for i in range(2, 6):
                        count_b(p, i)
                        if back:
                            zt_high(p, i)
                    count_b(p, 6)
                    count_b(p, 7)
                    count_last(p, ahead and not first)
                    gate_silu(p)

                pair(0, False, True, first=True)
                pair(1, True, True)
                with act.Fori(2, PAIRS - 1) as p:
                    pair(p, True, True)
                pair(PAIRS - 1, True, False)
                for k in range(KH):
                    act.wait_ge(full, k + 1)
                    act.activation(weff[:, k, :], bankf[k % 2], ACT.Copy).then_inc(free, 1)
                for i in range(2 * NG):
                    zt_high(PAIRS, i)

            @block_a.vector
            def _(dve):
                def split_lo(u):
                    dve.wait_ge(w_hi, u + 1)
                    dve.tensor_tensor(units[u][3], slot_ap(u), units[u][2].bitcast(F32),
                                      ALU.subtract).then_inc(w_lo, 1)

                def xt_low(p, t):
                    dve.wait_ge(xt_h, 2 * p + t + 1)
                    dve.tensor_tensor(xt_lo[:, t, :], ps_t[:, t, :], xt_hi[:, t, :].bitcast(F32),
                                      ALU.subtract).then_inc(xt_l, 1)

                def norm_stats(p):
                    dve.wait_ge(x_in, 16 * (p + 1))
                    for t in range(2):
                        dve.bn_stats(stats[:, t, :], xin[:, t, :]).then_inc(ln_st, 1)
                    for t in range(2):
                        dve.wait_ge(ln_st, 2 * p + t + 1)
                        settled(dve, dve_passed)
                        dve.bn_aggr(mv[:, t, :], stats[:, t, :]).then_inc(ln_mv, 1)
                    dve.wait_ge(ln_mv, 2 * p + 2)
                    dve.tensor_scalar(var_eps[:], mv[:, :, 1], EPS, None, ALU.add).then_inc(ln_ve, 1)

                def norm_apply(p):
                    dve.wait_ge(ln_rs, p + 1)
                    for t in range(2):
                        dve.tensor_scalar(xin[:, t, :], xin[:, t, :], mv[:, t, 0:1], rstd[:, t:t + 1],
                                          ALU.subtract, ALU.mult).then_inc(xn_ready, 1)

                norm_stats(0)
                norm_apply(0)
                for k in range(KH):
                    dve.wait_ge(t_mag, k + 1)
                    dve.tensor_scalar(thr[:, k:k + 1], mags[:, k:k + 1], 1.0 / HID, TERNARY,
                                      ALU.mult, ALU.mult).then_inc(t_thr, 1)
                    dve.wait_ge(t_thr, 2 * k + 1)
                    dve.tensor_scalar(thr_neg[:, k:k + 1], thr[:, k:k + 1], -1.0, None,
                                      ALU.mult).then_inc(t_thr, 1)
                    w = s_buf[:, k // 2, (k % 2) * HID:(k % 2 + 1) * HID]
                    neg = gate2[:, k % 2, :]
                    dve.wait_ge(t_thr, 2 * k + 2)
                    if k >= 2:
                        dve.wait_ge(t_q, k - 1)
                    dve.tensor_scalar(neg, w, thr_neg[:, k:k + 1], None, ALU.is_lt).then_inc(t_neg, 1)
                    dve.wait_ge(t_neg, k + 1)
                    dve.scalar_tensor_tensor(out=w, in0=w, scalar=thr[:, k:k + 1], in1=neg,
                                             op0=ALU.is_gt, op1=ALU.subtract).then_inc(t_q, 1)
                for t in range(2):
                    xt_low(0, t)
                for k in range(KH):
                    dve.wait_ge(t_tr, k + 1)
                    dve.tensor_copy(q_t[:, k, :], ps_b[:, k % 3, :]).then_inc(t_cp, 1)
                for u in range(N_GU):
                    split_lo(u)

                def product(p, t):
                    dve.wait_ge(up_done, 2 * p + t + 1)
                    dve.wait_ge(k_ready, 2 * p + t + 1)
                    dve.tensor_tensor(s_buf[:, t, :], s_buf[:, t, :],
                                      ps_b[:].rearrange("p a n -> p (a n)")[:, 0:INNER],
                                      ALU.mult).then_inc(z_ready, 1)

                def bracket(p):
                    dve.wait_ge(k_ready, 2 * p + 2)
                    dve.tensor_tensor(widths[:], powers[:],
                                      mag_sum[:].rearrange("p (o t) -> p o t", o=1).to_broadcast(
                                          [P, STEPS + 2, 2]), ALU.mult).then_inc(wid_ready, 1)
                    dve.tensor_scalar(cand[:], mag_sum[:], (LOW + HIGH) / 2 / INNER, None,
                                      ALU.mult).then_inc(cand_ready, 1)

                def halve(p, n):
                    dve.wait_ge(cand_ready, CANDS * p + n + 1)
                    if n == 0:
                        dve.wait_ge(wid_ready, p + 1)
                    if n < STEPS - 1:
                        dve.tensor_tensor(cand_low[:], cand[:], widths[:, n + 2, :],
                                          ALU.subtract).then_inc(candlow_ready, 1)
                    else:
                        dve.tensor_copy(cand_low[:], cand[:]).then_inc(candlow_ready, 1)
                    dve.tensor_scalar(junk_d[:], k_buf[:, 0, :], cand[:, 0:1], -float(DROP),
                                      ALU.is_lt, ALU.add, accum_out=below[:, 0:1]).then_inc(cnt_dve, 1)
                    dve.wait_ge(cnt_dve, STEPS * p + n + 1)
                    dve.wait_ge(cnt_act, ACT_COUNTS * p + n + 1)
                    dve.scalar_tensor_tensor(out=rise[:], in0=below[:], scalar=0.0, in1=widths[:, n + 1, :],
                                             op0=ALU.is_lt, op1=ALU.mult).then_inc(rise_ready, 1)
                    dve.wait_ge(rise_ready, STEPS * p + n + 1)
                    dve.wait_ge(candlow_ready, STEPS * p + n + 1)
                    dve.tensor_tensor(cand[:], cand_low[:], rise[:], ALU.add).then_inc(cand_ready, 1)

                def largest_under(p, t, back):
                    dve.wait_ge(cand_ready, CANDS * p + STEPS + 1)
                    if back:
                        dve.wait_ge(zt_psum, 2 * NG * (p - 1) + NG * (t + 1))
                    dve.scalar_tensor_tensor(out=m_buf[:, t, 0:INNER], in0=k_buf[:, t, :],
                                             scalar=cand[:, t:t + 1], in1=k_buf[:, t, :],
                                             op0=ALU.is_le, op1=ALU.mult).then_inc(small_ready, 1)
                    dve.wait_ge(small_ready, 2 * p + t + 1)
                    settled(dve, dve_passed)
                    dve.max(top8[:, t, :], m_buf[:, t, 0:INNER]).then_inc(top_ready, 1)

                def choose(p):
                    done = [PICKS * p]

                    def step(ins):
                        done[0] = done[0] + 1
                        ins.then_inc(picked, 1)
                        dve.wait_ge(picked, done[0])

                    dve.wait_ge(cnt_act, ACT_COUNTS * (p + 1))
                    dve.wait_ge(top_ready, 2 * p + 2)
                    step(dve.tensor_scalar(rank[:], at_most[:], 0.5, 0.25, ALU.mult, ALU.add))
                    step(dve.tensor_tensor(pick[:], iota8[:], col(rank[:], 8), ALU.subtract))
                    step(dve.tensor_tensor(pick[:], pick[:], pick[:], ALU.mult))
                    step(dve.scalar_tensor_tensor(out=pick[:], in0=pick[:], scalar=0.1, in1=top8[:],
                                                  op0=ALU.is_lt, op1=ALU.mult))
                    step(dve.tensor_reduce(tau[:], pick[:], AX_X, ALU.add))
                    step(dve.tensor_tensor(pick[:], top8[:], col(tau[:], 8), ALU.is_gt))
                    step(dve.tensor_reduce(above[:], pick[:], AX_X, ALU.add))
                    step(dve.tensor_tensor(above[:], above[:], rank[:], ALU.subtract))
                    step(dve.tensor_tensor(above[:], above[:], above[:], ALU.mult))
                    step(dve.tensor_scalar(bad[:], tau[:], 0.0, None, ALU.is_le))
                    step(dve.scalar_tensor_tensor(out=bad[:], in0=above[:], scalar=0.1, in1=bad[:],
                                                  op0=ALU.is_gt, op1=ALU.max))
                    dve.wait_ge(bad_sum, p + 1)
                    step(dve.tensor_tensor(bad_int[:, 0:1], bad_all[:, 0:1], bad_all[:, 1:2], ALU.add))
                    settled(dve, dve_passed)
                    failed = dve.value_load(bad_int[0:1, 0:1], min_val=0, max_val=2 * P)
                    with dve.If(failed > 0):
                        exact_choice()

                def exact_choice():
                    dve.memset(lo_bits[:], 0)
                    dve.memset(bit[:], 1 << 30)
                    dve.drain()
                    with dve.Fori(0, 31):
                        dve.tensor_tensor(cand_bits[:], lo_bits[:], bit[:], ALU.bitwise_or)
                        dve.drain()
                        for t in range(2):
                            dve.tensor_scalar(junk_d[:], k_buf[:, t, :], cand_bits[:, t:t + 1].bitcast(F32),
                                              -float(DROP), ALU.is_lt, ALU.add, accum_out=above[:, t:t + 1])
                            dve.drain()
                        dve.scalar_tensor_tensor(out=set_bits[:], in0=above[:], scalar=0.0, in1=bit[:],
                                                 op0=ALU.is_lt, op1=ALU.mult)
                        dve.drain()
                        dve.tensor_tensor(lo_bits[:], lo_bits[:], set_bits[:], ALU.bitwise_or)
                        dve.tensor_scalar(bit[:], bit[:], 1, None, ALU.logical_shift_right)
                        dve.drain()
                    dve.tensor_copy(tau[:], lo_bits[:].bitcast(F32))
                    dve.drain()
                    for t in range(2):
                        keys, tau_t = k_buf[:, t, :], tau[:, t:t + 1]
                        equal, seen = m_buf[:, 0, 0:INNER], m_buf[:, 1, 0:INNER]
                        dve.tensor_scalar(junk_d[:], keys, tau_t, -float(DROP), ALU.is_lt, ALU.add,
                                          accum_out=above[:, t:t + 1])
                        dve.tensor_scalar(equal, keys, tau_t, None, ALU.is_equal)
                        dve.drain()
                        dve.tensor_scalar(above[:, t:t + 1], above[:, t:t + 1], -1.0, None, ALU.mult)
                        dve.tensor_tensor_scan(seen, one[:].to_broadcast([P, INNER]), equal, 0.0,
                                               ALU.mult, ALU.add)
                        dve.drain()
                        dve.scalar_tensor_tensor(out=seen, in0=seen, scalar=above[:, t:t + 1], in1=equal,
                                                 op0=ALU.is_gt, op1=ALU.mult)
                        dve.drain()
                        dve.scalar_tensor_tensor(out=keys, in0=seen, scalar=3.0e38, in1=keys,
                                                 op0=ALU.mult, op1=ALU.max)
                        dve.drain()

                def mask(p):
                    for t in range(2):
                        dve.wait_ge(z_ready, 2 * p + t + 1)
                        dve.scalar_tensor_tensor(out=m_buf[:, t, 0:INNER], in0=k_buf[:, t, :],
                                                 scalar=tau[:, t:t + 1], in1=s_buf[:, t, :],
                                                 op0=ALU.is_gt, op1=ALU.mult).then_inc(mask_ready, 1)

                def zt_low(p, i):
                    n = 2 * NG * (p - 1) + i
                    c0, c1 = GROUPS[i % NG]
                    dve.wait_ge(zt_h, n + 1)
                    dve.tensor_tensor(zt_lo[:, c0 * P:c1 * P], ps_t[:, i % 2, 0:(c1 - c0) * P],
                                      zt_hi[:, c0 * P:c1 * P].bitcast(F32), ALU.subtract).then_inc(zt_l, 1)

                def down_gate(p, t):
                    dve.wait_ge(down_done, 2 * NG * (p - 1) + NG * (t + 1))
                    dve.wait_ge(g_ready, 2 * (p - 1) + t + 1)
                    dve.tensor_tensor(gate2[:, t, :], ps_a[:, t, :], gate2[:, t, :],
                                      ALU.mult).then_inc(down_out, 1)

                def q_bias(p, t, back):
                    dve.wait_ge(q_done, 2 * p + t + 1)
                    if back:
                        dve.wait_ge(x1_ready, 2 * (p - 1) + t + 1)
                    dve.tensor_tensor(gate2[:, t, :], ps_b[:, t, :], bias_b[:], ALU.add).then_inc(q_biased, 1)

                def pair(p, back, ahead, first=False):
                    product(p, 0)
                    if first:
                        for u in range(N_GU, len(units)):
                            split_lo(u)
                    if ahead:
                        norm_stats(p + 1)
                    if first:
                        norm_apply(p + 1)
                    bracket(p)
                    if first:
                        product(p, 1)
                    halve(p, 0)
                    halve(p, 1)
                    if back:
                        zt_low(p, 0)
                    if not first:
                        product(p, 1)
                    if first:
                        for t in range(2):
                            xt_low(p + 1, t)
                        dve.wait_ge(bias_in, 16)
                        for t in range(2):
                            q_bias(p, t, back)
                    if back:
                        zt_low(p, 1)
                    if ahead and not first:
                        norm_apply(p + 1)
                    for i in range(2, 6):
                        halve(p, i)
                        if back:
                            zt_low(p, i)
                    if back:
                        down_gate(p, 0)
                    halve(p, 6)
                    halve(p, 7)
                    if back:
                        down_gate(p, 1)
                    for t in range(2):
                        if ahead and not first:
                            xt_low(p + 1, t)
                        largest_under(p, t, back)
                    if not first:
                        for t in range(2):
                            q_bias(p, t, back)
                    choose(p)
                    mask(p)

                pair(0, False, True, first=True)
                pair(1, True, True)
                with dve.Fori(2, PAIRS - 1) as p:
                    pair(p, True, True)
                pair(PAIRS - 1, True, False)
                for i in range(2 * NG):
                    zt_low(PAIRS, i)
                    if i < 2:
                        norm2_stats(dve, i)
                    elif i == 2:
                        norm2_root(dve, 0, 0, 2)
                    elif i < 5:
                        norm2_apply(dve, i - 3)
                down_gate(PAIRS, 0)
                norm2_stats(dve, 2)
                down_gate(PAIRS, 1)

            @block_a.tensor
            def _(pe):
                def x_transpose(p, t):
                    pe.wait_ge(xn_ready, 2 * p + t + 1)
                    for k in range(KH):
                        last = pe.transpose(ps_t[:, t, k * P:(k + 1) * P], xin[:, t, k * P:(k + 1) * P], ident[:])
                    last.then_inc(xt_psum, 1)

                def project(p, t, hi, lo, bank, done, unit0):
                    for k in range(KH):
                        if isinstance(p, int) and p == 0 and t == 0:
                            pe.wait_ge(w_lo, unit0 + k + 1)
                        xh, xl = xt_hi[:, t, k * P:(k + 1) * P], xt_lo[:, t, k * P:(k + 1) * P]
                        for n, (xs, ws) in enumerate(((xh, hi), (xh, lo), (xl, hi))):
                            for c, (c0, c1) in enumerate(NCOL):
                                last = pe.matmul(bank[:, c, 0:c1 - c0], xs, ws[:, k, c0:c1],
                                                 start=(k == 0 and n == 0), stop=(k == KH - 1 and n == 2))
                    last.then_inc(done, 1)

                def zt_transpose(p, i):
                    n = 2 * NG * (p - 1) + i
                    t, (c0, c1) = i // NG, GROUPS[i % NG]
                    pe.wait_ge(mask_ready, 2 * (p - 1) + t + 1)
                    if not (isinstance(n, int) and n < 2):
                        pe.wait_ge(zt_l, n - 1)
                    for c in range(c0, c1):
                        last = pe.transpose(ps_t[:, i % 2, (c - c0) * P:(c - c0 + 1) * P],
                                            m_buf[:, t, c * P:(c + 1) * P], ident[:])
                    last.then_inc(zt_psum, 1)

                def down(p, i):
                    t, (c0, c1) = i // NG, GROUPS[i % NG]
                    pe.wait_ge(zt_l, 2 * NG * (p - 1) + i + 1)
                    if isinstance(p, int) and p == 1:
                        pe.wait_ge(w_lo, len(units))
                    for c in range(c0, c1):
                        rows = min(P, INNER - c * P)
                        zh = zt_hi[0:rows, c * P:(c + 1) * P]
                        zl = zt_lo[0:rows, c * P:(c + 1) * P]
                        for n, (zs, ws) in enumerate(((zh, wd_hi), (zh, wd_lo), (zl, wd_hi))):
                            last = pe.matmul(ps_a[:, t, :], zs, ws[0:rows, c, :],
                                             start=(c == 0 and n == 0), stop=(c == CHUNKS - 1 and n == 2))
                    last.then_inc(down_done, 1)

                def ternary(p, t):
                    for k in range(KH):
                        for n, xs in enumerate((xt_hi, xt_lo)):
                            last = pe.matmul(ps_b[:, t, :], xs[:, t, k * P:(k + 1) * P], q_t[:, k, :],
                                             start=(k == 0 and n == 0), stop=(k == KH - 1 and n == 1))
                    last.then_inc(q_done, 1)

                def back_half(p):
                    down(p, 0)
                    for i in range(2, 2 * NG):
                        zt_transpose(p, i)
                        down(p, i - 1)
                    down(p, 2 * NG - 1)

                def pair(p, back, ahead):
                    for t in range(2):
                        pe.wait_ge(xt_l, 2 * p + t + 1)
                        if t == 1:
                            pe.wait_ge(s_ready, 2 * p + 1)
                        elif not (isinstance(p, int) and p < 2):
                            pe.wait_ge(down_out, 2 * (p - 1))
                        project(p, t, wg_hi, wg_lo, ps_a, gate_done, 0)
                        if back and t == 1:
                            zt_transpose(p, 0)
                            zt_transpose(p, 1)
                        if t == 1:
                            pe.wait_ge(z_ready, 2 * p + 1)
                        elif not (isinstance(p, int) and p == 0):
                            pe.wait_ge(q_biased, 2 * p)
                        project(p, t, wu_hi, wu_lo, ps_b, up_done, KH)
                    if back:
                        pe.wait_ge(s_ready, 2 * p + 2)
                        back_half(p)
                    for t in range(2):
                        if t == 0:
                            pe.wait_ge(z_ready, 2 * p + 2)
                        ternary(p, t)
                        if ahead:
                            x_transpose(p + 1, t)

                pe.wait_ge(c_const, 2)
                for t in range(2):
                    x_transpose(0, t)
                for k in range(KH):
                    pe.wait_ge(t_q, KH)
                    if k == 3:
                        pe.wait_ge(t_cp, 1)
                    for o in range(KH):
                        last = pe.transpose(ps_b[:, k % 3, o * P:(o + 1) * P],
                                            s_buf[:, o // 2, (o % 2) * HID + k * P:(o % 2) * HID + (k + 1) * P],
                                            ident[:])
                    last.then_inc(t_tr, 1)
                pe.wait_ge(t_cp, KH)
                pair(0, False, True)
                pair(1, True, True)
                with pe.Fori(2, PAIRS - 1) as p:
                    pair(p, True, True)
                pair(PAIRS - 1, True, False)
                pe.wait_ge(fold_b, ER // P)
                for k in range(KH):
                    if k >= 2:
                        pe.wait_ge(free, k - 1)
                    for e in range(ER // P):
                        pe.matmul(bankf[k % 2], f_a[:, e, k * P:(k + 1) * P], f_b[:, e, :],
                                  start=(e == 0), stop=False)
                    pe.matmul(bankf[k % 2], ident[:], f_wt[:, k, :], start=False, stop=True).then_inc(full, 1)
                zt_transpose(PAIRS, 0)
                zt_transpose(PAIRS, 1)
                back_half(PAIRS)

        with ExitStack() as bctx:
            def sb(name, shape, dt=F32):
                return bctx.enter_context(nc.sbuf_tensor(name, shape, dt))

            xt = sb("xt", [P, KH, TOKENS])
            g2 = sb("g2", [P, TILES, HID])
            f_bias = over_weights(HID)
            bout_b = sb("bout_b", [P, VOCAB])
            b1_c = sb("b1_c", [P, DEPTH * 2])
            w1 = sb("w1", [P, BATCH, DFF])
            w2 = sb("w2", [P, BATCH, 2, P])
            wout = sb("wout", [P, BATCH, VOCAB])
            center = sb("center", [P, P])
            means = sb("means", [P, 2])
            expo2 = sb("expo2", [P, 16])
            h = over_weights(SEQ)
            y = sb("y", [P, SEQ])
            xc = sb("xc", [P, SEQ])
            lnv = sb("lnv", [P, HALVES, 8])
            lnr = sb("lnr", [P, HALVES, 8])
            rot_c = sb("rot_c", [P, DEPTH, SEQ])
            rot_s = sb("rot_s", [P, DEPTH, SEQ])
            tbig = sb("tbig", [P, SEQ])
            rho = sb("rho", [P, DEPTH])

            last_in = sem("last_in")
            lay_in = sem("lay_in")
            mk = sem("mk")
            xt_ps = sem("xt_ps")
            xt_a = sem("xt_a")
            xt_v = sem("xt_v")
            xt_n = sem("xt_n")
            g_full = sem("g_full")
            g_free = sem("g_free")
            g_done = sem("g_done")
            f_full = sem("f_full")
            f_free = sem("f_free")
            bg = sem("bg")
            x1_b = sem("x1_b")
            h_ps = sem("h_ps")
            h_ready = sem("h_ready")
            rho_s = sem("rho_s")
            ln_cent = sem("ln_cent")
            ln_xc = sem("ln_xc")
            ln_sq = sem("ln_sq")
            ln_var = sem("ln_var")
            ln_v = sem("ln_v")
            ln_r = sem("ln_r")
            ln_w = sem("ln_w")
            ln_bc = sem("ln_bc")
            ln_y = sem("ln_y")
            ln_o = sem("ln_o")
            cv_wr = sem("cv_wr")
            cv_wi = sem("cv_wi")
            cv_ur = sem("cv_ur")
            cv_ui = sem("cv_ui")
            cv_a = sem("cv_a")
            cv_b = sem("cv_b")
            cv_ab = sem("cv_ab")
            ff_2 = sem("ff_2")
            o_ps = sem("o_ps")
            o_used = sem("o_used")
            o_dve = sem("o_dve")
            o_pool = sem("o_pool")
            o_out = sem("o_out")

            bank1 = [ps_a[:, 0, :], ps_a[:, 1, :]]
            bank2 = [ps_a[:, 2, :], ps_b[:, 0, :]]
            bankv = [ps_b[:, 1, :], ps_b[:, 2, :]]
            bankx = [ps_t[:, 0, :], ps_t[:, 1, :]]
            obank = bankx + bankv
            FF = 2 * 4
            OUT = [4 * g + j for g in ORDER for j in range(4)]

            def on_pool(m):
                return m % 2 == 0

            def cs(c):
                return slice(c * NB, (c + 1) * NB)

            def pcol(l, j):
                return par[:, bass.ds(NPAR * l + j, 1)]

            block_b = bctx.enter_context(nc.Block())

            @block_b.sync
            def _(sp):
                sp.dma_start(b1_c[:], b1_cols).then_inc(last_in, 16)
                sp.dma_start(f_bias, f1_bias.partition_broadcast(P)).then_inc(last_in, 16)
                sp.dma_start(bout_b[:], bout.partition_broadcast(P)).then_inc(last_in, 16)
                sp.wait_ge(mk, N_MK)
                for b in range(BATCH):
                    sp.dma_start(wout[b * DIM:(b + 1) * DIM, b, :], wout_t).then_inc(last_in, 16)
                with sp.Fori(0, DEPTH) as l:
                    sp.wait_ge(h_ready, 4 * l + 2)
                    for b in range(BATCH):
                        sp.dma_start(w1[b * DIM:(b + 1) * DIM, b:b + 1, :], w1_t[bass.ds(l, 1), :, :].rearrange("o p n -> p o n")).then_inc(lay_in, 16)
                        sp.dma_start(w2[:, b, :, b * DIM:(b + 1) * DIM],
                                     w2_t[bass.ds(l, 1), :, :].rearrange("o (m p) d -> p (o m) d", p=P)
                                     ).then_inc(lay_in, 16)
                for m, t in enumerate(OUT):
                    done = o_pool if on_pool(m) else o_dve
                    sp.wait_ge(done, sum(on_pool(v) == on_pool(m) for v in range(m + 1)))
                    sp.dma_start(out[t * P:(t + 1) * P, :], x1[:, t, :]).then_inc(o_out, 16)
                sp.wait_ge(o_out, 16 * TILES)

            @block_b.gpsimd
            def _(pool):
                made = [0]

                def make(ins):
                    made[0] += 1
                    ins.then_inc(mk, 1)
                    pool.wait_ge(mk, made[0])

                make(pool.memset(w1[:], 0.0))
                make(pool.memset(w2[:], 0.0))
                make(pool.memset(wout[:], 0.0))
                make(pool.memset(expo2[:], -0.5))
                make(pool.memset(center[:], 0.0))
                make(pool.memset(means[:], 0.0))
                for b in range(BATCH):
                    half = slice(b * DIM, (b + 1) * DIM)
                    make(pool.memset(center[half, half], -1.0 / DIM))
                    make(pool.memset(means[half, b:b + 1], 1.0 / DIM))
                make(pool.tensor_tensor(center[:], center[:], ident[:], ALU.add))
                assert made[0] == N_MK

                def tables(l, first):
                    done = [first]

                    def big(o, a, b, op):
                        done[0] = done[0] + 1
                        settled(pool, pool_passed)
                        pool.tensor_tensor(o, a, b, op).then_inc(tb, 1)
                        pool.wait_ge(tb, done[0])

                    def part(j, fine):
                        s = small[:, j, bass.ds(l, 1), :]
                        s = s.rearrange("p o n -> p o n" if fine else "p o n -> p n o")
                        return s.to_broadcast([P, COARSE, COARSE])

                    fr, fi, cr, ci = part(0, True), part(1, True), part(2, False), part(3, False)
                    grid = "p o (a b) -> p (o a) b"
                    co = rot_c[:, bass.ds(l, 1), :].rearrange(grid, b=COARSE)
                    si = rot_s[:, bass.ds(l, 1), :].rearrange(grid, b=COARSE)
                    t = tbig[:].rearrange("p (a b) -> p a b", b=COARSE)
                    big(t, ci, fi, ALU.mult)
                    big(co, cr, fr, ALU.mult)
                    big(co, co, t, ALU.subtract)
                    big(t, ci, fr, ALU.mult)
                    big(si, cr, fi, ALU.mult)
                    big(si, si, t, ALU.add)

                def root(q, c):
                    pool.wait_ge(ln_v, 2 * q + c + 1)
                    pool.tensor_tensor(lnr[:, c, :], lnv[:, c, :], expo2[:, 0:8], ALU.pow).then_inc(ln_r, 1)

                def times_sin(l, c, src, ready, count, done):
                    pool.wait_ge(ready, count)
                    settled(pool, pool_passed)
                    pool.tensor_tensor(w_im[:, cs(c)].rearrange("p (o n) -> p o n", o=1),
                                       src[:, cs(c)].rearrange("p (o n) -> p o n", o=1),
                                       rot_s[:, bass.ds(l, 1), cs(c)], ALU.mult).then_inc(done, 1)

                tables_powers(pool, 1, DOUBLINGS - 1, DOUBLINGS)
                tables(0, N_SMALL)
                def bias_out(l, k):
                    def tile(ap):
                        return ap[:, bass.ds(4 * l + k, 1), :]

                    s = tbig[:, (k % 2) * HID:(k % 2 + 1) * HID].rearrange("p (o n) -> p o n", o=1)
                    pool.wait_ge(g_done, 4 * l + k + 1)
                    settled(pool, pool_passed)
                    pool.tensor_tensor(s, bout_b[:].rearrange("p (o n) -> p o n", o=1), tile(g2),
                                       ALU.mult).then_inc(bg, 1)
                    pool.wait_ge(bg, 4 * l + k + 1)
                    settled(pool, pool_passed)
                    pool.tensor_tensor(tile(x1), tile(x1), s, ALU.add).then_inc(x1_b, 1)
                    pool.wait_ge(x1_b, 4 * l + k + 1)

                def layer(l, lagging, ahead):
                    for c in range(HALVES):
                        root(2 * l, c)
                    for c in range(HALVES):
                        times_sin(l, c, y, ln_o, 4 * l + c + 1, cv_wi)
                    for c in range(HALVES):
                        times_sin(l, c, u_im, cv_ui, 2 * l + c + 1, cv_b)
                        if lagging:
                            bias_out(l - 1, c)
                    for c in range(HALVES):
                        root(2 * l + 1, c)
                        if lagging:
                            bias_out(l - 1, 2 + c)
                    if ahead:
                        tables(l + 1, 6 * l + 6 + N_SMALL)

                pool.wait_ge(last_in, 16 * 5)
                layer(0, False, True)
                with pool.Fori(1, DEPTH - 1) as l:
                    layer(l, True, True)
                layer(DEPTH - 1, True, False)
                for k in range(4):
                    bias_out(DEPTH - 1, k)
                for c in range(HALVES):
                    root(2 * DEPTH, c)
                for m, t in enumerate(OUT):
                    if on_pool(m):
                        pool.wait_ge(o_used, m + 1)
                        pool.tensor_tensor(x1[:, t, :], g2[:, t, :], x1[:, t, :], ALU.add).then_inc(o_pool, 1)

            @block_b.scalar
            def _(act):
                act.wait_ge(tb, N_RAD)
                act.activation(rho[:], rad, ACT.Tanh).then_inc(rho_s, 1)
                for i in range(0, TILES, 2):
                    t = 4 * ORDER[i // 4] + i % 4
                    act.wait_ge(xt_ps, i + 1)
                    act.activation(xt[:, :, t * P:(t + 1) * P],
                                   obank[i % 4].rearrange("p (k n) -> p k n", k=KH), ACT.Copy).then_inc(xt_a, 1)

                def squares(q, c):
                    act.wait_ge(ln_xc, 2 * q + c + 1)
                    act.activation(sq[:, cs(c)], xc[:, cs(c)], ACT.Square).then_inc(ln_sq, 1)

                def norm_out(q, c, func, w, b):
                    act.wait_ge(ln_y, 2 * q + c + 1)
                    settled(act, act_passed)
                    act.activation(y[:, cs(c)], xc[:, cs(c)], func, scale=w, bias=b).then_inc(ln_o, 1)

                def gate(l, k):
                    tile = g2[:, bass.ds(4 * l + k, 1), :]
                    act.wait_ge(g_free, 4 * l + k + 1)
                    settled(act, act_passed)
                    act.activation(tile, tile, ACT.Silu).then_inc(g_done, 1)

                def take_tokens(l, n):
                    act.activation(xt_now[:, n, :], xt[:, n, bass.ds(NB * l, NB)], ACT.Copy).then_inc(xt_n, 1)

                def layer(l, ahead):
                    for c in range(HALVES):
                        squares(2 * l, c)
                    for c in range(HALVES):
                        norm_out(2 * l, c, ACT.Silu, pcol(l, C_L1W), pcol(l, C_L1B))
                    gate(l, 0)
                    squares(2 * l + 1, 0)
                    gate(l, 1)
                    squares(2 * l + 1, 1)
                    gate(l, 2)
                    norm_out(2 * l + 1, 0, ACT.Identity, pcol(l, C_L2W), pcol(l, C_L2B))
                    for c in range(HALVES):
                        for u in range(4):
                            if c == 0 and u == 2:
                                norm_out(2 * l + 1, 1, ACT.Identity, pcol(l, C_L2W), pcol(l, C_L2B))
                                gate(l, 3)
                            act.wait_ge(f_full, FF * l + 4 * c + u + 1)
                            if c == 1 and u == 0:
                                act.wait_ge(ff_2, 2 * l + 1)
                            settled(act, act_passed)
                            act.activation(hs[:, u, :], bankx[u % 2], ACT.Silu,
                                           bias=b1_c[:, bass.ds(2 * l + u % 2, 1)]).then_inc(f_free, 1)
                            if c == 1 and ahead:
                                take_tokens(l + 1, u)

                act.wait_ge(par_in, 16 * 4)
                act.wait_ge(last_in, 16 * 5)
                act.wait_ge(xt_a, TILES // 2)
                act.wait_ge(xt_v, 2)
                for n in range(KH):
                    take_tokens(0, n)
                with act.Fori(0, DEPTH - 1) as l:
                    layer(l, True)
                layer(DEPTH - 1, False)
                for c in range(HALVES):
                    squares(2 * DEPTH, c)
                for c in range(HALVES):
                    norm_out(2 * DEPTH, c, ACT.Identity, par_last[:, 0:1], par_last[:, 1:2])

            @block_b.vector
            def _(dve):
                def xt_odd(i):
                    for j in (1, 3):
                        t = 4 * ORDER[i] + j
                        dve.wait_ge(xt_ps, 4 * i + j + 1)
                        dve.tensor_copy(xt[:, :, t * P:(t + 1) * P],
                                        obank[j].rearrange("p (k n) -> p k n", k=KH)).then_inc(xt_v, 1)

                def h_in(c):
                    dve.wait_ge(h_ps, c + 1)
                    if c == 0:
                        dve.wait_ge(par_in, 16 * 4)
                    dve.tensor_scalar(h[:, cs(c)], bank1[c], par_last[:, 2:3], None, ALU.add).then_inc(h_ready, 1)

                xt_odd(0)
                xt_odd(1)
                norm2_root(dve, 1, 2, 3)
                norm2_apply(dve, 2)
                norm2_stats(dve, 3)
                norm2_root(dve, 2, 3, 4)
                norm2_apply(dve, 3)
                xt_odd(2)
                h_in(0)
                xt_odd(3)
                h_in(1)

                def centered(q, c):
                    dve.wait_ge(ln_cent, 2 * q + c + 1)
                    dve.tensor_copy(xc[:, cs(c)], bank1[c]).then_inc(ln_xc, 1)

                def variance(q, c):
                    dve.wait_ge(ln_var, 2 * q + c + 1)
                    dve.tensor_scalar(lnv[:, c, :], bankv[c][:, 0:8], EPS, None, ALU.add).then_inc(ln_v, 1)

                def widen(q, c):
                    dve.wait_ge(ln_r, 2 * q + c + 1)
                    dve.tensor_copy(sq[:, cs(c)].rearrange("p (t d) -> p t d", d=DIM),
                                    lnr[:, c, :].rearrange("p (t o) -> p t o", o=1).to_broadcast([P, 8, DIM])
                                    ).then_inc(ln_w, 1)

                def normed(q, c):
                    dve.wait_ge(ln_bc, 2 * q + c + 1)
                    dve.wait_ge(ln_xc, 2 * q + c + 1)
                    dve.tensor_tensor(xc[:, cs(c)], xc[:, cs(c)], bank2[c], ALU.mult).then_inc(ln_y, 1)

                def norm(q):
                    for part in (centered, variance):
                        for c in range(HALVES):
                            part(q, c)
                    for c in range(HALVES):
                        widen(q, c)
                        normed(q, c)

                def gate_bias(l, k):
                    dve.wait_ge(g_full, 4 * l + k + 1)
                    dve.tensor_tensor(g2[:, bass.ds(4 * l + k, 1), :], bankx[k % 2].rearrange("p (o n) -> p o n", o=1),
                                      f_bias.rearrange("p (o n) -> p o n", o=1), ALU.add).then_inc(g_free, 1)

                def one(ap):
                    return ap.rearrange("p (o n) -> p o n", o=1)

                def cos(l, c):
                    return rot_c[:, bass.ds(l, 1), cs(c)]

                def turn(l, c):
                    dve.wait_ge(ln_o, 4 * l + c + 1)
                    dve.tensor_tensor(one(w_re[:, cs(c)]), one(y[:, cs(c)]), cos(l, c), ALU.mult).then_inc(cv_wr, 1)

                def scan(l, c, imaginary):
                    w, u, ready, done = (w_im, u_im, cv_wi, cv_ui) if imaginary else (w_re, u_re, cv_wr, cv_ur)
                    dve.wait_ge(ready, 2 * l + c + 1)
                    if c == 0:
                        first = u0[:, int(imaginary), bass.ds(l, 1)]
                    else:
                        dve.wait_ge(done, 2 * l + 1)
                        first = u[:, NB - 1:NB]
                    dve.tensor_tensor_scan(u[:, cs(c)], rho[:, bass.ds(l, 1)].to_broadcast([P, NB]), w[:, cs(c)],
                                           first, ALU.mult, ALU.add).then_inc(done, 1)

                def turn_back(l, c):
                    dve.wait_ge(cv_ur, 2 * l + c + 1)
                    dve.tensor_tensor(one(w_re[:, cs(c)]), one(u_re[:, cs(c)]), cos(l, c),
                                      ALU.mult).then_inc(cv_a, 1)

                def into_h(l, c):
                    dve.wait_ge(cv_a, 2 * l + c + 1)
                    dve.wait_ge(cv_b, 2 * l + c + 1)
                    dve.tensor_tensor(w_re[:, cs(c)], w_re[:, cs(c)], w_im[:, cs(c)], ALU.add).then_inc(cv_ab, 1)
                    dve.wait_ge(cv_ab, 2 * l + c + 1)
                    dve.scalar_tensor_tensor(out=h[:, cs(c)], in0=w_re[:, cs(c)], scalar=pcol(l, C_SCL),
                                             in1=h[:, cs(c)], op0=ALU.mult, op1=ALU.add).then_inc(h_ready, 1)

                dve.wait_ge(last_in, 16 * 5)
                dve.wait_ge(rho_s, 1)
                with dve.Fori(0, DEPTH) as l:
                    norm(2 * l)
                    dve.wait_ge(tb, N_SMALL + 6 * l + 6)
                    gate_bias(l, 0)
                    turn(l, 0)
                    scan(l, 0, False)
                    scan(l, 0, True)
                    turn_back(l, 0)
                    turn(l, 1)
                    scan(l, 1, False)
                    into_h(l, 0)
                    scan(l, 1, True)
                    turn_back(l, 1)
                    centered(2 * l + 1, 0)
                    into_h(l, 1)
                    gate_bias(l, 1)
                    variance(2 * l + 1, 0)
                    centered(2 * l + 1, 1)
                    gate_bias(l, 2)
                    widen(2 * l + 1, 0)
                    normed(2 * l + 1, 0)
                    variance(2 * l + 1, 1)
                    gate_bias(l, 3)
                    widen(2 * l + 1, 1)
                    normed(2 * l + 1, 1)
                    for c in range(HALVES):
                        dve.wait_ge(ff_2, 2 * l + c + 1)
                        dve.scalar_tensor_tensor(out=h[:, cs(c)], in0=bank1[c], scalar=pcol(l, C_B2),
                                                 in1=h[:, cs(c)], op0=ALU.add, op1=ALU.add).then_inc(h_ready, 1)
                norm(2 * DEPTH)

                def residual(m):
                    if not on_pool(m):
                        t = OUT[m]
                        dve.wait_ge(o_used, m + 1)
                        dve.tensor_tensor(x1[:, t, :], g2[:, t, :], x1[:, t, :], ALU.add).then_inc(o_dve, 1)

                dve.wait_ge(x1_b, TILES)
                for m, t in enumerate(OUT):
                    dve.wait_ge(o_ps, m + 1)
                    dve.tensor_tensor(g2[:, t, :], obank[m % 4], g2[:, t, :], ALU.mult).then_inc(o_used, 1)
                    if m:
                        residual(m - 1)
                residual(TILES - 1)

            @block_b.tensor
            def _(pe):
                for i in range(TILES):
                    pe.wait_ge(xn_s, i + 1)
                    if i >= 4:
                        pe.wait_ge(xt_v if i % 2 else xt_a, i // 2 - 1)
                    for k in range(KH):
                        last = pe.transpose(obank[i % 4][:, k * P:(k + 1) * P], xn[:, i % 8, k * P:(k + 1) * P],
                                            ident[:])
                    last.then_inc(xt_ps, 1)
                    if i % 8 == 7:
                        c = i // 8
                        pe.wait_ge(win_in, 32)
                        pe.wait_ge(xt_a, 4 * c + 4)
                        pe.wait_ge(xt_v, 4 * c + 4)
                        for b in range(BATCH):
                            for k in range(KH):
                                last = pe.matmul(bank1[c], win[:, b, k, :],
                                                 xt[:, k, b * SEQ + c * NB:b * SEQ + (c + 1) * NB],
                                                 start=(b == 0 and k == 0), stop=(b == 1 and k == KH - 1))
                        last.then_inc(h_ps, 1)
                pe.wait_ge(mk, N_MK)

                def center_rows(q, c):
                    pe.wait_ge(h_ready, 2 * q + c + 1)
                    pe.matmul(bank1[c], center[:], h[:, cs(c)], start=True, stop=True).then_inc(ln_cent, 1)

                def variances(q, c):
                    pe.wait_ge(ln_sq, 2 * q + c + 1)
                    for j in range(4):
                        last = pe.matmul(bankv[c][:, 2 * j:2 * j + 2],
                                         sq[:, c * NB + j * P:c * NB + (j + 1) * P], means[:],
                                         start=True, stop=True)
                    last.then_inc(ln_var, 1)

                def spread(q, c):
                    pe.wait_ge(ln_w, 2 * q + c + 1)
                    for j in range(4):
                        last = pe.transpose(bank2[c][:, j * P:(j + 1) * P],
                                            sq[:, c * NB + j * P:c * NB + (j + 1) * P], ident[:])
                    last.then_inc(ln_bc, 1)

                def gate_step(l, i):
                    k, n = i // KH, i % KH
                    if i == 0:
                        pe.wait_ge(xt_n, KH * l + KH)
                    if n == 0 and k >= 2:
                        pe.wait_ge(g_free, 4 * l + k - 1)
                    last = pe.matmul(bankx[k % 2], xt_now[:, n, k * P:(k + 1) * P], weff[:, n, :],
                                     start=(n == 0), stop=(n == KH - 1))
                    if n == KH - 1:
                        last.then_inc(g_full, 1)

                def up_unit(l, c, u):
                    b, m = u // 2, u % 2
                    if c == 0 and u < 2:
                        pe.wait_ge(g_free, 4 * l + 3 + u)
                    else:
                        pe.wait_ge(f_free, FF * l + 4 * c + u - 1)
                    pe.matmul(bankx[u % 2], w1[:, b, m * P:(m + 1) * P], y[:, cs(c)],
                              start=True, stop=True).then_inc(f_full, 1)

                def down_unit(l, c, u):
                    b, m = u // 2, u % 2
                    pe.wait_ge(f_free, FF * l + 4 * c + u + 1)
                    last = pe.matmul(bank1[c], w2[:, b, m, :], hs[:, u, :], start=(u == 0), stop=(u == 3))
                    if u == 3:
                        last.then_inc(ff_2, 1)

                with pe.Fori(0, DEPTH) as l:
                    gates = iter(range(4 * KH))

                    def gate(n):
                        for _ in range(n):
                            gate_step(l, next(gates))

                    center_rows(2 * l, 0)
                    center_rows(2 * l, 1)
                    gate(GATES[0])
                    variances(2 * l, 0)
                    variances(2 * l, 1)
                    gate(GATES[1])
                    spread(2 * l, 0)
                    gate(GATES[2])
                    spread(2 * l, 1)
                    gate(GATES[3])
                    center_rows(2 * l + 1, 0)
                    gate(GATES[4])
                    variances(2 * l + 1, 0)
                    center_rows(2 * l + 1, 1)
                    gate(GATES[5])
                    variances(2 * l + 1, 1)
                    spread(2 * l + 1, 0)
                    gate(GATES[6])
                    pe.wait_ge(lay_in, 64 * l + 64)
                    for c in range(HALVES):
                        pe.wait_ge(ln_o, 4 * l + 2 + c + 1)
                        up_unit(l, c, 0)
                        up_unit(l, c, 1)
                        if c == 0:
                            spread(2 * l + 1, 1)
                        down_unit(l, c, 0)
                        up_unit(l, c, 2)
                        down_unit(l, c, 1)
                        up_unit(l, c, 3)
                        down_unit(l, c, 2)
                        down_unit(l, c, 3)
                q = 2 * DEPTH
                for part in (center_rows, variances, spread):
                    for c in range(HALVES):
                        part(q, c)

                for m, t in enumerate(OUT):
                    if m % 8 == 0:
                        pe.wait_ge(ln_o, 2 * q + m // 8 + 1)
                    if m >= 4:
                        pe.wait_ge(o_used, m - 3)
                    b, j = t // (TILES // BATCH), t % (TILES // BATCH)
                    pe.matmul(obank[m % 4], y[:, j * P:(j + 1) * P], wout[:, b, :],
                              start=True, stop=True).then_inc(o_ps, 1)


def _program(nc, args, out):
    mixture_kernel(nc, *args, out)


def layout(**inputs):
    import numpy as np

    a = {k: np.asarray(v) for k, v in inputs.items()}

    def t(name):
        return np.ascontiguousarray(a[name].T)

    def l1(name):
        return a["L1_attn_" + name]

    per_layer = ["ln1_w", "ln1_b", "phz_re", "phz_im", "lc_re", "lc_im", "sc_lin", "ln2_w", "ln2_b", "b2"]
    data = {
        "x": a["L0_attn_x"].reshape(TOKENS, HID),
        "wg_t": t("L0_attn_w_gate"), "wu_t": t("L0_attn_w_up"), "wd_t": t("L0_attn_w_down"),
        "tern_w": a["L0_ffn_weight"], "ffn_bias": a["L0_ffn_bias"],
        "win_t": t("L1_attn_Win"),
        "cols": np.stack([l1(n) for n in per_layer], axis=1).transpose(2, 0, 1).reshape(DIM, DEPTH * NPAR),
        "last_cols": np.stack([l1("lnl_w"), l1("lnl_b"), l1("bin")], axis=1),
        "b1_cols": l1("b1").reshape(DEPTH * DFF // P, P).T,
        "w1_t": l1("W1").transpose(0, 2, 1), "w2_t": l1("W2").transpose(0, 2, 1),
        "wout_t": t("L1_attn_Wout"), "bout": l1("bout"),
        "f1_w_t": t("L1_ffn_W"), "f1_bias": a["L1_ffn_bias"],
        "f1_a": a["L1_ffn_A"].reshape(ER, HID),
        "f1_b_t": a["L1_ffn_Bf"].transpose(0, 2, 1).reshape(ER, HID),
        "f1_mix": np.stack([np.repeat(a["L1_ffn_" + n], RANK).reshape(ER // P, P) for n in ("coeffs", "scales")])
        .transpose(2, 0, 1),
    }
    return {name: np.ascontiguousarray(value) for name, value in data.items()}


def kernel(**inputs):
    import concourse.bacc as bacc
    from concourse.bass_utils import run_bass_kernel_spmd

    nc = bacc.Bacc("TRN2", target_bir_lowering=False, num_devices=1)
    arrays, args = {}, []
    for name, value in layout(**inputs).items():
        arrays["in_" + name] = value
        args.append(nc.dram_tensor("in_" + name, value.shape, mybir.dt.from_np(value.dtype),
                                   kind="ExternalInput").ap())
    out = nc.dram_tensor("out_0", (TOKENS, HID), F32, kind="ExternalOutput").ap()
    _program(nc, args, out)
    r = run_bass_kernel_spmd(nc, [arrays], core_ids=[0])
    return r.results[0]["out_0"].reshape(2, TOKENS // 2, HID)
```
